# Optimizing a Trainium2 kernel written in Bass

```python
import numpy as np
import jax
import jax.numpy as jnp

def _softmax(x, axis=-1):
    return jax.nn.softmax(x, axis=axis)

def _gelu(x):
    return jax.nn.gelu(x, approximate=True)

def _silu(x):
    return jax.nn.silu(x)

def _sigmoid(x):
    return jax.nn.sigmoid(x)

def _layernorm(x, axis=-1, eps=1e-05):
    m = jnp.mean(x, axis=axis, keepdims=True)
    v = jnp.var(x, axis=axis, keepdims=True)
    return (x - m) / jnp.sqrt(v + eps)

def _scatter_add(tgt, idx, src, axis=0):
    return tgt.at[idx].add(src)

def _segment_sum(src, seg, n):
    return jax.ops.segment_sum(src, seg, n)
kernel_name = 'mk_seq_postln_d1_jaxref_r8_d7ed37'

def setup_inputs(seed: int=0):
    np.random.seed(seed)
    _w = jnp.asarray

    def _L0_attn_setup():
        import jax, jax.numpy as jnp
        from jax import lax
        import numpy as np
        D_MODEL = 128
        K = 32
        K_Q = 4
        N_ANCHOR = 4
        N_DECAY = K - N_ANCHOR
        M = 8
        KS = 4
        H = D_MODEL // K
        N_REP = K // K_Q
        DIM_K = D_MODEL
        DIM_DECAY = K
        DIM_Q = K_Q * H * M * 2
        TOTAL = DIM_K + DIM_DECAY + DIM_Q
        B, L = (2, 256)
        key = jax.random.key(seed)
        ks = jax.random.split(key, 8)
        x = jax.random.normal(ks[0], (B, L, D_MODEL), jnp.float32)
        W_in = jax.random.normal(ks[1], (D_MODEL, TOTAL), jnp.float32) * D_MODEL ** (-0.5)
        conv_k = jax.random.normal(ks[2], (KS, 1, DIM_K + DIM_DECAY), jnp.float32) * 0.3
        grid = np.linspace(-np.pi / 3, np.pi / 3, M)
        theta = jnp.asarray(np.tile(grid.reshape(1, 1, 1, 1, M), (1, 1, K, H, 1)), jnp.float32)
        decay_slopes = jnp.log(jnp.exp(jnp.asarray(np.geomspace(0.001, 0.1, N_DECAY), jnp.float32)) - 1.0)
        anchor_slopes = jnp.log(jnp.exp(jnp.asarray(np.geomspace(0.01, 0.1, N_ANCHOR), jnp.float32)) - 1.0)
        score_scale = jnp.ones((K,), jnp.float32)
        lim = float(np.sqrt(6.0 / (H + H)))
        W_re = jax.random.uniform(ks[3], (H, H), jnp.float32, -lim, lim)
        W_im = jax.random.uniform(ks[4], (H, H), jnp.float32, -lim, lim)
        norm_scale = jnp.ones((2 * H,), jnp.float32)
        W_out = jax.random.normal(ks[5], (D_MODEL, D_MODEL), jnp.float32) * D_MODEL ** (-0.5)
        return dict(x=x, W_in=W_in, conv_k=conv_k, theta=theta, decay_slopes=decay_slopes, anchor_slopes=anchor_slopes, score_scale=score_scale, W_re=W_re, W_im=W_im, norm_scale=norm_scale, W_out=W_out)
    _L0_attn_in = _L0_attn_setup()

    def _L0_ffn_setup():
        import jax, jax.numpy as jnp
        import numpy as np
        TOP_K = 2

        def _mlp(x, w_fc, w_proj):
            return jnp.square(jax.nn.relu(x @ w_fc.T)) @ w_proj.T
        key = jax.random.key(seed)
        ks = jax.random.split(key, 6)
        B, S, D, E = (4, 256, 128, 8)
        d_ff = 4 * D
        x = jax.random.normal(ks[0], (B, S, D), dtype=jnp.float32)
        router_w = jax.random.normal(ks[1], (E, D), dtype=jnp.float32) * 0.02
        w_fc = jax.random.normal(ks[2], (E, d_ff, D), dtype=jnp.float32) * 0.02
        w_proj = jax.random.normal(ks[3], (E, D, d_ff), dtype=jnp.float32) * 0.02
        shared_fc = jax.random.normal(ks[4], (d_ff, D), dtype=jnp.float32) * 0.02
        shared_proj = jax.random.normal(ks[5], (D, d_ff), dtype=jnp.float32) * 0.02
        return {'x': x, 'router_w': router_w, 'w_fc': w_fc, 'w_proj': w_proj, 'shared_fc': shared_fc, 'shared_proj': shared_proj}
    _L0_ffn_in = _L0_ffn_setup()
    _d = {'L0_attn_x': _L0_attn_in['x'], 'L0_attn_W_in': _L0_attn_in['W_in'], 'L0_attn_conv_k': _L0_attn_in['conv_k'], 'L0_attn_theta': _L0_attn_in['theta'], 'L0_attn_decay_slopes': _L0_attn_in['decay_slopes'], 'L0_attn_anchor_slopes': _L0_attn_in['anchor_slopes'], 'L0_attn_score_scale': _L0_attn_in['score_scale'], 'L0_attn_W_re': _L0_attn_in['W_re'], 'L0_attn_W_im': _L0_attn_in['W_im'], 'L0_attn_norm_scale': _L0_attn_in['norm_scale'], 'L0_attn_W_out': _L0_attn_in['W_out'], 'L0_ffn_router_w': _L0_ffn_in['router_w'], 'L0_ffn_w_fc': _L0_ffn_in['w_fc'], 'L0_ffn_w_proj': _L0_ffn_in['w_proj'], 'L0_ffn_shared_fc': _L0_ffn_in['shared_fc'], 'L0_ffn_shared_proj': _L0_ffn_in['shared_proj']}
    _x0 = _d['L0_attn_x']
    _d['L0_attn_x'] = jax.random.normal(jax.random.fold_in(jax.random.key(seed), 1), (4, 1024, 128), dtype=_x0.dtype)
    del _x0
    return _d

def reference(L0_attn_x, L0_attn_W_in, L0_attn_conv_k, L0_attn_theta, L0_attn_decay_slopes, L0_attn_anchor_slopes, L0_attn_score_scale, L0_attn_W_re, L0_attn_W_im, L0_attn_norm_scale, L0_attn_W_out, L0_ffn_router_w, L0_ffn_w_fc, L0_ffn_w_proj, L0_ffn_shared_fc, L0_ffn_shared_proj):

    def _L0_attn_ref(x, W_in, conv_k, theta, decay_slopes, anchor_slopes, score_scale, W_re, W_im, norm_scale, W_out):
        import jax, jax.numpy as jnp
        from jax import lax
        import numpy as np
        D_MODEL = 128
        K = 32
        K_Q = 4
        N_ANCHOR = 4
        N_DECAY = K - N_ANCHOR
        M = 8
        KS = 4
        H = D_MODEL // K
        N_REP = K // K_Q
        DIM_K = D_MODEL
        DIM_DECAY = K
        DIM_Q = K_Q * H * M * 2
        TOTAL = DIM_K + DIM_DECAY + DIM_Q
        B, L = (2, 256)
        b, l, _ = x.shape
        z = x @ W_in
        z_mem = z[..., :DIM_K + DIM_DECAY]
        q_raw = z[..., DIM_K + DIM_DECAY:]
        zp = jnp.pad(z_mem, ((0, 0), (KS - 1, 0), (0, 0)))
        z_mem = lax.conv_general_dilated(zp, conv_k, window_strides=(1,), padding='VALID', dimension_numbers=('NWC', 'WIO', 'NWC'), feature_group_count=DIM_K + DIM_DECAY)
        k_val = z_mem[..., :DIM_K].reshape(b, l, K, H)
        s_raw = z_mem[..., -K:].reshape(b, l, K, 1)
        q = q_raw.reshape(b, l, K_Q, H, M, 2)
        q_re, q_im = (q[..., 0], q[..., 1])
        pos = jnp.arange(l, dtype=jnp.float32)
        slopes_d = jax.nn.softplus(decay_slopes).reshape(1, 1, N_DECAY, 1)
        dist = jnp.maximum(jnp.float32(l - 1) - pos, 0.0)
        lw_d = -slopes_d * dist[None, :, None, None]
        slopes_a = jax.nn.softplus(anchor_slopes).reshape(1, 1, N_ANCHOR, 1)
        lw_a = -slopes_a * pos[None, :, None, None]
        log_tw = jnp.concatenate([lw_d, lw_a], axis=2)
        log_p = jnp.clip(score_scale[None, None, :, None] * s_raw, -20.0, 20.0)
        p_w = jnp.exp(log_p + log_tw)
        phi = k_val[..., None] * theta
        re_k = jnp.cos(phi)
        im_k = jnp.sin(phi)
        den = jnp.cumsum(p_w[..., 0], axis=1)
        pwb = p_w[..., None]
        num_re = jnp.cumsum(pwb * re_k, axis=1)
        num_im = jnp.cumsum(pwb * im_k, axis=1)
        inv = lax.rsqrt(jnp.maximum(den, 0.0001))
        inv = (inv * inv)[..., None, None]
        s_re = (num_re * inv).reshape(b, l, K_Q, N_REP, H, M)
        s_im = (num_im * inv).reshape(b, l, K_Q, N_REP, H, M)
        qr = q_re.reshape(b, l, K_Q, 1, H, M)
        qi = q_im.reshape(b, l, K_Q, 1, H, M)
        out_re = jnp.sum(s_re * qr + s_im * qi, axis=-1).reshape(b, l, K, H)
        out_im = jnp.sum(s_im * qr - s_re * qi, axis=-1).reshape(b, l, K, H)
        y_re = out_re * norm_scale[:H] * jnp.diagonal(W_re)
        y_im = out_im * norm_scale[H:] * jnp.diagonal(W_im)
        y = jax.nn.silu((y_re + y_im).reshape(b, l, DIM_K))
        return y @ W_out

    def _L0_ffn_ref(x, router_w, w_fc, w_proj, shared_fc, shared_proj):
        import jax, jax.numpy as jnp
        import numpy as np
        TOP_K = 2

        def _mlp(x, w_fc, w_proj):
            return jnp.square(jax.nn.relu(x @ w_fc.T)) @ w_proj.T
        B, S, D = x.shape
        E = router_w.shape[0]
        T = B * S
        flat = x.reshape(T, D)
        logits = flat @ router_w.T
        probs = jax.nn.softmax(logits.astype(jnp.float32), axis=-1)
        topk_p, topk_i = jax.lax.top_k(probs, TOP_K)
        topk_w = (topk_p / jnp.maximum(topk_p.sum(-1, keepdims=True), 1e-09)).astype(flat.dtype)
        combine = jnp.zeros((T, E), dtype=flat.dtype)
        combine = combine.at[jnp.arange(T)[:, None], topk_i].add(topk_w)
        out = jnp.zeros_like(flat)
        for e in range(E):
            out = out + _mlp(flat, w_fc[e], w_proj[e]) * combine[:, e:e + 1]
        out = out + _mlp(flat, shared_fc, shared_proj)
        return out.reshape(B, S, D)
    x = L0_attn_x
    x = _layernorm(x + _L0_attn_ref(x, L0_attn_W_in, L0_attn_conv_k, L0_attn_theta, L0_attn_decay_slopes, L0_attn_anchor_slopes, L0_attn_score_scale, L0_attn_W_re, L0_attn_W_im, L0_attn_norm_scale, L0_attn_W_out), axis=-1)
    x = _layernorm(x + _L0_ffn_ref(x, L0_ffn_router_w, L0_ffn_w_fc, L0_ffn_w_proj, L0_ffn_shared_fc, L0_ffn_shared_proj), axis=-1)
    return x

_drawn_inputs = setup_inputs


def setup_inputs(seed=0):
    import zlib

    import numpy as np

    out = dict(_drawn_inputs(seed))
    spreads = {'L0_attn_score_scale': (1.0, 0.6), 'L0_attn_norm_scale': (1.0, 0.2)}
    factors = {'L0_attn_anchor_slopes': 35.712,
     'L0_ffn_router_w': 3.247,
     'L0_ffn_w_fc': 3.095,
     'L0_ffn_w_proj': 2.816}
    for name, (base, spread) in spreads.items():
        noise = np.random.default_rng([zlib.crc32(name.encode()), seed]).standard_normal(out[name].shape)
        drawn = base * np.exp(spread * noise) if base else spread * noise
        out[name] = jnp.asarray(drawn.astype(out[name].dtype))
    for name, factor in factors.items():
        out[name] = (out[name] * factor).astype(out[name].dtype)
    return out
```

```python
from contextlib import ExitStack

import concourse.bass as bass
from concourse import mybir

ALU = mybir.AluOpType
ACT = mybir.ActivationFunctionType
AX = mybir.AxisListType
F32 = mybir.dt.float32
F32R = mybir.dt.float32r

P = 128
D = 128
B, L = 4, 1024
TPB = L // P
NT = B * TPB
K, H, M, KQ = 32, 4, 8, 4
REP = K // KQ
KH = K * H
HM = H * M
NF = KH * M
TAPS = 4
HALO = TAPS - 1
E, FF = 8, 512
FC = FF // P
NE = E + 1
ROUND = 12582912.0
TURN = 6.283185
HALF_PI = 1.5707963267948966
EPS = 1e-5


def build(nc, x, W_in, conv_k, theta, decay_slopes, anchor_slopes, score_scale, W_re, W_im,
          norm_scale, W_out, router_w, w_fc, w_proj, shared_fc, shared_proj, tables, out):
    ctx = ExitStack()

    def sb(name, shape, dt=F32, c=ctx):
        return c.enter_context(nc.sbuf_tensor(name, shape, dt))

    def ps(name, shape, c):
        return c.enter_context(nc.psum_tensor(name, shape, F32))

    with ctx:
        x_tok = sb("x_tok", [P, NT + 1, D])
        xT = sb("xT", [P, 2, B, HALO + L + P], F32R)
        y_all = sb("y_all", [P, NT, KH])
        p_tok = sb("p_tok", [P, TPB, B, K])
        inv_den = sb("inv_den", [P, TPB, B, K])
        ident = sb("ident", [P, P])
        tri = sb("tri", [P, P])
        wconv = sb("wconv", [P, 2, TAPS, KH], F32R)
        wq = sb("wq", [P, 2, 2 * KQ * HM], F32R)
        thblk = sb("thblk", [P, 2, NF], F32R)
        w_out = sb("w_out", [P, D])
        routerT = sb("routerT", [P, E])
        half_pi = sb("half_pi", [P, 1])

        setup(nc, x, W_in, conv_k, theta, decay_slopes, anchor_slopes, score_scale, W_re, W_im,
              norm_scale, W_out, router_w, tables, x_tok, xT, p_tok, inv_den, ident, tri, wconv, wq,
              thblk, w_out, routerT, half_pi)
        memory(nc, xT, y_all, p_tok, inv_den, tri, wconv, wq, thblk, half_pi)
        mixture(nc, x_tok, xT, y_all, ident, w_out, routerT, w_fc, w_proj, shared_fc, shared_proj, out)


def setup(nc, x, W_in, conv_k, theta, decay_slopes, anchor_slopes, score_scale, W_re, W_im,
          norm_scale, W_out, router_w, tables, x_tok, xT, p_tok, inv_den, ident, tri, wconv, wq,
          thblk, w_out, routerT, half_pi):
    with ExitStack() as c:
        def sb(name, shape, dt=F32):
            return c.enter_context(nc.sbuf_tensor(name, shape, dt))

        def ps(name, shape):
            return c.enter_context(nc.psum_tensor(name, shape, F32))

        def sem(name):
            return c.enter_context(nc.semaphore(name))

        TOTAL = KH + K + 2 * KQ * HM
        w_in = sb("w_in", [P, TOTAL])
        taps_row = sb("taps_row", [P, TAPS, KH])
        theta_k = sb("theta_k", [P, M])
        slope_raw = sb("slope_raw", [P, 1])
        score = sb("score", [P, 1])
        taps_s = sb("taps_s", [P, TAPS])
        dist = sb("dist", [P, L])
        diag = sb("diag", [P, 2, H])
        norm = sb("norm", [P, 2, H])
        coef = sb("coef", [P, 2, H])
        r_w = sb("r_w", [E, D])
        ones = sb("ones", [P, P])
        wconv_f = sb("wconv_f", [P, TAPS, KH])
        wq_f = sb("wq_f", [P, 2, KQ, HM])
        wq_t = sb("wq_t", [P, 2, KQ, HM])
        th_f = sb("th_f", [P, NF])
        ws_f = sb("ws_f", [P, B, P])
        ws = sb("ws", [P, 2, B, P], F32R)
        zs = sb("zs", [P, HALO + L])
        lp = sb("lp", [P, L])
        lq = sb("lq", [P, L])
        sp = sb("sp", [P, 8])
        den = sb("den", [P, TPB, B * K])
        tot = sb("tot", [P, TPB, B * K])
        pst = [ps(f"pst{i}", [P, 512]) for i in range(2)]
        pz = ps("pz", [P, 512])
        pp = ps("pp", [P, 1024])
        pt = ps("pt", [P, 1024])

        x_in = [sem(f"x_in{b}") for b in range(B)]
        w_arrived = sem("w_arrived")
        tabs_in = sem("tabs_in")
        small_in = sem("small_in")
        folded = sem("folded")
        dchain = sem("dchain")
        x_turned = sem("x_turned")
        x_high = sem("x_high")
        x_low = sem("x_low")
        z_done = sem("z_done")
        z_kept = sem("z_kept")
        soft_exp = sem("soft_exp")
        soft_in = sem("soft_in")
        lp_ready = sem("lp_ready")
        p_exp = sem("p_exp")
        p_turned = sem("p_turned")
        p_kept = sem("p_kept")
        sums = sem("sums")
        den_ready = sem("den_ready")
        r_turned = sem("r_turned")
        out_kept = sem("out_kept")
        block = c.enter_context(nc.Block())
        N_SMALL = 3 * B + B + 2 + 2 + 3

        @block.sync
        def _(sp_):
            sp_.dma_start(ident[:], tables[:, 0:P]).then_inc(tabs_in, 16)
            for b in range(B):
                sp_.dma_start(x_tok[:, b * TPB:(b + 1) * TPB, :],
                              x[b].rearrange("(j p) d -> p j d", p=P)).then_inc(x_in[b], 16)
            sp_.dma_start(tri[:], tables[:, P:2 * P]).then_inc(tabs_in, 16)
            sp_.dma_start(dist[:], tables[:, 2 * P:2 * P + L]).then_inc(tabs_in, 16)

        @block.scalar
        def _(act):
            act.dma_start(w_in[:], W_in).then_inc(w_arrived, 16)
            with nc.allow_non_contiguous_dma(reason="small parameter rows"):
                act.dma_start(taps_row[:], conv_k[:, 0, 0:KH].unsqueeze(0).broadcast_to([P, TAPS, KH])
                              ).then_inc(small_in, 16)
                for b in range(B):
                    act.dma_start(slope_raw[b * K:b * K + K - 4, :], decay_slopes.unsqueeze(1)).then_inc(small_in, 16)
                    act.dma_start(slope_raw[b * K + K - 4:(b + 1) * K, :], anchor_slopes.unsqueeze(1)
                                  ).then_inc(small_in, 16)
                    act.dma_start(score[b * K:(b + 1) * K, :], score_scale.unsqueeze(1)).then_inc(small_in, 16)
                    act.dma_start(taps_s[b * K:(b + 1) * K, :],
                                  conv_k[:, 0, KH:KH + K].rearrange("t k -> k t")).then_inc(small_in, 16)
                act.dma_start(theta_k[:], theta[0, 0].rearrange("k h m -> (k h) m")).then_inc(small_in, 16)
                for i, w in enumerate((W_re, W_im)):
                    dg = w.rearrange("a b -> (a b)")[0:H * H:H + 1]
                    act.dma_start(diag[:, i, :], dg.unsqueeze(0).broadcast_to([P, H])).then_inc(small_in, 16)
                act.dma_start(norm[:], norm_scale.rearrange("(i h) -> i h", i=2).unsqueeze(0)
                              .broadcast_to([P, 2, H])).then_inc(small_in, 16)
                act.dma_start(w_out[:], W_out).then_inc(small_in, 16)
                act.dma_start(r_w[:], router_w).then_inc(small_in, 16)
            act.wait_ge(soft_in, 1)
            nc.scalar.activation(sp[:, 1:2], sp[:, 0:1], ACT.Exp).then_inc(soft_exp, 1)
            for g in range(2 * B):
                act.wait_ge(x_turned, g + 1)
                b, half = g // 2, g % 2
                nc.scalar.copy(xT[:, 0, b, HALO + half * 512:HALO + (half + 1) * 512], pst[g % 2][:]
                               ).then_inc(x_high, 1)
            for half in range(2):
                act.wait_ge(z_done, half + 1)
                nc.scalar.copy(zs[:, HALO + half * 512:HALO + (half + 1) * 512], pz[:]).then_inc(z_kept, 1)
            act.wait_ge(lp_ready, 1)
            nc.scalar.activation(lq[:], lp[:], ACT.Exp).then_inc(p_exp, 1)

        @block.tensor
        def _(pe):
            pe.wait_ge(tabs_in, 16)
            for g in range(2 * B):
                b, half = g // 2, g % 2
                if half == 0:
                    pe.wait_ge(x_in[b], 16)
                if g >= 2:
                    pe.wait_ge(x_low, g - 1)
                for q in range(4):
                    last = nc.tensor.transpose(pst[g % 2][:, q * P:(q + 1) * P],
                                               x_tok[:, b * TPB + half * 4 + q, :], ident[:])
                last.then_inc(x_turned, 1)
            pe.wait_ge(small_in, 16 * N_SMALL)
            pe.wait_ge(x_low, 2 * B)
            nc.tensor.transpose(pst[0][:, 0:E], r_w[:], ident[0:E, 0:E]).then_inc(r_turned, 1)
            pe.wait_ge(folded, 1)
            for half in range(2):
                if half:
                    pe.wait_ge(z_kept, half)
                n = 0
                for b in range(B):
                    for a, w in ((0, 0), (1, 0), (0, 1)):
                        last = nc.tensor.matmul(pz[:], ws[:, w, b, :],
                                                xT[:, a, b, HALO + half * 512:HALO + (half + 1) * 512],
                                                start=(n == 0), stop=(n == 3 * B - 1))
                        n += 1
                last.then_inc(z_done, 1)
            pe.wait_ge(p_exp, 1)
            for j in range(TPB):
                last = nc.tensor.transpose(pp[:, j * P:(j + 1) * P], lq[:, j * P:(j + 1) * P], ident[:])
            last.then_inc(p_turned, 1)
            pe.wait_ge(tabs_in, 48)
            pe.wait_ge(p_kept, 1)
            pv = p_tok[:].rearrange("p j b k -> p (j b k)")
            for h in range(2):
                nc.tensor.matmul(pp[:, h * 512:(h + 1) * 512], tri[:], pv[:, h * 512:(h + 1) * 512],
                                 start=True, stop=True)
                last = nc.tensor.matmul(pt[:, h * 512:(h + 1) * 512], ones[:], pv[:, h * 512:(h + 1) * 512],
                                        start=True, stop=True)
            last.then_inc(sums, 1)

        @block.vector
        def _(dve):
            n = [0]

            def link(ins):
                n[0] += 1
                ins.then_inc(dchain, 1)
                dve.wait_ge(dchain, n[0])

            nc.vector.memset(ones[:], 1.0)
            nc.vector.memset(half_pi[:], HALF_PI)
            nc.vector.memset(xT[:, :, :, 0:HALO].bitcast(F32), 0.0)
            nc.vector.memset(xT[:, :, :, HALO + L:].bitcast(F32), 0.0)
            nc.vector.memset(zs[:, 0:HALO], 0.0)
            nc.vector.memset(x_tok[:, NT, :], 0.0)
            link(nc.vector.memset(ws_f[:], 0.0))
            dve.wait_ge(w_arrived, 16)
            for b in range(B):
                last = nc.vector.tensor_copy(ws_f[:, b, b * K:(b + 1) * K], w_in[:, KH:KH + K])
            link(last)
            link(nc.vector.tensor_copy(ws[:, 0], ws_f[:]))
            nc.vector.tensor_tensor(ws[:, 1], ws_f[:], ws[:, 0].bitcast(F32), ALU.subtract).then_inc(folded, 1)
            dve.wait_ge(small_in, 16 * N_SMALL)
            link(nc.vector.tensor_scalar(sp[:, 2:3], slope_raw[:], -1.0, None, ALU.mult))
            link(nc.vector.tensor_tensor(sp[:, 0:1], slope_raw[:], sp[:, 2:3], ALU.min))
            nc.vector.sem_inc(soft_in, 1)
            for g in range(2 * B):
                b, half = g // 2, g % 2
                dve.wait_ge(x_high, g + 1)
                hi = xT[:, 0, b, HALO + half * 512:HALO + (half + 1) * 512]
                nc.vector.tensor_tensor(xT[:, 1, b, HALO + half * 512:HALO + (half + 1) * 512],
                                        pst[g % 2][:], hi.bitcast(F32), ALU.subtract).then_inc(x_low, 1)
            dve.wait_ge(soft_exp, 1)
            ex, zt, z2, acc = sp[:, 1:2], sp[:, 3:4], sp[:, 4:5], sp[:, 5:6]
            link(nc.vector.tensor_scalar(zt, ex, 2.0, None, ALU.add))
            link(nc.vector.reciprocal(z2, zt))
            link(nc.vector.tensor_tensor(zt, z2, ex, ALU.mult))
            link(nc.vector.tensor_tensor(z2, zt, zt, ALU.mult))
            link(nc.vector.tensor_scalar(acc, z2, 1.0 / 17, 1.0 / 15, ALU.mult, ALU.add))
            for k in (13, 11, 9, 7, 5, 3, 1):
                link(nc.vector.tensor_tensor(acc, acc, z2, ALU.mult))
                link(nc.vector.tensor_scalar(acc, acc, 1.0 / k, None, ALU.add))
            link(nc.vector.tensor_tensor(acc, acc, zt, ALU.mult))
            link(nc.vector.tensor_scalar(acc, acc, 2.0, None, ALU.mult))
            link(nc.vector.tensor_scalar(sp[:, 6:7], slope_raw[:], 0.0, None, ALU.max))
            link(nc.vector.tensor_tensor(acc, acc, sp[:, 6:7], ALU.add))
            link(nc.vector.tensor_scalar(sp[:, 7:8], acc, -1.0, None, ALU.mult))
            dve.wait_ge(r_turned, 1)
            nc.vector.tensor_copy(routerT[:], pst[0][:, 0:E])
            link(nc.vector.tensor_tensor(wconv_f[:], taps_row[:],
                                         w_in[:, 0:KH].unsqueeze(1).broadcast_to([P, TAPS, KH]), ALU.mult))
            link(nc.vector.tensor_copy(wconv[:, 0], wconv_f[:]))
            nc.vector.tensor_tensor(wconv[:, 1], wconv_f[:], wconv[:, 0].bitcast(F32), ALU.subtract)
            link(nc.vector.tensor_scalar(theta_k[:], theta_k[:], 0.15915494309189535, None, ALU.mult))
            link(nc.vector.tensor_tensor(th_f[:].rearrange("p (c m) -> p c m", m=M),
                                         ident[:].unsqueeze(2).broadcast_to([P, P, M]),
                                         theta_k[:].unsqueeze(1).broadcast_to([P, P, M]), ALU.mult))
            link(nc.vector.tensor_copy(thblk[:, 0], th_f[:]))
            nc.vector.tensor_tensor(thblk[:, 1], th_f[:], thblk[:, 0].bitcast(F32), ALU.subtract)
            link(nc.vector.tensor_tensor(coef[:], norm[:], diag[:], ALU.mult))
            wv = w_in[:, KH + K:TOTAL].rearrange("p (q h m r) -> p q h m r", q=KQ, h=H, m=M)
            for q in range(KQ):
                qr, qi = wv[:, q, :, :, 0], wv[:, q, :, :, 1]
                ca = coef[:, 0, :].unsqueeze(2).broadcast_to([P, H, M])
                cb = coef[:, 1, :].unsqueeze(2).broadcast_to([P, H, M])
                v = [t[:, i, q, :].rearrange("p (h m) -> p h m", m=M) for t in (wq_f, wq_t) for i in range(2)]
                nc.vector.tensor_tensor(v[0], qi, ca, ALU.mult)
                nc.vector.tensor_tensor(v[2], qr, cb, ALU.mult)
                nc.vector.tensor_tensor(v[1], qr, ca, ALU.mult)
                last = nc.vector.tensor_tensor(v[3], qi, cb, ALU.mult)
            link(last)
            link(nc.vector.scalar_tensor_tensor(wq_f[:, 0], wq_f[:, 0], -1.0, wq_t[:, 0], ALU.mult, ALU.subtract))
            link(nc.vector.tensor_tensor(wq_f[:, 1], wq_f[:, 1], wq_t[:, 1], ALU.subtract))
            wf = wq_f[:].rearrange("p i q m -> p (i q m)")
            link(nc.vector.tensor_copy(wq[:, 0], wf))
            nc.vector.tensor_tensor(wq[:, 1], wf, wq[:, 0].bitcast(F32), ALU.subtract)
            dve.wait_ge(z_kept, 2)
            link(nc.vector.tensor_scalar(lp[:], zs[:, 0:L], taps_s[:, 0:1], None, ALU.mult))
            for t in range(1, TAPS):
                link(nc.vector.scalar_tensor_tensor(lp[:], zs[:, t:t + L], taps_s[:, t:t + 1], lp[:],
                                                    ALU.mult, ALU.add))
            link(nc.vector.tensor_scalar(lp[:], lp[:], score[:], 20.0, ALU.mult, ALU.min))
            link(nc.vector.tensor_scalar(lp[:], lp[:], -20.0, None, ALU.max))
            dve.wait_ge(tabs_in, 48)
            nc.vector.scalar_tensor_tensor(lp[:], dist[:], sp[:, 7:8], lp[:], ALU.mult, ALU.add
                                           ).then_inc(lp_ready, 1)
            dve.wait_ge(p_turned, 1)
            nc.vector.tensor_copy(p_tok[:].rearrange("p j b k -> p (j b k)"), pp[:]).then_inc(p_kept, 1)
            dve.wait_ge(sums, 1)
            link(nc.vector.tensor_copy(tot[:].rearrange("p j c -> p (j c)"), pt[:]))
            for j in range(1, TPB):
                link(nc.vector.tensor_tensor(tot[:, j], tot[:, j], tot[:, j - 1], ALU.add))
            nc.vector.tensor_copy(den[:, 0], pp[:, 0:B * K])
            link(nc.vector.tensor_tensor(den[:, 1:], pp[:].rearrange("p (j c) -> p j c", j=TPB)[:, 1:],
                                         tot[:, 0:TPB - 1], ALU.add))
            dv = den[:].rearrange("p j c -> p (j c)")
            link(nc.vector.tensor_scalar(dv, dv, 1e-4, None, ALU.max))
            nc.vector.reciprocal(inv_den[:].rearrange("p j b k -> p (j b k)"), dv)


def memory(nc, xT, y_all, p_tok, inv_den, tri, wconv, wq, thblk, half_pi):
    with ExitStack() as c:
        def sb(name, shape, dt=F32):
            return c.enter_context(nc.sbuf_tensor(name, shape, dt))

        def ps(name, shape):
            return c.enter_context(nc.psum_tensor(name, shape, F32))

        def sem(name):
            return c.enter_context(nc.semaphore(name))

        x_st = sb("x_st", [P, 2, 2, P], F32R)
        k_st = sb("k_st", [P, 2, 2, P], F32R)
        rounded = sb("rounded", [P, 2, NF])
        frac = sb("frac", [P, 2, NF])
        afrac = sb("afrac", [P, 2, NF])
        feat = sb("feat", [P, 2, 2, NF])
        wfeat = sb("wfeat", [P, 2, 2, NF])
        query = sb("query", [P, B, 2 * KQ * HM])
        prod = sb("prod", [P, 2, NF])
        y_raw = sb("y_raw", [P, KH])
        last_rows = sb("last_rows", [P, B, 2 * NF])
        ph = ps("ph", [P, NF])
        nsum = ps("nsum", [P, 2 * NF])
        pk = ps("pk", [P, P])
        pq = ps("pq", [P, 2 * KQ * HM])

        x_ready = sem("x_ready")
        k_done = sem("k_done")
        k_high = sem("k_high")
        k_low = sem("k_low")
        q_done = sem("q_done")
        q_kept = sem("q_kept")
        ph_done = sem("ph_done")
        rnd_done = sem("rnd_done")
        frac_done = sem("frac_done")
        abs_done = sem("abs_done")
        feat_done = sem("feat_done")
        wfeat_done = sem("wfeat_done")
        carried = [sem(f"carried{b}") for b in range(B)]
        carry_due = sem("carry_due")
        sum_done = sem("sum_done")
        prod_done = sem("prod_done")
        rows_kept = sem("rows_kept")
        red_done = sem("red_done")
        y_done = sem("y_done")
        block = c.enter_context(nc.Block())

        def steps(eng, front, body):
            front()
            body(0, True, False)
            with eng.Fori(1, TPB - 1) as step:
                body(step, False, False)
            body(TPB - 1, False, True)

        def ahead(step, b, n):
            return (step, b + n) if b + n < B else (step + 1, b + n - B)

        @block.tensor
        def _(pe):
            def values(step, b, lead=False):
                i, s = B * step + b, b % 2
                if not lead or b > 0:
                    pe.wait_ge(k_low, i)
                n = 0
                for t in range(TAPS):
                    for a, w in ((0, 0), (1, 0), (0, 1)):
                        last = nc.tensor.matmul(pk[:], wconv[:, w, t, :],
                                                xT[:, a, b, bass.ds(step * P + t, P)],
                                                start=(n == 0), stop=(n == 3 * TAPS - 1))
                        n += 1
                last.then_inc(k_done, 1)

            def phases(step, b, lead=False):
                i, s = B * step + b, b % 2
                pe.wait_ge(x_ready, i + 1)
                if not lead or b > 0:
                    pe.wait_ge(q_kept, i)
                for n, (a, w) in enumerate(((0, 0), (1, 0), (0, 1))):
                    last = nc.tensor.matmul(pq[:], x_st[:, s, a, :], wq[:, w, :], start=(n == 0), stop=(n == 2))
                last.then_inc(q_done, 1)
                pe.wait_ge(k_low, i + 1)
                if not lead or b > 0:
                    pe.wait_ge(frac_done, i)
                for h in range(2):
                    for n, (a, w) in enumerate(((0, 0), (1, 0), (0, 1))):
                        last = nc.tensor.matmul(ph[:, h * 512:(h + 1) * 512], k_st[:, s, a, :],
                                                thblk[:, w, h * 512:(h + 1) * 512], start=(n == 0), stop=(n == 2))
                last.then_inc(ph_done, 1)

            def sums(step, b, first):
                i, s = B * step + b, b % 2
                pe.wait_ge(wfeat_done, i + 1)
                if not first:
                    pe.wait_ge(carried[b], 16 * step)
                for h in range(2):
                    if not (first and b == 0):
                        pe.wait_ge(prod_done, 2 * i - 1 + h)
                        pe.wait_ge(rows_kept, 2 * i - 1 + h)
                    for q in range(2):
                        o = h * NF + q * 512
                        last = nc.tensor.matmul(nsum[:, o:o + 512], tri[:],
                                                wfeat[:, s, h, q * 512:(q + 1) * 512], start=True, stop=True)
                    last.then_inc(sum_done, 1)

            def front():
                for b in range(3):
                    values(0, b, True)
                    if b < 2:
                        phases(0, b, True)

            def body(step, first, last):
                for b in range(B):
                    if not (last and b + 2 >= B):
                        phases(*ahead(step, b, 2))
                    if not (last and b + 3 >= B):
                        values(*ahead(step, b, 3))
                    sums(step, b, first)
            steps(pe, front, body)

        @block.scalar
        def _(act):
            def k_part(step, b, lead=False):
                i, s = B * step + b, b % 2
                act.wait_ge(k_done, i + 1)
                if not lead or b >= 2:
                    act.wait_ge(ph_done, i - 1)
                nc.scalar.copy(k_st[:, s, 0, :], pk[:]).then_inc(k_high, 1)

            def rounding(step, b, lead=False):
                i, s = B * step + b, b % 2
                act.wait_ge(ph_done, i + 1)
                if not lead:
                    act.wait_ge(frac_done, i - 1)
                nc.scalar.activation(rounded[:, s, :], ph[:], ACT.Copy, bias=ROUND).then_inc(rnd_done, 1)
                act.wait_ge(q_done, i + 1)
                if not (lead or isinstance(step, int) and step == 0):
                    act.wait_ge(prod_done, 2 * i - 6)
                nc.scalar.copy(query[:, b, :], pq[:]).then_inc(q_kept, 1)

            def sine(step, b, lead=False):
                i, s = B * step + b, b % 2
                act.wait_ge(frac_done, i + 1)
                nc.scalar.activation(afrac[:, s, :], frac[:, s, :], ACT.Abs).then_inc(abs_done, 1)
                if not lead:
                    act.wait_ge(wfeat_done, i - 1)
                nc.scalar.activation(feat[:, s, 0, :], frac[:, s, :], ACT.Sin, scale=TURN)

            def cosine(step, b):
                i, s = B * step + b, b % 2
                act.wait_ge(abs_done, i + 1)
                nc.scalar.activation(feat[:, s, 1, :], afrac[:, s, :], ACT.Sin, scale=-TURN,
                                     bias=half_pi[:]).then_inc(feat_done, 1)

            def rows(step, b, h, first):
                i = B * step + b
                if not first:
                    act.wait_ge(carried[b], 16 * step)
                act.wait_ge(prod_done, 2 * i + 1 + h)
                nc.scalar.copy(last_rows[96:P, b, h * NF:(h + 1) * NF], nsum[96:P, h * NF:(h + 1) * NF]
                               ).then_inc(rows_kept, 1)

            def front():
                for b in range(3):
                    k_part(0, b, True)
                    if b < 2:
                        rounding(0, b, True)
                        sine(0, b, True)
                        cosine(0, b)

            def body(step, first, last):
                for b in range(B):
                    if not (last and b + 2 >= B):
                        rounding(*ahead(step, b, 2))
                    if not (last and b + 3 >= B):
                        k_part(*ahead(step, b, 3))
                    if not (last and b + 2 >= B):
                        sine(*ahead(step, b, 2))
                    rows(step, b, 0, first)
                    if not (last and b + 2 >= B):
                        cosine(*ahead(step, b, 2))
                    rows(step, b, 1, first)
            steps(act, front, body)

        @block.vector
        def _(dve):
            def x_part(step, b, lead=False):
                i, s = B * step + b, b % 2
                if not lead or b >= 2:
                    dve.wait_ge(q_done, i - 1)
                nc.vector.tensor_copy(x_st[:, s], xT[:, :, b, bass.ds(step * P + HALO, P)].bitcast(F32)
                                      ).then_inc(x_ready, 1)

            def k_part(step, b, lead=False):
                i, s = B * step + b, b % 2
                dve.wait_ge(k_high, i + 1)
                nc.vector.tensor_tensor(k_st[:, s, 1, :], pk[:], k_st[:, s, 0, :].bitcast(F32), ALU.subtract
                                        ).then_inc(k_low, 1)

            def fraction(step, b, lead=False):
                i, s = B * step + b, b % 2
                dve.wait_ge(rnd_done, i + 1)
                if not lead:
                    dve.wait_ge(feat_done, i - 1)
                nc.vector.scalar_tensor_tensor(frac[:, s, :], rounded[:, s, :], -ROUND, ph[:],
                                               ALU.add, ALU.subtract).then_inc(frac_done, 1)

            def read_out(step, b, first):
                i, s = B * step + b, b % 2
                dve.wait_ge(q_kept, i + 1)
                if not (first and b == 0):
                    dve.wait_ge(red_done, i)
                for h in range(2):
                    dve.wait_ge(sum_done, 2 * i + 1 + h)
                    nv = nsum[:, h * NF:(h + 1) * NF].rearrange("p (q r c) -> p q r c", q=KQ, r=REP)
                    qv = query[:, b, h * KQ * HM:(h + 1) * KQ * HM].rearrange("p (q c) -> p q c", q=KQ)
                    nc.vector.tensor_tensor(prod[:, h, :].rearrange("p (q r c) -> p q r c", q=KQ, r=REP),
                                            nv, qv.unsqueeze(2).broadcast_to([P, KQ, REP, HM]), ALU.mult
                                            ).then_inc(prod_done, 1)
                dve.wait_ge(prod_done, 2 * i + 2)
                if not (first and b == 0):
                    dve.wait_ge(y_done, i)
                nc.vector.tensor_reduce(y_raw[:], prod[:].rearrange("p h (c m) -> p c h m", m=M), AX.XY, ALU.add
                                        ).then_inc(red_done, 1)
                dve.wait_ge(red_done, i + 1)
                nc.vector.tensor_tensor(
                    y_all[:, bass.ds(step + b * TPB, 1), :].rearrange("p o (k h) -> p (o k) h", h=H),
                    y_raw[:].rearrange("p (k h) -> p k h", h=H),
                    inv_den[:, bass.ds(step, 1), b, :].rearrange("p o k -> p (o k)").unsqueeze(2)
                    .broadcast_to([P, K, H]), ALU.mult).then_inc(y_done, 1)

            def front():
                for b in range(3):
                    x_part(0, b, True)
                    k_part(0, b, True)
                    if b < 2:
                        fraction(0, b, True)

            def body(step, first, last):
                for b in range(B):
                    if not (last and b + 2 >= B):
                        fraction(*ahead(step, b, 2))
                    if not (last and b + 3 >= B):
                        x_part(*ahead(step, b, 3))
                        k_part(*ahead(step, b, 3))
                    read_out(step, b, first)
            steps(dve, front, body)

        @block.gpsimd
        def _(pool):
            def weigh(step, b, lead, first):
                i, s = B * step + b, b % 2
                pool.wait_ge(feat_done, i + 1)
                if not lead:
                    pool.wait_ge(sum_done, 2 * i - 2)
                pv = p_tok[:, bass.ds(step, 1), b, :].rearrange("p o k -> p (o k)").unsqueeze(2)
                for h in range(2):
                    ins = nc.gpsimd.tensor_tensor(wfeat[:, s, h].rearrange("p (k c) -> p k c", k=K),
                                                  feat[:, s, h].rearrange("p (k c) -> p k c", k=K),
                                                  pv.broadcast_to([P, K, HM]), ALU.mult)
                ins.then_inc(wfeat_done, 1)
                if not first:
                    pool.wait_ge(wfeat_done, i + 1)
                    pool.wait_ge(rows_kept, 2 * (i - B) + 2)
                    nc.gpsimd.sem_inc(carry_due, 1)
                    pool.dma_start(wfeat[0:1, s].rearrange("p h c -> p (h c)"),
                                   last_rows[P - 1:P, b, :], accum_op=ALU.add).then_inc(carried[b], 16)

            for b in range(B):
                weigh(0, b, b < 2, True)
            with pool.Fori(1, TPB) as step:
                for b in range(B):
                    weigh(step, b, False, False)


def mixture(nc, x_tok, xT, y_all, ident, w_out, routerT, w_fc, w_proj, shared_fc, shared_proj, out):
    GT = 4
    NG = NT // GT
    with ExitStack() as c:
        def sb(name, shape, dt=F32, cc=c):
            return cc.enter_context(nc.sbuf_tensor(name, shape, dt))

        def ps(name, shape, cc):
            return cc.enter_context(nc.psum_tensor(name, shape, F32))

        def sem(name, cc):
            return cc.enter_context(nc.semaphore(name))

        w1 = sb("w1", [P, 2, NE, FF], F32R)
        w2 = sb("w2", [P, NE, FC, D])
        combine = sb("combine", [P, NT, E])
        with ExitStack() as k:
            w_nat = sb("w_nat", [P, 2, 2, FC, D], F32, k)
            pw = [ps(f"pw{i}", [P, 512], k) for i in range(4)]
            w_in = [sem(f"w_in_slot{i}", k) for i in range(2)]
            turned = sem("w_turned", k)
            w_high = sem("w_high", k)
            w_low = sem("w_low", k)
            sy = sb("sy", [P, GT * KH], F32, k)
            syT = sb("syT", [P, GT, P], F32, k)
            res = sb("res", [P, GT, D], F32, k)
            stats = sb("stats", [P, GT, 6], F32, k)
            mv = sb("mv", [P, GT, 2], F32, k)
            std = sb("std", [P, GT], F32, k)
            rstd = sb("rstd", [P, GT], F32, k)
            eps = sb("eps1", [P, 1], F32, k)
            xn = sb("xn", [P, GT, D], F32, k)
            xnT = sb("xnT", [P, GT, P], F32, k)
            logits = sb("logits", [P, NT, E], F32, k)
            ord_ = sb("ord_", [P, NT, E], F32, k)
            tA = sb("tA", [P, NT, E], F32, k)
            tB = sb("tB", [P, NT, E], F32, k)
            oh = sb("oh", [P, 2, NT, E], F32, k)
            mx = sb("mx", [P, 6, NT], F32, k)
            pa = ps("pa", [P, 512], k)
            po = ps("po", [P, 512], k)
            px = ps("px", [P, 512], k)
            pl = ps("pl", [P, GT * E], k)
            silu_done = sem("silu_done", k)
            yT_done = sem("yT_done", k)
            yT_kept = sem("yT_kept", k)
            proj_done = sem("proj_done", k)
            var_done = sem("var_done", k)
            std_done = sem("std_done", k)
            xn_done = sem("xn_done", k)
            xnT_done = sem("xnT_done", k)
            xnT_kept = sem("xnT_kept", k)
            xn_split = sem("xn_split", k)
            log_done = sem("log_done", k)
            vch = sem("vch", k)
            log_all = sem("log_all", k)
            stats_due = sem("stats_due", k)
            exp_done = sem("exp_done", k)
            block = k.enter_context(nc.Block())

            def experts(eng, body):
                body(0, 0, True)
                body(1, 1, True)
                with eng.Fori(2, E - 1, 2) as e:
                    body(e, 0, False)
                    body(e + 1, 1, False)
                body(E, 0, False)

            @block.sync
            def _(sp):
                def load(e, s, first):
                    if not first:
                        sp.wait_ge(turned, 2 * (e - 2) + 2)
                    if isinstance(e, int) and e == E:
                        fc, pj = shared_fc, shared_proj
                    else:
                        fc = w_fc[bass.ds(e, 1), :, :].rearrange("o f d -> (o f) d")
                        pj = w_proj[bass.ds(e, 1), :, :].rearrange("o d f -> (o d) f")
                    sp.dma_start(w_nat[:, s, 0], fc.rearrange("(c p) d -> p c d", p=P)).then_inc(w_in[s], 16)
                    sp.dma_start(w_nat[:, s, 1].rearrange("p c d -> p (c d)"), pj).then_inc(w_in[s], 16)
                experts(sp, load)

            @block.tensor
            def _(pe):
                def turn(e, s, first):
                    pe.wait_ge(w_in[s], 16 * (e - s) + 32)
                    for m in range(2):
                        if not first:
                            pe.wait_ge(w_low if m == 0 else w_high, (e - 1) if m == 0 else 2 * e - 2)
                        for q in range(FC):
                            last = nc.tensor.transpose(pw[2 * s + m][:, q * P:(q + 1) * P], w_nat[:, s, m, q, :],
                                                       ident[:])
                        last.then_inc(turned, 1)
                experts(pe, turn)

                def group(g, first):
                    pe.wait_ge(silu_done, g + 1)
                    for t in range(GT):
                        last = nc.tensor.transpose(pa[:, t * P:(t + 1) * P], sy[:, t * KH:(t + 1) * KH], ident[:])
                    last.then_inc(yT_done, 1)
                    pe.wait_ge(yT_kept, g + 1)
                    for t in range(GT):
                        last = nc.tensor.matmul(po[:, t * D:(t + 1) * D], syT[:, t, :], w_out[:], start=True, stop=True)
                    last.then_inc(proj_done, 1)
                    pe.wait_ge(xn_done, g + 1)
                    for t in range(GT):
                        last = nc.tensor.transpose(px[:, t * P:(t + 1) * P], xn[:, t, :], ident[:])
                    last.then_inc(xnT_done, 1)
                    pe.wait_ge(xnT_kept, g + 1)
                    for t in range(GT):
                        last = nc.tensor.matmul(pl[:, t * E:(t + 1) * E], xnT[:, t, :], routerT[:], start=True, stop=True)
                    last.then_inc(log_done, 1)
                group(0, True)
                with pe.Fori(1, NG) as g:
                    group(g, False)

            @block.scalar
            def _(act):
                def keep(e, s, first):
                    act.wait_ge(turned, 2 * e + 1)
                    nc.scalar.copy(w1[:, 0, bass.ds(e, 1), :].rearrange("p o f -> p (o f)"), pw[2 * s][:]
                                   ).then_inc(w_high, 1)
                    act.wait_ge(turned, 2 * e + 2)
                    nc.scalar.copy(w2[:, bass.ds(e, 1)].rearrange("p o c d -> p (o c d)"), pw[2 * s + 1][:]
                                   ).then_inc(w_high, 1)
                experts(act, keep)

                def group(g, first):
                    if not first:
                        act.wait_ge(yT_done, g)
                    nc.scalar.activation(sy[:], y_all[:, bass.ds(g * GT, GT), :].rearrange("p t c -> p (t c)"),
                                         ACT.Silu).then_inc(silu_done, 1)
                    act.wait_ge(yT_done, g + 1)
                    if not first:
                        act.wait_ge(proj_done, g)
                    nc.scalar.copy(syT[:].rearrange("p t c -> p (t c)"), pa[:]).then_inc(yT_kept, 1)
                    act.wait_ge(var_done, g + 1)
                    nc.scalar.activation(std[:], mv[:, :, 1], ACT.Sqrt, bias=eps[:]).then_inc(std_done, 1)
                    act.wait_ge(xnT_done, g + 1)
                    if not first:
                        act.wait_ge(log_done, g)
                        act.wait_ge(xn_split, g)
                    nc.scalar.copy(xnT[:].rearrange("p t c -> p (t c)"), px[:]).then_inc(xnT_kept, 1)
                group(0, True)
                with act.Fori(1, NG) as g:
                    group(g, False)
                act.wait_ge(log_all, 1)
                nc.scalar.activation(tB[:], tA[:], ACT.Exp).then_inc(exp_done, 1)

            @block.vector
            def _(dve):
                nv = [0]

                nc.vector.memset(eps[:], EPS)

                def keep(e, s, first):
                    dve.wait_ge(w_high, 2 * e + 1)
                    nc.vector.tensor_tensor(w1[:, 1, bass.ds(e, 1), :].rearrange("p o f -> p (o f)"), pw[2 * s][:],
                                            w1[:, 0, bass.ds(e, 1), :].rearrange("p o f -> p (o f)").bitcast(F32),
                                            ALU.subtract).then_inc(w_low, 1)
                experts(dve, keep)
                for e in range(E):
                    nc.vector.memset(ord_[:, :, e], float(E - e))

                CH = 5 + GT

                def group(g, first):
                    at = [0]

                    def link(ins):
                        at[0] += 1
                        ins.then_inc(vch, 1)
                        dve.wait_ge(vch, g * CH + at[0])

                    dve.wait_ge(proj_done, g + 1)
                    if not first:
                        dve.wait_ge(xnT_done, g)
                    link(nc.vector.tensor_tensor(res[:].rearrange("p t c -> p (t c)"), po[:],
                                                 x_tok[:, bass.ds(g * GT, GT), :].rearrange("p t c -> p (t c)"),
                                                 ALU.add))
                    for t in range(GT):
                        last = nc.vector.bn_stats(stats[:, t, :], res[:, t, :])
                    link(last)
                    nc.vector.sem_inc(stats_due, 1)
                    for t in range(GT):
                        last = nc.vector.bn_aggr(mv[:, t, :], stats[:, t, :])
                    last.then_inc(var_done, 1)
                    dve.wait_ge(std_done, g + 1)
                    link(nc.vector.reciprocal(rstd[:], std[:]))
                    for t in range(GT):
                        link(nc.vector.tensor_scalar(xn[:, t, :], res[:, t, :], mv[:, t, 0:1], rstd[:, t:t + 1],
                                                     ALU.subtract, ALU.mult))
                    nc.vector.sem_inc(xn_done, 1)
                    link(nc.vector.tensor_copy(x_tok[:, bass.ds(g * GT, GT), :], xn[:]))
                    dve.wait_ge(xnT_kept, g + 1)
                    xv = xnT[:].rearrange("p t c -> p (t c)")
                    hi = xT[:].rearrange("p a b l -> p a (b l)")[:, 0, bass.ds(g * GT * P, GT * P)]
                    lo = xT[:].rearrange("p a b l -> p a (b l)")[:, 1, bass.ds(g * GT * P, GT * P)]
                    link(nc.vector.tensor_copy(hi, xv))
                    nc.vector.tensor_tensor(lo, xv, hi.bitcast(F32), ALU.subtract).then_inc(xn_split, 1)
                    dve.wait_ge(log_done, g + 1)
                    nc.vector.tensor_copy(logits[:, bass.ds(g * GT, GT), :].rearrange("p t e -> p (t e)"), pl[:])
                group(0, True)
                with dve.Fori(1, NG) as g:
                    group(g, False)
                done = NG * CH
                cnt = [done]

                def link(ins):
                    cnt[0] += 1
                    ins.then_inc(vch, 1)
                    dve.wait_ge(vch, cnt[0])

                def over_e(v):
                    return v.unsqueeze(2).broadcast_to([P, NT, E])

                link(nc.vector.memset(mx[:], 0.0))
                link(nc.vector.tensor_reduce(mx[:, 0], logits[:], AX.X, ALU.max))
                nc.vector.tensor_tensor(tA[:], logits[:], over_e(mx[:, 0]), ALU.subtract).then_inc(log_all, 1)
                dve.wait_ge(exp_done, 1)
                link(nc.vector.tensor_reduce(mx[:, 1], tB[:], AX.X, ALU.add))
                link(nc.vector.reciprocal(mx[:, 2], mx[:, 1]))
                link(nc.vector.tensor_tensor(tB[:], tB[:], over_e(mx[:, 2]), ALU.mult))
                for r in range(2):
                    link(nc.vector.tensor_reduce(mx[:, 3 + r], tB[:], AX.X, ALU.max))
                    link(nc.vector.tensor_tensor(tA[:], tB[:], over_e(mx[:, 3 + r]), ALU.is_equal))
                    link(nc.vector.tensor_tensor(tA[:], tA[:], ord_[:], ALU.mult))
                    link(nc.vector.tensor_reduce(mx[:, 5], tA[:], AX.X, ALU.max))
                    link(nc.vector.tensor_tensor(oh[:, r], tA[:], over_e(mx[:, 5]), ALU.is_equal))
                    if r == 0:
                        link(nc.vector.scalar_tensor_tensor(tB[:], oh[:, 0], -2.0, tB[:], ALU.mult, ALU.add))
                link(nc.vector.tensor_tensor(mx[:, 0], mx[:, 3], mx[:, 4], ALU.add))
                link(nc.vector.tensor_scalar(mx[:, 0], mx[:, 0], 1e-9, None, ALU.max))
                link(nc.vector.reciprocal(mx[:, 1], mx[:, 0]))
                for r in range(2):
                    link(nc.vector.tensor_tensor(mx[:, 3 + r], mx[:, 3 + r], mx[:, 1], ALU.mult))
                    link(nc.vector.tensor_tensor(oh[:, r], oh[:, r], over_e(mx[:, 3 + r]), ALU.mult))
                link(nc.vector.tensor_tensor(combine[:], oh[:, 0], oh[:, 1], ALU.add))

        with ExitStack() as k:
            hid = [sb(f"hid{i}", [P, FC, GT * P], F32, k) for i in range(2)]
            rel = sb("rel", [P, 2, GT * P], F32, k)
            acc = sb("acc", [P, 2, GT, D], F32, k)
            stats = sb("stats2", [P, GT, 6], F32, k)
            mv = sb("mv2", [P, GT, 2], F32, k)
            std = sb("std2", [P, GT], F32, k)
            rstd = sb("rstd2", [P, GT], F32, k)
            eps = sb("eps2", [P, 1], F32, k)
            xo = sb("xo", [P, 2, GT, D], F32, k)
            phid = [ps(f"phid{i}", [P, GT * P], k) for i in range(4)]
            pout = [ps(f"pout{i}", [P, GT * D], k) for i in range(2)]
            up_done = sem("up_done", k)
            rel_done = sem("rel_done", k)
            hid_done = sem("hid_done", k)
            down_done = sem("down_done", k)
            acc_done = sem("acc_done", k)
            dch = sem("dch", k)
            var_done = sem("var2_done", k)
            std_done = sem("std2_done", k)
            xo_done = sem("xo_done", k)
            eps_set = sem("eps_set", k)
            stats_due = sem("stats2_due", k)
            stored = [sem(f"stored{i}", k) for i in range(2)]
            block = k.enter_context(nc.Block())
            xflat = xT[:].rearrange("p a b l -> p a (b l)")

            def groups(eng, body):
                body(0, 0, True)
                body(1, 1, True)
                with eng.Fori(2, NG - 1, 2) as g:
                    body(g, 0, False)
                    body(g + 1, 1, False)

            @block.tensor
            def _(pe):
                def group(g, gp, first):
                    def up(e):
                        n = g * NE + e
                        for q in range(FC):
                            if not (first and gp == 0 and e == 0):
                                pe.wait_ge(rel_done, n * FC + q - 3)
                            for m, (a, w) in enumerate(((0, 0), (1, 0), (0, 1))):
                                last = nc.tensor.matmul(phid[q][:], w1[:, w, e, q * P:(q + 1) * P],
                                                        xflat[:, a, bass.ds(g * GT * P, GT * P)],
                                                        start=(m == 0), stop=(m == 2))
                            last.then_inc(up_done, 1)

                    def down(e):
                        n = g * NE + e
                        s = (gp * NE + e) % 2
                        pe.wait_ge(hid_done, n * FC + FC)
                        if not (first and gp == 0 and e < 2):
                            pe.wait_ge(acc_done, n - 1)
                        for t in range(GT):
                            for q in range(FC):
                                last = nc.tensor.matmul(pout[s][:, t * D:(t + 1) * D],
                                                        hid[s][:, q, t * P:(t + 1) * P], w2[:, e, q, :],
                                                        start=(q == 0), stop=(q == FC - 1))
                        last.then_inc(down_done, 1)
                    up(0)
                    for e in range(NE):
                        if e + 1 < NE:
                            up(e + 1)
                        down(e)
                groups(pe, group)

            @block.scalar
            def _(act):
                def group(g, gp, first):
                    for e in range(NE):
                        n = g * NE + e
                        s = (gp * NE + e) % 2
                        for q in range(FC):
                            act.wait_ge(up_done, n * FC + q + 1)
                            if not (first and gp == 0 and e == 0 and q < 2):
                                act.wait_ge(hid_done, n * FC + q - 1)
                            nc.scalar.activation(rel[:, q % 2, :], phid[q][:], ACT.Relu).then_inc(rel_done, 1)
                            act.wait_ge(rel_done, n * FC + q + 1)
                            if q == 0 and not (first and gp == 0 and e < 2):
                                act.wait_ge(down_done, n - 1)
                            nc.scalar.activation(hid[s][:, q, :], rel[:, q % 2, :], ACT.Square).then_inc(hid_done, 1)
                    act.wait_ge(var_done, g + 1)
                    if first and gp == 0:
                        act.wait_ge(eps_set, 1)
                    nc.scalar.activation(std[:], mv[:, :, 1], ACT.Sqrt, bias=eps[:]).then_inc(std_done, 1)
                groups(act, group)

            CH = NE + 2 + GT

            @block.vector
            def _(dve):
                nc.vector.memset(eps[:], EPS).then_inc(eps_set, 1)

                def group(g, gp, first):
                    at = [0]

                    def link(ins):
                        at[0] += 1
                        ins.then_inc(dch, 1)
                        dve.wait_ge(dch, g * CH + at[0])

                    for e in range(NE):
                        n = g * NE + e
                        s = (gp * NE + e) % 2
                        dve.wait_ge(down_done, n + 1)
                        for t in range(GT):
                            base = (x_tok[:, bass.ds(g * GT + t, 1), :].rearrange("p o d -> p (o d)")
                                    if e == 0 else acc[:, gp, t, :])
                            if e < E:
                                cb = combine[:, bass.ds(g * GT + t, 1), e]
                                last = nc.vector.scalar_tensor_tensor(acc[:, gp, t, :], pout[s][:, t * D:(t + 1) * D],
                                                                      cb, base, ALU.mult, ALU.add)
                            else:
                                last = nc.vector.tensor_tensor(acc[:, gp, t, :], pout[s][:, t * D:(t + 1) * D],
                                                               base, ALU.add)
                        last.then_inc(acc_done, 1)
                        dve.wait_ge(acc_done, n + 1)
                    for t in range(GT):
                        last = nc.vector.bn_stats(stats[:, t, :], acc[:, gp, t, :])
                    link(last)
                    nc.vector.sem_inc(stats_due, 1)
                    for t in range(GT):
                        last = nc.vector.bn_aggr(mv[:, t, :], stats[:, t, :])
                    last.then_inc(var_done, 1)
                    dve.wait_ge(std_done, g + 1)
                    link(nc.vector.reciprocal(rstd[:], std[:]))
                    if not first:
                        dve.wait_ge(stored[gp], 8 * (g - gp))
                    for t in range(GT):
                        last = nc.vector.tensor_scalar(xo[:, gp, t, :], acc[:, gp, t, :], mv[:, t, 0:1],
                                                       rstd[:, t:t + 1], ALU.subtract, ALU.mult)
                    last.then_inc(xo_done, 1)
                    for _ in range(CH - at[0]):
                        nc.vector.sem_inc(dch, 1)
                groups(dve, group)

            @block.sync
            def _(sp):
                ov = out.rearrange("b (j p) d -> (b j) p d", p=P)

                def group(g, gp, first):
                    sp.wait_ge(xo_done, g + 1)
                    sp.dma_start(ov[bass.ds(g * GT, GT)].rearrange("j p d -> p j d"), xo[:, gp]
                                 ).then_inc(stored[gp], 16)
                groups(sp, group)
                for i in range(2):
                    sp.wait_ge(stored[i], 16 * NG // 2)


INS = ["L0_attn_x", "L0_attn_W_in", "L0_attn_conv_k", "L0_attn_theta", "L0_attn_decay_slopes",
       "L0_attn_anchor_slopes", "L0_attn_score_scale", "L0_attn_W_re", "L0_attn_W_im",
       "L0_attn_norm_scale", "L0_attn_W_out", "L0_ffn_router_w", "L0_ffn_w_fc", "L0_ffn_w_proj",
       "L0_ffn_shared_fc", "L0_ffn_shared_proj"]


def kernel(**inputs):
    import numpy as np
    import concourse.bacc as bacc
    from concourse import mybir as mb
    from concourse.bass_utils import run_bass_kernel_spmd as run

    nc = bacc.Bacc("TRN2", target_bir_lowering=False, num_devices=1)
    tables = np.zeros((P, 2 * P + L), np.float32)
    tables[:, 0:P] = np.eye(P)
    tables[:, P:2 * P] = np.triu(np.ones((P, P)))
    pos = np.arange(L)
    tables[:, 2 * P:] = [(L - 1 - pos) if k % K < K - 4 else pos for k in range(P)]
    arrays = {n: np.ascontiguousarray(inputs[n]) for n in INS}
    arrays["tables"] = tables
    args = [nc.dram_tensor(n, a.shape, mb.dt.float32, kind="ExternalInput").ap() for n, a in arrays.items()]
    out = nc.dram_tensor("out", (B, L, D), mb.dt.float32, kind="ExternalOutput").ap()
    build(nc, *args, out)
    r = run(nc, [arrays], core_ids=[0])
    return r.results[0]["out"]
```

```python
from contextlib import ExitStack

import concourse.bass as bass
from concourse import mybir

ALU = mybir.AluOpType
ACT = mybir.ActivationFunctionType
AX = mybir.AxisListType
F32 = mybir.dt.float32
F32R = mybir.dt.float32r
I32 = mybir.dt.int32
U32 = mybir.dt.uint32

P = 128
D = 128
B, L = 4, 1024
TPB = L // P
NT = B * TPB
K, H, M, KQ = 32, 4, 8, 4
REP = K // KQ
KH = K * H
HM = H * M
NF = KH * M
TAPS = 4
HALO = TAPS - 1
E, FF = 8, 512
FC = FF // P
NE = E + 1
GT = 4
NG = NT // GT
NTOK = B * L
ROWS = 256
TILES = (2 * NTOK + E * (ROWS - 1)) // ROWS
SLOTS = TILES * ROWS // P
ROUND = 12582912.0
TURN = 6.283185
HALF_PI = 1.5707963267948966
EPS = 1e-5


def build(nc, x, W_in, conv_k, theta, decay_slopes, anchor_slopes, score_scale, W_re, W_im,
          norm_scale, W_out, router_w, w_fc, w_proj, shared_fc, shared_proj, tables, out):
    ctx = ExitStack()

    def sb(name, shape, dt=F32, c=ctx):
        return c.enter_context(nc.sbuf_tensor(name, shape, dt))

    def ps(name, shape, c):
        return c.enter_context(nc.psum_tensor(name, shape, F32))

    with ctx:
        x_tok = sb("x_tok", [P, NT + 1, D])
        xT = sb("xT", [P, 2, B, HALO + L + P], F32R)
        y_all = sb("y_all", [P, NT, KH])
        p_tok = sb("p_tok", [P, TPB, B, K])
        inv_den = sb("inv_den", [P, TPB, B, K])
        ident = sb("ident", [P, P])
        tri = sb("tri", [P, P])
        wconv = sb("wconv", [P, 2, TAPS, KH], F32R)
        wq = sb("wq", [P, 2, 2 * KQ * HM], F32R)
        thblk = sb("thblk", [P, 2, NF], F32R)
        w_out = sb("w_out", [P, D])
        routerT = sb("routerT", [P, E])
        half_pi = sb("half_pi", [P, 1])
        rows = sb("rows", [P, P + NT])
        x1_dram = nc.dram_tensor("x1_scratch", (NTOK, D), F32, kind="Internal").ap()
        pick_dram = nc.dram_tensor("pick_scratch", (2 * NTOK, D), F32, kind="Internal").ap()

        setup(nc, x, W_in, conv_k, theta, decay_slopes, anchor_slopes, score_scale, W_re, W_im,
              norm_scale, W_out, router_w, tables, x_tok, xT, p_tok, inv_den, ident, tri, wconv, wq,
              thblk, w_out, routerT, half_pi, rows)
        memory(nc, xT, y_all, p_tok, inv_den, tri, wconv, wq, thblk, half_pi)
        mixture(nc, x_tok, y_all, ident, tri, rows, w_out, routerT, w_fc, w_proj, shared_fc, shared_proj,
                x1_dram, pick_dram, out)


def setup(nc, x, W_in, conv_k, theta, decay_slopes, anchor_slopes, score_scale, W_re, W_im,
          norm_scale, W_out, router_w, tables, x_tok, xT, p_tok, inv_den, ident, tri, wconv, wq,
          thblk, w_out, routerT, half_pi, rows):
    with ExitStack() as c:
        def sb(name, shape, dt=F32):
            return c.enter_context(nc.sbuf_tensor("setup_" + name, shape, dt))

        def ps(name, shape):
            return c.enter_context(nc.psum_tensor("setup_" + name, shape, F32))

        def sem(name):
            return c.enter_context(nc.semaphore("setup_" + name))

        TOTAL = KH + K + 2 * KQ * HM
        w_in = sb("w_in", [P, TOTAL])
        taps_row = sb("taps_row", [P, TAPS, KH])
        theta_k = sb("theta_k", [P, M])
        slope_raw = sb("slope_raw", [P, 1])
        score = sb("score", [P, 1])
        taps_s = sb("taps_s", [P, TAPS])
        dist = sb("dist", [P, L])
        diag = sb("diag", [P, 2, H])
        norm = sb("norm", [P, 2, H])
        coef = sb("coef", [P, 2, H])
        r_w = sb("r_w", [E, D])
        ones = sb("ones", [P, P])
        wconv_f = sb("wconv_f", [P, TAPS, KH])
        wq_f = sb("wq_f", [P, 2, KQ, HM])
        wq_t = sb("wq_t", [P, 2, KQ, HM])
        th_f = sb("th_f", [P, NF])
        ws_f = sb("ws_f", [P, B, P])
        ws = sb("ws", [P, 2, B, P], F32R)
        zs = sb("zs", [P, HALO + L])
        lp = sb("lp", [P, L])
        lq = sb("lq", [P, L])
        sp = sb("sp", [P, 8])
        den = sb("den", [P, TPB, B * K])
        tot = sb("tot", [P, TPB, B * K])
        pst = [ps(f"pst{i}", [P, 512]) for i in range(2)]
        pz = ps("pz", [P, 512])
        pp = ps("pp", [P, 1024])
        pt = ps("pt", [P, 1024])

        x_in = [sem(f"x_in{b}") for b in range(B)]
        w_arrived = sem("w_arrived")
        tabs_in = sem("tabs_in")
        ident_in = sem("ident_in")
        small_in = sem("small_in")
        folded = sem("folded")
        dchain = sem("dchain")
        x_turned = sem("x_turned")
        x_high = sem("x_high")
        x_low = sem("x_low")
        z_done = sem("z_done")
        z_kept = sem("z_kept")
        soft_exp = sem("soft_exp")
        soft_in = sem("soft_in")
        lp_ready = sem("lp_ready")
        p_exp = sem("p_exp")
        p_turned = sem("p_turned")
        p_kept = sem("p_kept")
        sums = sem("sums")
        den_ready = sem("den_ready")
        r_turned = sem("r_turned")
        out_kept = sem("out_kept")
        block = c.enter_context(nc.Block())
        N_SMALL = 3 * B + B + 2 + 2 + 3

        @block.sync
        def _(sp_):
            sp_.dma_start(ident[:], tables[:, 0:P]).then_inc(ident_in, 16)
            for b in range(B):
                sp_.dma_start(x_tok[:, b * TPB:(b + 1) * TPB, :],
                              x[b].rearrange("(j p) d -> p j d", p=P)).then_inc(x_in[b], 16)
            sp_.dma_start(tri[:], tables[:, P:2 * P]).then_inc(tabs_in, 16)
            sp_.dma_start(dist[:], tables[:, 2 * P:2 * P + L]).then_inc(tabs_in, 16)
            sp_.dma_start(rows[:], tables[:, 2 * P + L:]).then_inc(tabs_in, 16)
            sp_.wait_ge(tabs_in, 48)

        @block.scalar
        def _(act):
            act.dma_start(w_in[:], W_in).then_inc(w_arrived, 16)
            with nc.allow_non_contiguous_dma(reason="small parameter rows"):
                act.dma_start(taps_row[:], conv_k[:, 0, 0:KH].unsqueeze(0).broadcast_to([P, TAPS, KH])
                              ).then_inc(small_in, 16)
                for b in range(B):
                    act.dma_start(slope_raw[b * K:b * K + K - 4, :], decay_slopes.unsqueeze(1)).then_inc(small_in, 16)
                    act.dma_start(slope_raw[b * K + K - 4:(b + 1) * K, :], anchor_slopes.unsqueeze(1)
                                  ).then_inc(small_in, 16)
                    act.dma_start(score[b * K:(b + 1) * K, :], score_scale.unsqueeze(1)).then_inc(small_in, 16)
                    act.dma_start(taps_s[b * K:(b + 1) * K, :],
                                  conv_k[:, 0, KH:KH + K].rearrange("t k -> k t")).then_inc(small_in, 16)
                act.dma_start(theta_k[:], theta[0, 0].rearrange("k h m -> (k h) m")).then_inc(small_in, 16)
                for i, w in enumerate((W_re, W_im)):
                    dg = w.rearrange("a b -> (a b)")[0:H * H:H + 1]
                    act.dma_start(diag[:, i, :], dg.unsqueeze(0).broadcast_to([P, H])).then_inc(small_in, 16)
                act.dma_start(norm[:], norm_scale.rearrange("(i h) -> i h", i=2).unsqueeze(0)
                              .broadcast_to([P, 2, H])).then_inc(small_in, 16)
                act.dma_start(w_out[:], W_out).then_inc(small_in, 16)
                act.dma_start(r_w[:], router_w).then_inc(small_in, 16)
            act.wait_ge(soft_in, 1)
            nc.scalar.activation(sp[:, 1:2], sp[:, 0:1], ACT.Exp).then_inc(soft_exp, 1)
            for g in range(2 * B):
                act.wait_ge(x_turned, g + 1)
                b, half = g // 2, g % 2
                nc.scalar.copy(xT[:, 0, b, HALO + half * 512:HALO + (half + 1) * 512], pst[g % 2][:]
                               ).then_inc(x_high, 1)
            for half in range(2):
                act.wait_ge(z_done, half + 1)
                nc.scalar.copy(zs[:, HALO + half * 512:HALO + (half + 1) * 512], pz[:]).then_inc(z_kept, 1)
            act.wait_ge(lp_ready, 1)
            nc.scalar.activation(lq[:], lp[:], ACT.Exp).then_inc(p_exp, 1)

        @block.tensor
        def _(pe):
            pe.wait_ge(ident_in, 16)
            for g in range(2 * B):
                b, half = g // 2, g % 2
                if half == 0:
                    pe.wait_ge(x_in[b], 16)
                if g >= 2:
                    pe.wait_ge(x_low, g - 1)
                for q in range(4):
                    last = nc.tensor.transpose(pst[g % 2][:, q * P:(q + 1) * P],
                                               x_tok[:, b * TPB + half * 4 + q, :], ident[:])
                last.then_inc(x_turned, 1)
            pe.wait_ge(small_in, 16 * N_SMALL)
            pe.wait_ge(x_low, 2 * B)
            nc.tensor.transpose(pst[0][:, 0:E], r_w[:], ident[0:E, 0:E]).then_inc(r_turned, 1)
            pe.wait_ge(folded, 1)
            for half in range(2):
                if half:
                    pe.wait_ge(z_kept, half)
                n = 0
                for b in range(B):
                    for a, w in ((0, 0), (1, 0), (0, 1)):
                        last = nc.tensor.matmul(pz[:], ws[:, w, b, :],
                                                xT[:, a, b, HALO + half * 512:HALO + (half + 1) * 512],
                                                start=(n == 0), stop=(n == 3 * B - 1))
                        n += 1
                last.then_inc(z_done, 1)
            pe.wait_ge(p_exp, 1)
            for j in range(TPB):
                last = nc.tensor.transpose(pp[:, j * P:(j + 1) * P], lq[:, j * P:(j + 1) * P], ident[:])
            last.then_inc(p_turned, 1)
            pe.wait_ge(tabs_in, 48)
            pe.wait_ge(p_kept, 1)
            pv = p_tok[:].rearrange("p j b k -> p (j b k)")
            for h in range(2):
                nc.tensor.matmul(pp[:, h * 512:(h + 1) * 512], tri[:], pv[:, h * 512:(h + 1) * 512],
                                 start=True, stop=True)
                last = nc.tensor.matmul(pt[:, h * 512:(h + 1) * 512], ones[:], pv[:, h * 512:(h + 1) * 512],
                                        start=True, stop=True)
            last.then_inc(sums, 1)

        @block.vector
        def _(dve):
            n = [0]

            def link(ins):
                n[0] += 1
                ins.then_inc(dchain, 1)
                dve.wait_ge(dchain, n[0])

            nc.vector.memset(ones[:], 1.0)
            nc.vector.memset(half_pi[:], HALF_PI)
            nc.vector.memset(xT[:, :, :, 0:HALO].bitcast(F32), 0.0)
            nc.vector.memset(xT[:, :, :, HALO + L:].bitcast(F32), 0.0)
            nc.vector.memset(zs[:, 0:HALO], 0.0)
            nc.vector.memset(x_tok[:, NT, :], 0.0)
            link(nc.vector.memset(ws_f[:], 0.0))
            dve.wait_ge(w_arrived, 16)
            for b in range(B):
                last = nc.vector.tensor_copy(ws_f[:, b, b * K:(b + 1) * K], w_in[:, KH:KH + K])
            link(last)
            link(nc.vector.tensor_copy(ws[:, 0], ws_f[:]))
            nc.vector.tensor_tensor(ws[:, 1], ws_f[:], ws[:, 0].bitcast(F32), ALU.subtract).then_inc(folded, 1)
            dve.wait_ge(small_in, 16 * N_SMALL)
            link(nc.vector.tensor_scalar(sp[:, 2:3], slope_raw[:], -1.0, None, ALU.mult))
            link(nc.vector.tensor_tensor(sp[:, 0:1], slope_raw[:], sp[:, 2:3], ALU.min))
            nc.vector.sem_inc(soft_in, 1)
            for g in range(2 * B):
                b, half = g // 2, g % 2
                dve.wait_ge(x_high, g + 1)
                hi = xT[:, 0, b, HALO + half * 512:HALO + (half + 1) * 512]
                nc.vector.tensor_tensor(xT[:, 1, b, HALO + half * 512:HALO + (half + 1) * 512],
                                        pst[g % 2][:], hi.bitcast(F32), ALU.subtract).then_inc(x_low, 1)
            dve.wait_ge(soft_exp, 1)
            ex, zt, z2, acc = sp[:, 1:2], sp[:, 3:4], sp[:, 4:5], sp[:, 5:6]
            link(nc.vector.tensor_scalar(zt, ex, 2.0, None, ALU.add))
            link(nc.vector.reciprocal(z2, zt))
            link(nc.vector.tensor_tensor(zt, z2, ex, ALU.mult))
            link(nc.vector.tensor_tensor(z2, zt, zt, ALU.mult))
            link(nc.vector.tensor_scalar(acc, z2, 1.0 / 17, 1.0 / 15, ALU.mult, ALU.add))
            for k in (13, 11, 9, 7, 5, 3, 1):
                link(nc.vector.tensor_tensor(acc, acc, z2, ALU.mult))
                link(nc.vector.tensor_scalar(acc, acc, 1.0 / k, None, ALU.add))
            link(nc.vector.tensor_tensor(acc, acc, zt, ALU.mult))
            link(nc.vector.tensor_scalar(acc, acc, 2.0, None, ALU.mult))
            link(nc.vector.tensor_scalar(sp[:, 6:7], slope_raw[:], 0.0, None, ALU.max))
            link(nc.vector.tensor_tensor(acc, acc, sp[:, 6:7], ALU.add))
            link(nc.vector.tensor_scalar(sp[:, 7:8], acc, -1.0, None, ALU.mult))
            dve.wait_ge(r_turned, 1)
            nc.vector.tensor_copy(routerT[:], pst[0][:, 0:E])
            link(nc.vector.tensor_tensor(wconv_f[:], taps_row[:],
                                         w_in[:, 0:KH].unsqueeze(1).broadcast_to([P, TAPS, KH]), ALU.mult))
            link(nc.vector.tensor_copy(wconv[:, 0], wconv_f[:]))
            nc.vector.tensor_tensor(wconv[:, 1], wconv_f[:], wconv[:, 0].bitcast(F32), ALU.subtract)
            link(nc.vector.tensor_scalar(theta_k[:], theta_k[:], 0.15915494309189535, None, ALU.mult))
            link(nc.vector.tensor_tensor(th_f[:].rearrange("p (c m) -> p c m", m=M),
                                         ident[:].unsqueeze(2).broadcast_to([P, P, M]),
                                         theta_k[:].unsqueeze(1).broadcast_to([P, P, M]), ALU.mult))
            link(nc.vector.tensor_copy(thblk[:, 0], th_f[:]))
            nc.vector.tensor_tensor(thblk[:, 1], th_f[:], thblk[:, 0].bitcast(F32), ALU.subtract)
            link(nc.vector.tensor_tensor(coef[:], norm[:], diag[:], ALU.mult))
            wv = w_in[:, KH + K:TOTAL].rearrange("p (q h m r) -> p q h m r", q=KQ, h=H, m=M)
            for q in range(KQ):
                qr, qi = wv[:, q, :, :, 0], wv[:, q, :, :, 1]
                ca = coef[:, 0, :].unsqueeze(2).broadcast_to([P, H, M])
                cb = coef[:, 1, :].unsqueeze(2).broadcast_to([P, H, M])
                v = [t[:, i, q, :].rearrange("p (h m) -> p h m", m=M) for t in (wq_f, wq_t) for i in range(2)]
                nc.vector.tensor_tensor(v[0], qi, ca, ALU.mult)
                nc.vector.tensor_tensor(v[2], qr, cb, ALU.mult)
                nc.vector.tensor_tensor(v[1], qr, ca, ALU.mult)
                last = nc.vector.tensor_tensor(v[3], qi, cb, ALU.mult)
            link(last)
            link(nc.vector.scalar_tensor_tensor(wq_f[:, 0], wq_f[:, 0], -1.0, wq_t[:, 0], ALU.mult, ALU.subtract))
            link(nc.vector.tensor_tensor(wq_f[:, 1], wq_f[:, 1], wq_t[:, 1], ALU.subtract))
            wf = wq_f[:].rearrange("p i q m -> p (i q m)")
            link(nc.vector.tensor_copy(wq[:, 0], wf))
            nc.vector.tensor_tensor(wq[:, 1], wf, wq[:, 0].bitcast(F32), ALU.subtract)
            dve.wait_ge(z_kept, 2)
            link(nc.vector.tensor_scalar(lp[:], zs[:, 0:L], taps_s[:, 0:1], None, ALU.mult))
            for t in range(1, TAPS):
                link(nc.vector.scalar_tensor_tensor(lp[:], zs[:, t:t + L], taps_s[:, t:t + 1], lp[:],
                                                    ALU.mult, ALU.add))
            link(nc.vector.tensor_scalar(lp[:], lp[:], score[:], 20.0, ALU.mult, ALU.min))
            link(nc.vector.tensor_scalar(lp[:], lp[:], -20.0, None, ALU.max))
            dve.wait_ge(tabs_in, 48)
            nc.vector.scalar_tensor_tensor(lp[:], dist[:], sp[:, 7:8], lp[:], ALU.mult, ALU.add
                                           ).then_inc(lp_ready, 1)
            dve.wait_ge(p_turned, 1)
            nc.vector.tensor_copy(p_tok[:].rearrange("p j b k -> p (j b k)"), pp[:]).then_inc(p_kept, 1)
            dve.wait_ge(sums, 1)
            link(nc.vector.tensor_copy(tot[:].rearrange("p j c -> p (j c)"), pt[:]))
            for j in range(1, TPB):
                link(nc.vector.tensor_tensor(tot[:, j], tot[:, j], tot[:, j - 1], ALU.add))
            nc.vector.tensor_copy(den[:, 0], pp[:, 0:B * K])
            link(nc.vector.tensor_tensor(den[:, 1:], pp[:].rearrange("p (j c) -> p j c", j=TPB)[:, 1:],
                                         tot[:, 0:TPB - 1], ALU.add))
            dv = den[:].rearrange("p j c -> p (j c)")
            link(nc.vector.tensor_scalar(dv, dv, 1e-4, None, ALU.max))
            nc.vector.reciprocal(inv_den[:].rearrange("p j b k -> p (j b k)"), dv)


def memory(nc, xT, y_all, p_tok, inv_den, tri, wconv, wq, thblk, half_pi):
    with ExitStack() as c:
        def sb(name, shape, dt=F32):
            return c.enter_context(nc.sbuf_tensor("memory_" + name, shape, dt))

        def ps(name, shape):
            return c.enter_context(nc.psum_tensor("memory_" + name, shape, F32))

        def sem(name):
            return c.enter_context(nc.semaphore("memory_" + name))

        x_st = sb("x_st", [P, 2, 2, P], F32R)
        k_st = sb("k_st", [P, 2, 2, P], F32R)
        rounded = sb("rounded", [P, 2, NF])
        frac = sb("frac", [P, 2, NF])
        afrac = sb("afrac", [P, 2, NF])
        feat = sb("feat", [P, 2, 2, NF])
        wfeat = sb("wfeat", [P, 2, 2, NF])
        query = sb("query", [P, B, 2 * KQ * HM])
        prod = sb("prod", [P, 2, NF])
        y_raw = sb("y_raw", [P, KH])
        last_rows = sb("last_rows", [P, B, 2 * NF])
        ph = ps("ph", [P, NF])
        nsum = ps("nsum", [P, 2 * NF])
        pk = ps("pk", [P, P])
        pq = ps("pq", [P, 2 * KQ * HM])

        x_ready = sem("x_ready")
        k_done = sem("k_done")
        k_high = sem("k_high")
        k_low = sem("k_low")
        q_done = sem("q_done")
        q_kept = sem("q_kept")
        ph_done = sem("ph_done")
        rnd_done = sem("rnd_done")
        frac_done = sem("frac_done")
        abs_done = sem("abs_done")
        feat_done = sem("feat_done")
        wfeat_done = sem("wfeat_done")
        carried = [sem(f"carried{b}") for b in range(B)]
        carry_due = sem("carry_due")
        sum_done = sem("sum_done")
        prod_done = sem("prod_done")
        rows_kept = sem("rows_kept")
        red_done = sem("red_done")
        y_done = sem("y_done")
        block = c.enter_context(nc.Block())

        def steps(eng, front, body):
            front()
            body(0, True, False)
            with eng.Fori(1, TPB - 1) as step:
                body(step, False, False)
            body(TPB - 1, False, True)

        def ahead(step, b, n):
            return (step, b + n) if b + n < B else (step + 1, b + n - B)

        @block.tensor
        def _(pe):
            def values(step, b, lead=False):
                i, s = B * step + b, b % 2
                if not lead or b > 0:
                    pe.wait_ge(k_low, i)
                n = 0
                for t in range(TAPS):
                    for a, w in ((0, 0), (1, 0), (0, 1)):
                        last = nc.tensor.matmul(pk[:], wconv[:, w, t, :],
                                                xT[:, a, b, bass.ds(step * P + t, P)],
                                                start=(n == 0), stop=(n == 3 * TAPS - 1))
                        n += 1
                last.then_inc(k_done, 1)

            def phases(step, b, lead=False):
                i, s = B * step + b, b % 2
                pe.wait_ge(x_ready, i + 1)
                if not lead or b > 0:
                    pe.wait_ge(q_kept, i)
                for n, (a, w) in enumerate(((0, 0), (1, 0), (0, 1))):
                    last = nc.tensor.matmul(pq[:], x_st[:, s, a, :], wq[:, w, :], start=(n == 0), stop=(n == 2))
                last.then_inc(q_done, 1)
                pe.wait_ge(k_low, i + 1)
                if not lead or b > 0:
                    pe.wait_ge(frac_done, i)
                for h in range(2):
                    for n, (a, w) in enumerate(((0, 0), (1, 0), (0, 1))):
                        last = nc.tensor.matmul(ph[:, h * 512:(h + 1) * 512], k_st[:, s, a, :],
                                                thblk[:, w, h * 512:(h + 1) * 512], start=(n == 0), stop=(n == 2))
                last.then_inc(ph_done, 1)

            def sums(step, b, first):
                i, s = B * step + b, b % 2
                pe.wait_ge(wfeat_done, i + 1)
                if not first:
                    pe.wait_ge(carried[b], 16 * step)
                for h in range(2):
                    if not (first and b == 0):
                        pe.wait_ge(prod_done, 2 * i - 1 + h)
                        pe.wait_ge(rows_kept, 2 * i - 1 + h)
                    for q in range(2):
                        o = h * NF + q * 512
                        last = nc.tensor.matmul(nsum[:, o:o + 512], tri[:],
                                                wfeat[:, s, h, q * 512:(q + 1) * 512], start=True, stop=True)
                    last.then_inc(sum_done, 1)

            def front():
                for b in range(3):
                    values(0, b, True)
                    if b < 2:
                        phases(0, b, True)

            def body(step, first, last):
                for b in range(B):
                    if not (last and b + 2 >= B):
                        phases(*ahead(step, b, 2))
                    if not (last and b + 3 >= B):
                        values(*ahead(step, b, 3))
                    sums(step, b, first)
            steps(pe, front, body)

        @block.scalar
        def _(act):
            def k_part(step, b, lead=False):
                i, s = B * step + b, b % 2
                act.wait_ge(k_done, i + 1)
                if not lead or b >= 2:
                    act.wait_ge(ph_done, i - 1)
                nc.scalar.copy(k_st[:, s, 0, :], pk[:]).then_inc(k_high, 1)

            def rounding(step, b, lead=False):
                i, s = B * step + b, b % 2
                act.wait_ge(ph_done, i + 1)
                if not lead:
                    act.wait_ge(frac_done, i - 1)
                nc.scalar.activation(rounded[:, s, :], ph[:], ACT.Copy, bias=ROUND).then_inc(rnd_done, 1)
                act.wait_ge(q_done, i + 1)
                if not (lead or isinstance(step, int) and step == 0):
                    act.wait_ge(prod_done, 2 * i - 6)
                nc.scalar.copy(query[:, b, :], pq[:]).then_inc(q_kept, 1)

            def sine(step, b, lead=False):
                i, s = B * step + b, b % 2
                act.wait_ge(frac_done, i + 1)
                nc.scalar.activation(afrac[:, s, :], frac[:, s, :], ACT.Abs).then_inc(abs_done, 1)
                if not lead:
                    act.wait_ge(wfeat_done, i - 1)
                nc.scalar.activation(feat[:, s, 0, :], frac[:, s, :], ACT.Sin, scale=TURN)

            def cosine(step, b):
                i, s = B * step + b, b % 2
                act.wait_ge(abs_done, i + 1)
                nc.scalar.activation(feat[:, s, 1, :], afrac[:, s, :], ACT.Sin, scale=-TURN,
                                     bias=half_pi[:]).then_inc(feat_done, 1)

            def rows(step, b, h, first):
                i = B * step + b
                if not first:
                    act.wait_ge(carried[b], 16 * step)
                act.wait_ge(prod_done, 2 * i + 1 + h)
                nc.scalar.copy(last_rows[96:P, b, h * NF:(h + 1) * NF], nsum[96:P, h * NF:(h + 1) * NF]
                               ).then_inc(rows_kept, 1)

            def front():
                for b in range(3):
                    k_part(0, b, True)
                    if b < 2:
                        rounding(0, b, True)
                        sine(0, b, True)
                        cosine(0, b)

            def body(step, first, last):
                for b in range(B):
                    if not (last and b + 2 >= B):
                        rounding(*ahead(step, b, 2))
                    if not (last and b + 3 >= B):
                        k_part(*ahead(step, b, 3))
                    if not (last and b + 2 >= B):
                        sine(*ahead(step, b, 2))
                    rows(step, b, 0, first)
                    if not (last and b + 2 >= B):
                        cosine(*ahead(step, b, 2))
                    rows(step, b, 1, first)
            steps(act, front, body)

        @block.vector
        def _(dve):
            def x_part(step, b, lead=False):
                i, s = B * step + b, b % 2
                if not lead or b >= 2:
                    dve.wait_ge(q_done, i - 1)
                nc.vector.tensor_copy(x_st[:, s], xT[:, :, b, bass.ds(step * P + HALO, P)].bitcast(F32)
                                      ).then_inc(x_ready, 1)

            def k_part(step, b, lead=False):
                i, s = B * step + b, b % 2
                dve.wait_ge(k_high, i + 1)
                nc.vector.tensor_tensor(k_st[:, s, 1, :], pk[:], k_st[:, s, 0, :].bitcast(F32), ALU.subtract
                                        ).then_inc(k_low, 1)

            def fraction(step, b, lead=False):
                i, s = B * step + b, b % 2
                dve.wait_ge(rnd_done, i + 1)
                if not lead:
                    dve.wait_ge(feat_done, i - 1)
                nc.vector.scalar_tensor_tensor(frac[:, s, :], rounded[:, s, :], -ROUND, ph[:],
                                               ALU.add, ALU.subtract).then_inc(frac_done, 1)

            def read_out(step, b, first):
                i, s = B * step + b, b % 2
                dve.wait_ge(q_kept, i + 1)
                if not (first and b == 0):
                    dve.wait_ge(red_done, i)
                for h in range(2):
                    dve.wait_ge(sum_done, 2 * i + 1 + h)
                    nv = nsum[:, h * NF:(h + 1) * NF].rearrange("p (q r c) -> p q r c", q=KQ, r=REP)
                    qv = query[:, b, h * KQ * HM:(h + 1) * KQ * HM].rearrange("p (q c) -> p q c", q=KQ)
                    nc.vector.tensor_tensor(prod[:, h, :].rearrange("p (q r c) -> p q r c", q=KQ, r=REP),
                                            nv, qv.unsqueeze(2).broadcast_to([P, KQ, REP, HM]), ALU.mult
                                            ).then_inc(prod_done, 1)
                dve.wait_ge(prod_done, 2 * i + 2)
                if not (first and b == 0):
                    dve.wait_ge(y_done, i)
                nc.vector.tensor_reduce(y_raw[:], prod[:].rearrange("p h (c m) -> p c h m", m=M), AX.XY, ALU.add
                                        ).then_inc(red_done, 1)
                dve.wait_ge(red_done, i + 1)
                nc.vector.tensor_tensor(
                    y_all[:, bass.ds(step + b * TPB, 1), :].rearrange("p o (k h) -> p (o k) h", h=H),
                    y_raw[:].rearrange("p (k h) -> p k h", h=H),
                    inv_den[:, bass.ds(step, 1), b, :].rearrange("p o k -> p (o k)").unsqueeze(2)
                    .broadcast_to([P, K, H]), ALU.mult).then_inc(y_done, 1)

            def front():
                for b in range(3):
                    x_part(0, b, True)
                    k_part(0, b, True)
                    if b < 2:
                        fraction(0, b, True)

            def body(step, first, last):
                for b in range(B):
                    if not (last and b + 2 >= B):
                        fraction(*ahead(step, b, 2))
                    if not (last and b + 3 >= B):
                        x_part(*ahead(step, b, 3))
                        k_part(*ahead(step, b, 3))
                    read_out(step, b, first)
            steps(dve, front, body)

        @block.gpsimd
        def _(pool):
            def weigh(step, b, lead, first):
                i, s = B * step + b, b % 2
                pool.wait_ge(feat_done, i + 1)
                if not lead:
                    pool.wait_ge(sum_done, 2 * i - 2)
                pv = p_tok[:, bass.ds(step, 1), b, :].rearrange("p o k -> p (o k)").unsqueeze(2)
                for h in range(2):
                    ins = nc.gpsimd.tensor_tensor(wfeat[:, s, h].rearrange("p (k c) -> p k c", k=K),
                                                  feat[:, s, h].rearrange("p (k c) -> p k c", k=K),
                                                  pv.broadcast_to([P, K, HM]), ALU.mult)
                ins.then_inc(wfeat_done, 1)
                if not first:
                    pool.wait_ge(wfeat_done, i + 1)
                    pool.wait_ge(rows_kept, 2 * (i - B) + 2)
                    nc.gpsimd.sem_inc(carry_due, 1)
                    pool.dma_start(wfeat[0:1, s].rearrange("p h c -> p (h c)"),
                                   last_rows[P - 1:P, b, :], accum_op=ALU.add).then_inc(carried[b], 16)

            for b in range(B):
                weigh(0, b, b < 2, True)
            with pool.Fori(1, TPB) as step:
                for b in range(B):
                    weigh(step, b, False, False)


def mixture(nc, x_tok, y_all, ident, tri, rows, w_out, routerT, w_fc, w_proj, shared_fc, shared_proj,
            x1_dram, pick_dram, out):
    with ExitStack() as ctx:
        w1 = ctx.enter_context(nc.sbuf_tensor("w1", [P, 2, NE, FF], F32R))
        w2 = ctx.enter_context(nc.sbuf_tensor("w2", [P, NE, FC, D], F32))
        logits = ctx.enter_context(nc.sbuf_tensor("logits", [P, NT, E], F32))
        weight = ctx.enter_context(nc.sbuf_tensor("weight", [P, 2, NT], F32))
        take = ctx.enter_context(nc.sbuf_tensor("take", [P, SLOTS + ROWS // P], U32))
        put = ctx.enter_context(nc.sbuf_tensor("put", [P, SLOTS], U32))
        expert = ctx.enter_context(nc.sbuf_tensor("expert", [1, TILES], I32))
        project(nc, x_tok, y_all, ident, w_out, routerT, w_fc, w_proj, shared_fc, shared_proj, w1, w2,
                logits, x1_dram)
        route(nc, logits, tri, rows, weight, take, put, expert)
        routed(nc, ident, w1, w2, take, put, expert, x1_dram, pick_dram)
        finish(nc, y_all, weight, pick_dram, out)


def project(nc, x_tok, y_all, ident, w_out, routerT, w_fc, w_proj, shared_fc, shared_proj, w1, w2,
            logits, x1_dram):
    with ExitStack() as c:
        def sb(name, shape, dt=F32):
            return c.enter_context(nc.sbuf_tensor("project_" + name, shape, dt))

        def ps(name, shape):
            return c.enter_context(nc.psum_tensor("project_" + name, shape, F32))

        def sem(name):
            return c.enter_context(nc.semaphore("project_" + name))

        w_nat = sb("w_nat", [P, 2, 2, FC, D])
        sy = sb("sy", [P, GT * KH])
        syT = sb("syT", [P, GT, P])
        res = sb("res", [P, GT, D])
        stats = sb("stats", [P, GT, 6])
        mv = sb("mv", [P, GT, 2])
        std = sb("std", [P, GT])
        rstd = sb("rstd", [P, GT])
        eps = sb("eps", [P, 1])
        xn = sb("xn", [P, 2, GT, D])
        xnT = sb("xnT", [P, GT, P])
        xs = sb("xs", [P, 2, 2, GT * P], F32R)
        rel = sb("rel", [P, 2, GT * P])
        hid = sb("hid", [P, FC, GT * P])
        pw = [ps(f"pw{m}", [P, 512]) for m in range(2)]
        pa = ps("pa", [P, 512])
        pb = ps("pb", [P, 512])
        pl = ps("pl", [P, GT * E])
        phid = [ps(f"phid{i}", [P, GT * P]) for i in range(2)]
        pout = ps("pout", [P, GT * D])

        w_in = [sem(f"w_in_slot{i}") for i in range(2)]
        turned = sem("w_turned")
        w_kept = sem("w_kept")
        w_low = sem("w_low")
        silu_done = sem("silu_done")
        sy_ready = sem("sy_ready")
        yT_done = sem("yT_done")
        yT_kept = sem("yT_kept")
        proj_done = sem("proj_done")
        res_done = sem("res_done")
        stats_due = sem("stats_due")
        var_done = sem("var_done")
        std_done = sem("std_done")
        rstd_done = sem("rstd_done")
        xn_done = sem("xn_done")
        xnT_done = sem("xnT_done")
        xnT_kept = sem("xnT_kept")
        xs_high = sem("xs_high")
        xs_done = sem("xs_done")
        log_done = sem("log_done")
        log_kept = sem("log_kept")
        up_done = sem("up_done")
        rel_done = sem("rel_done")
        hid_done = sem("hid_done")
        down_done = sem("down_done")
        acc_done = sem("acc_done")
        stored = [sem(f"stored{i}") for i in range(2)]
        block = c.enter_context(nc.Block())

        def groups(eng, front, body):
            front()
            body(0, 0, False)
            body(1, 1, False)
            with eng.Fori(2, NG - 3, 2) as g:
                body(g, 0, False)
                body(g + 1, 1, False)
            body(NG - 2, 0, False)
            body(NG - 1, 1, True)


        @block.sync
        def _(sp):
            def load(n, s, fc, pj):
                sp.dma_start(w_nat[:, s, 0], fc.rearrange("(c p) d -> p c d", p=P)).then_inc(w_in[s], 16)
                sp.dma_start(w_nat[:, s, 1].rearrange("p c d -> p (c d)"), pj).then_inc(w_in[s], 16)

            def front():
                load(0, 1, shared_fc, shared_proj)
                load(1, 0, w_fc[0], w_proj[0])

            def body(g, s, last):
                if not last:
                    sp.wait_ge(turned, 2 * g + 2)
                    load(g + 2, 1 - s, w_fc[bass.ds(g + 1, 1), :, :].rearrange("o f d -> (o f) d"),
                         w_proj[bass.ds(g + 1, 1), :, :].rearrange("o d f -> (o d) f"))
                sp.wait_ge(xn_done, g + 1)
                sp.dma_start(x1_dram[bass.ds(g * (GT * P), GT * P), :].rearrange("(t p) d -> p t d", p=P), xn[:, s]
                             ).then_inc(stored[s], 16)
            groups(sp, front, body)
            for i in range(2):
                sp.wait_ge(stored[i], 16 * NG // 2)

        @block.tensor
        def _(pe):
            def turn(n, s, arrived, first=False):
                pe.wait_ge(w_in[s], arrived)
                for m in range(2):
                    if not first:
                        if m == 0:
                            pe.wait_ge(w_low, n)
                        else:
                            pe.wait_ge(w_kept, 2 * n)
                    for q in range(FC):
                        last = nc.tensor.transpose(pw[m][:, q * P:(q + 1) * P], w_nat[:, s, m, q, :], ident[:])
                    last.then_inc(turned, 1)

            def turn_y(g):
                pe.wait_ge(sy_ready, g + 1)
                for t in range(GT):
                    last = nc.tensor.transpose(pa[:, t * P:(t + 1) * P], sy[:, t * KH:(t + 1) * KH], ident[:])
                last.then_inc(yT_done, 1)

            def proj(g):
                pe.wait_ge(yT_kept, g + 1)
                for t in range(GT):
                    last = nc.tensor.matmul(pa[:, t * D:(t + 1) * D], syT[:, t, :], w_out[:], start=True, stop=True)
                last.then_inc(proj_done, 1)

            def norm_turned(g, s):
                pe.wait_ge(xn_done, g + 1)
                for t in range(GT):
                    last = nc.tensor.transpose(pb[:, t * P:(t + 1) * P], xn[:, s, t, :], ident[:])
                last.then_inc(xnT_done, 1)
                pe.wait_ge(xnT_kept, g + 1)
                for t in range(GT):
                    last = nc.tensor.matmul(pl[:, t * E:(t + 1) * E], xnT[:, t, :], routerT[:], start=True, stop=True)
                last.then_inc(log_done, 1)

            def up(g, s, q, first):
                if q == 0:
                    pe.wait_ge(xs_done, g + 1)
                if not (first and q < 2):
                    pe.wait_ge(rel_done, g * FC + q - 1)
                for m, (a, w) in enumerate(((0, 0), (1, 0), (0, 1))):
                    last = nc.tensor.matmul(phid[q % 2][:], w1[:, w, E, q * P:(q + 1) * P], xs[:, s, a, :],
                                            start=(m == 0), stop=(m == 2))
                last.then_inc(up_done, 1)

            def down(g, first):
                pe.wait_ge(hid_done, g * FC + FC)
                if not first:
                    pe.wait_ge(acc_done, g)
                for t in range(GT):
                    for q in range(FC):
                        last = nc.tensor.matmul(pout[:, t * D:(t + 1) * D], hid[:, q, t * P:(t + 1) * P],
                                                w2[:, E, q, :], start=(q == 0), stop=(q == FC - 1))
                last.then_inc(down_done, 1)

            def front():
                turn(0, 1, 32, True)
                turn_y(0)
                proj(0)
                norm_turned(0, 0)

            def body(g, s, last):
                if not last:
                    turn_y(g + 1)
                for q in range(FC):
                    up(g, s, q, isinstance(g, int) and g == 0)
                if not last:
                    proj(g + 1)
                turn(g + 1, s, 16 * (g - s) + 32 + 32 * s)
                down(g, isinstance(g, int) and g == 0)
                if not last:
                    norm_turned(g + 1, 1 - s)
            groups(pe, front, body)

        @block.scalar
        def _(act):
            def keep(n, e):
                act.wait_ge(turned, 2 * n + 1)
                nc.scalar.copy(w1[:, 0, bass.ds(e, 1), :].rearrange("p o f -> p (o f)"), pw[0][:]).then_inc(w_kept, 1)
                act.wait_ge(turned, 2 * n + 2)
                nc.scalar.copy(w2[:, bass.ds(e, 1)].rearrange("p o c d -> p (o c d)"), pw[1][:]).then_inc(w_kept, 1)

            def keep_y(g):
                act.wait_ge(yT_done, g + 1)
                nc.scalar.copy(syT[:].rearrange("p t c -> p (t c)"), pa[:]).then_inc(yT_kept, 1)

            def root(g):
                act.wait_ge(var_done, g + 1)
                nc.scalar.activation(std[:], mv[:, :, 1], ACT.Sqrt, bias=eps[:]).then_inc(std_done, 1)

            def keep_x(g, first):
                act.wait_ge(xnT_done, g + 1)
                if not first:
                    act.wait_ge(log_done, g)
                    act.wait_ge(xs_done, g)
                nc.scalar.copy(xnT[:].rearrange("p t c -> p (t c)"), pb[:]).then_inc(xnT_kept, 1)

            def relu(g, q, first):
                act.wait_ge(up_done, g * FC + q + 1)
                if not (first and q < 2):
                    act.wait_ge(hid_done, g * FC + q - 1)
                nc.scalar.activation(rel[:, q % 2, :], phid[q % 2][:], ACT.Relu).then_inc(rel_done, 1)

            def front():
                n = 8
                for h in range(n):
                    v = y_all[:, h * NT // n:(h + 1) * NT // n, :]
                    nc.scalar.activation(v, v, ACT.Silu).then_inc(silu_done, 1)
                keep(0, E)
                keep_y(0)
                root(0)
                keep_x(0, True)

            def body(g, s, last):
                if not last:
                    keep_y(g + 1)
                for q in range(FC):
                    relu(g, q, isinstance(g, int) and g == 0)
                if not last:
                    root(g + 1)
                keep(g + 1, g)
                if not last:
                    keep_x(g + 1, False)
            groups(act, front, body)

        @block.gpsimd
        def _(pool):
            def body(g, s, last):
                for q in range(FC):
                    pool.wait_ge(rel_done, g * FC + q + 1)
                    if q == 0 and not (isinstance(g, int) and g == 0):
                        pool.wait_ge(down_done, g)
                    nc.gpsimd.tensor_tensor(hid[:, q, :], rel[:, q % 2, :], rel[:, q % 2, :], ALU.mult
                                            ).then_inc(hid_done, 1)
            groups(pool, lambda: None, body)

        @block.vector
        def _(dve):
            nc.vector.memset(eps[:], EPS)

            def low(n, e):
                dve.wait_ge(w_kept, 2 * n + 1)
                nc.vector.tensor_tensor(w1[:, 1, bass.ds(e, 1), :].rearrange("p o f -> p (o f)"), pw[0][:],
                                        w1[:, 0, bass.ds(e, 1), :].rearrange("p o f -> p (o f)").bitcast(F32),
                                        ALU.subtract).then_inc(w_low, 1)

            def take_y(g, first):
                if not first:
                    dve.wait_ge(yT_done, g)
                    dve.wait_ge(res_done, g)
                nc.vector.tensor_copy(sy[:], y_all[:, bass.ds(g * GT, GT), :].rearrange("p t c -> p (t c)")
                                      ).then_inc(sy_ready, 1)

            def normalise(g, s, first):
                dve.wait_ge(proj_done, g + 1)
                nc.vector.tensor_tensor(res[:].rearrange("p t c -> p (t c)"), pa[:],
                                        x_tok[:, bass.ds(g * GT, GT), :].rearrange("p t c -> p (t c)"), ALU.add
                                        ).then_inc(res_done, 1)
                dve.wait_ge(res_done, g + 1)
                for t in range(GT):
                    last = nc.vector.bn_stats(stats[:, t, :], res[:, t, :])
                last.then_inc(stats_due, 1)
                dve.wait_ge(stats_due, 2 * g + 1)
                nc.vector.sem_inc(stats_due, 1)
                for t in range(GT):
                    last = nc.vector.bn_aggr(mv[:, t, :], stats[:, t, :])
                last.then_inc(var_done, 1)
                dve.wait_ge(std_done, g + 1)
                nc.vector.reciprocal(rstd[:], std[:]).then_inc(rstd_done, 1)
                dve.wait_ge(rstd_done, g + 1)
                if not first:
                    dve.wait_ge(stored[s], 8 * (g - s))
                for t in range(GT):
                    last = nc.vector.tensor_scalar(xn[:, s, t, :], res[:, t, :], mv[:, t, 0:1], rstd[:, t:t + 1],
                                                   ALU.subtract, ALU.mult)
                last.then_inc(xn_done, 1)

            def split(g, s):
                dve.wait_ge(xnT_kept, g + 1)
                xv = xnT[:].rearrange("p t c -> p (t c)")
                nc.vector.tensor_copy(xs[:, s, 0, :], xv).then_inc(xs_high, 1)
                dve.wait_ge(xs_high, g + 1)
                nc.vector.tensor_tensor(xs[:, s, 1, :], xv, xs[:, s, 0, :].bitcast(F32), ALU.subtract
                                        ).then_inc(xs_done, 1)
                dve.wait_ge(log_done, g + 1)
                nc.vector.tensor_copy(logits[:, bass.ds(g * GT, GT), :].rearrange("p t e -> p (t e)"), pl[:]
                                      ).then_inc(log_kept, 1)

            def front():
                dve.wait_ge(silu_done, 8)
                take_y(0, True)
                low(0, E)
                normalise(0, 0, True)
                split(0, 0)

            def body(g, s, last):
                if not last:
                    take_y(g + 1, False)
                if not last:
                    normalise(g + 1, 1 - s, isinstance(g, int) and g == 0)
                low(g + 1, g)
                dve.wait_ge(down_done, g + 1)
                nc.vector.tensor_tensor(y_all[:, bass.ds(g * GT, GT), :].rearrange("p t c -> p (t c)"), pout[:],
                                        xn[:, s].rearrange("p t c -> p (t c)"), ALU.add).then_inc(acc_done, 1)
                if not last:
                    split(g + 1, 1 - s)
            groups(dve, front, body)


def route(nc, logits, tri, rows, weight, take, put, expert):
    with ExitStack() as c:
        def sb(name, shape, dt=F32):
            return c.enter_context(nc.sbuf_tensor("route_" + name, shape, dt))

        def ps(name, shape):
            return c.enter_context(nc.psum_tensor("route_" + name, shape, F32))

        def sem(name):
            return c.enter_context(nc.semaphore("route_" + name))

        prob = sb("prob", [P, NT, E])
        tmp = sb("tmp", [P, NT, E])
        order = sb("order", [P, NT, E])
        oh = sb("oh", [P, 2, NT, E])
        sel = sb("sel", [P, NT, E])
        mx = sb("mx", [P, 6, NT])
        ones = sb("ones_r", [P, P])
        keep = sb("keep", [P, E, NT])
        total = sb("total", [P, E, NT])
        upto = sb("upto", [P, E, NT])
        base = sb("base", [P, NT, E])
        fills = sb("fills", [P, E, 16])
        tiles = sb("tiles", [P, 4, E])
        texp = sb("texp", [P, TILES, E])
        tex = sb("tex", [P, TILES])
        pos = sb("pos", [P, 2, NT])
        hi = sb("hi", [P, 2, NT])
        lo = sb("lo", [P, 2, NT])
        val = sb("val", [P, 2, NT])
        oneA = sb("oneA", [P, 4, P], F32R)
        oneB = sb("oneB", [P, 4, SLOTS], F32R)
        sl = sb("sl", [P, 3, SLOTS])
        pr = ps("pr", [P, NT * E])
        pt = ps("pt", [P, NT * E])
        plist = ps("plist", [P, SLOTS])
        chain = sem("chain")
        shifted = sem("shifted")
        exp_done = sem("exp_done")
        sel_done = sem("sel_done")
        ranked = sem("ranked")
        hot = sem("hot")
        listed = sem("listed")
        block = c.enter_context(nc.Block())
        iota = rows[:, 0:P]
        token = rows[:, P:P + NT]
        NP = 2 * NT

        @block.scalar
        def _(act):
            act.wait_ge(shifted, 1)
            nc.scalar.activation(prob[:], tmp[:], ACT.Exp).then_inc(exp_done, 1)

        @block.tensor
        def _(pe):
            pe.wait_ge(sel_done, 1)
            sv = sel[:].rearrange("p i e -> p (i e)")
            nc.tensor.matmul(pr[:], tri[:], sv, start=True, stop=True)
            nc.tensor.matmul(pt[:], ones[:], sv, start=True, stop=True).then_inc(ranked, 1)

            def body(n, first, last):
                for u in range(4):
                    pe.wait_ge(hot, n * 4 + u + 1)
                    nc.tensor.matmul(plist[:], oneA[:, u, :], oneB[:, u, :], start=(first and u == 0),
                                     stop=(last and u == 3)).then_inc(listed, 1)
            body(0, True, False)
            with pe.Fori(1, NP // 4 - 1) as n:
                body(n, False, False)
            body(NP // 4 - 1, False, True)

        @block.vector
        def _(dve):
            cnt = [0]

            def link(ins):
                cnt[0] += 1
                ins.then_inc(chain, 1)
                dve.wait_ge(chain, cnt[0])

            def over_e(v):
                return v.unsqueeze(2).broadcast_to([P, NT, E])

            for e in range(E):
                nc.vector.memset(order[:, :, e], float(E - e))
            nc.vector.memset(ones[:], 1.0)
            nc.vector.memset(take[:, SLOTS:], 0)
            nc.vector.memset(keep[:, :, 1:], 1.0)
            nc.vector.memset(keep[:, :, 0:1], 0.0)
            link(nc.vector.tensor_reduce(mx[:, 0], logits[:], AX.X, ALU.max))
            nc.vector.tensor_tensor(tmp[:], logits[:], over_e(mx[:, 0]), ALU.subtract).then_inc(shifted, 1)
            dve.wait_ge(exp_done, 1)
            link(nc.vector.tensor_reduce(mx[:, 1], prob[:], AX.X, ALU.add))
            link(nc.vector.reciprocal(mx[:, 2], mx[:, 1]))
            link(nc.vector.tensor_tensor(prob[:], prob[:], over_e(mx[:, 2]), ALU.mult))
            for r in range(2):
                link(nc.vector.tensor_reduce(mx[:, 3 + r], prob[:], AX.X, ALU.max))
                link(nc.vector.tensor_tensor(tmp[:], prob[:], over_e(mx[:, 3 + r]), ALU.is_equal))
                link(nc.vector.tensor_tensor(tmp[:], tmp[:], order[:], ALU.mult))
                link(nc.vector.tensor_reduce(mx[:, 5], tmp[:], AX.X, ALU.max))
                link(nc.vector.tensor_tensor(oh[:, r], tmp[:], over_e(mx[:, 5]), ALU.is_equal))
                if r == 0:
                    link(nc.vector.scalar_tensor_tensor(prob[:], oh[:, 0], -2.0, prob[:], ALU.mult, ALU.add))
            nc.vector.tensor_tensor(sel[:], oh[:, 0], oh[:, 1], ALU.add).then_inc(sel_done, 1)
            link(nc.vector.tensor_tensor(mx[:, 0], mx[:, 3], mx[:, 4], ALU.add))
            link(nc.vector.tensor_scalar(mx[:, 0], mx[:, 0], 1e-9, None, ALU.max))
            link(nc.vector.reciprocal(mx[:, 1], mx[:, 0]))
            for r in range(2):
                nc.vector.tensor_tensor(weight[:, r], mx[:, 3 + r], mx[:, 1], ALU.mult)
            dve.wait_ge(ranked, 1)
            link(nc.vector.tensor_copy(total[:], pt[:].rearrange("p (i e) -> p e i", e=E)))
            fl = "p e i -> p (e i)"
            link(nc.vector.tensor_tensor_scan(upto[:].rearrange(fl), keep[:].rearrange(fl), total[:].rearrange(fl),
                                              0.0, ALU.mult, ALU.add))
            for m in range(16):
                last = nc.vector.tensor_scalar(fills[:, :, m], upto[:, :, NT - 1], float(ROWS * m), None, ALU.is_gt)
            link(last)
            link(nc.vector.tensor_reduce(tiles[:, 0], fills[:], AX.X, ALU.add))
            link(nc.vector.memset(tiles[:, 1], 1.0))
            link(nc.vector.tensor_tensor_scan(tiles[:, 2], tiles[:, 1], tiles[:, 0], 0.0, ALU.mult, ALU.add))
            link(nc.vector.tensor_tensor(tiles[:, 3], tiles[:, 2], tiles[:, 0], ALU.subtract))
            link(nc.vector.tensor_tensor(texp[:], iota[:, 0:TILES].unsqueeze(2).broadcast_to([P, TILES, E]),
                                         tiles[:, 2].unsqueeze(1).broadcast_to([P, TILES, E]), ALU.is_ge))
            link(nc.vector.tensor_reduce(tex[:], texp[:], AX.X, ALU.add))
            nc.vector.tensor_scalar(expert[:], tex[0:1, :], float(E - 1), None, ALU.min)
            link(nc.vector.tensor_tensor(total[:], upto[:], total[:], ALU.subtract))
            link(nc.vector.tensor_scalar(tiles[:, 3], tiles[:, 3], float(ROWS), -1.0, ALU.mult, ALU.add))
            link(nc.vector.tensor_tensor(base[:], pr[:].rearrange("p (i e) -> p i e", e=E),
                                         total[:].rearrange("p e i -> p i e"), ALU.add))
            link(nc.vector.tensor_tensor(base[:], base[:], tiles[:, 3].unsqueeze(1).broadcast_to([P, NT, E]),
                                         ALU.add))
            for r in range(2):
                link(nc.vector.tensor_tensor(tmp[:], base[:], oh[:, r], ALU.mult))
                link(nc.vector.tensor_reduce(pos[:, r], tmp[:], AX.X, ALU.add))
            link(nc.vector.tensor_scalar(hi[:], pos[:], 1.0 / P, -127.0 / 256, ALU.mult, ALU.add))
            link(nc.vector.tensor_scalar(hi[:], hi[:], ROUND, -ROUND, ALU.add, ALU.add))
            link(nc.vector.scalar_tensor_tensor(lo[:], hi[:], -float(P), pos[:], ALU.mult, ALU.add))
            nc.vector.tensor_copy(val[:, 0], token)
            link(nc.vector.tensor_scalar(val[:, 1], token, -1.0, None, ALU.mult))
            flat = [v[:].rearrange("p r i -> p (r i)") for v in (lo, hi, val)]

            def body(n, first):
                for u in range(4):
                    if not first:
                        dve.wait_ge(listed, n * 4 + u - 3)
                    c1, c2, c3 = (v[:, bass.ds(n * 4 + u, 1)] for v in flat)
                    nc.vector.tensor_scalar(oneA[:, u, :], iota, c1, None, ALU.is_equal)
                    nc.vector.tensor_scalar(oneB[:, u, :], iota[:, 0:SLOTS], c2, c3, ALU.is_equal, ALU.mult
                                            ).then_inc(hot, 1)
            body(0, True)
            with dve.Fori(1, NP // 4) as n:
                body(n, False)
            dve.wait_ge(listed, NP)
            link(nc.vector.tensor_copy(sl[:, 0], plist[:]))
            link(nc.vector.tensor_scalar(sl[:, 1], sl[:, 0], -1.0, None, ALU.mult))
            link(nc.vector.tensor_tensor(sl[:, 1], sl[:, 1], sl[:, 0], ALU.max))
            link(nc.vector.tensor_scalar(sl[:, 1], sl[:, 1], -1.0, None, ALU.add))
            nc.vector.tensor_scalar(take[:, 0:SLOTS], sl[:, 1], 0.0, None, ALU.max)
            link(nc.vector.tensor_scalar(sl[:, 2], sl[:, 0], 0.0, float(NTOK), ALU.is_lt, ALU.mult))
            link(nc.vector.tensor_tensor(sl[:, 1], sl[:, 1], sl[:, 2], ALU.add))
            link(nc.vector.tensor_scalar(sl[:, 2], sl[:, 0], 0.0, float(4 * NTOK), ALU.is_equal, ALU.mult))
            nc.vector.tensor_tensor(put[:], sl[:, 1], sl[:, 2], ALU.add)


def routed(nc, ident, w1, w2, take, put, expert, x1_dram, pick_dram):
    HALVES = ROWS // P
    U = 4
    with ExitStack() as c:
        def sb(name, shape, dt=F32):
            return c.enter_context(nc.sbuf_tensor("routed_" + name, shape, dt))

        def ps(name, shape):
            return c.enter_context(nc.psum_tensor("routed_" + name, shape, F32))

        def sem(name):
            return c.enter_context(nc.semaphore("routed_" + name))

        take_st = sb("take_st", [P, U, HALVES], U32)
        put_st = sb("put_st", [P, U, HALVES], U32)
        xg = sb("xg", [P, U, HALVES, D])
        xs = sb("xsr", [P, 2, 2, ROWS], F32R)
        w1c = sb("w1c", [P, U, 2, FF], F32R)
        w2c = sb("w2c", [P, U, FC, D])
        rel = sb("relr", [P, 2, 2 * ROWS])
        hid = sb("hidr", [P, 2, FC * ROWS])
        ob = sb("ob", [P, U, HALVES, D])
        px = [ps(f"px{i}", [P, ROWS]) for i in range(2)]
        ph = [ps(f"phr{i}", [P, FC * ROWS]) for i in range(2)]
        po = [ps(f"por{i}", [P, HALVES * D]) for i in range(2)]
        take_ready = sem("take_ready")
        put_ready = sem("put_ready")
        gather_due = sem("gather_due")
        scatter_due = sem("scatter_due")
        gathered = [sem(f"gathered{u}") for u in range(U)]
        scattered = [sem(f"scattered{u}") for u in range(U)]
        turned = sem("x_turned_r")
        x_high = sem("x_high_r")
        x_low = sem("x_low_r")
        w_ready = sem("w_ready")
        up_done = sem("up_done_r")
        rel_done = sem("rel_done_r")
        hid_done = sem("hid_done_r")
        down_done = sem("down_done_r")
        kept = sem("kept")
        block = c.enter_context(nc.Block())
        LAST = TILES // U * U if TILES % U else TILES - U

        def tiles(eng, front, body):
            front()
            for u in range(U):
                body(u, u)
            with eng.Fori(U, LAST - U + 1, U) as t:
                for u in range(U):
                    body(t + u, u)
            for u in range(TILES - LAST):
                body(LAST + u, u)

        def beyond(t, n):
            return isinstance(t, int) and t + n >= TILES

        def early(t, n):
            return isinstance(t, int) and t < n

        def passes(t, u):
            return (16 * HALVES // U) * (t - u) + 16 * HALVES

        @block.gpsimd
        def _(pool):
            def gather(t, u):
                pool.wait_ge(take_ready, t + 1)
                if not early(t, U):
                    pool.wait_ge(turned, t - U + 1)
                pool.sem_inc(gather_due, 1)
                for h in range(HALVES):
                    nc.gpsimd.indirect_dma_start(
                        out=xg[:, u, h, :], out_offset=None, in_=x1_dram,
                        in_offset=bass.IndirectOffsetOnAxis(ap=take_st[:, u, h:h + 1], axis=0)
                    ).then_inc(gathered[u], 16)

            def front():
                for t in range(U):
                    gather(t, t)

            def body(t, u):
                if not beyond(t, U):
                    gather(t + U, u)
                pool.wait_ge(kept, t + 1)
                pool.wait_ge(put_ready, t + 1)
                pool.sem_inc(scatter_due, 1)
                for h in range(HALVES):
                    nc.gpsimd.indirect_dma_start(
                        out=pick_dram, in_=ob[:, u, h, :], in_offset=None,
                        out_offset=bass.IndirectOffsetOnAxis(ap=put_st[:, u, h:h + 1], axis=0),
                        bounds_check=2 * NTOK - 1, oob_is_err=False).then_inc(scattered[u], 16)
            tiles(pool, front, body)
            for u in range(U):
                pool.wait_ge(scattered[u], 16 * HALVES * len(range(u, TILES, U)))

        @block.tensor
        def _(pe):
            def turn(t, u):
                pe.wait_ge(gathered[u], passes(t, u))
                if not early(t, 2):
                    pe.wait_ge(x_low, t - 1)
                for h in range(HALVES):
                    last = nc.tensor.transpose(px[u % 2][:, h * P:(h + 1) * P], xg[:, u, h, :], ident[:])
                last.then_inc(turned, 1)

            def up(t, u):
                s = u % 2
                pe.wait_ge(x_low, t + 1)
                pe.wait_ge(w_ready, t + 1)
                for q in range(FC):
                    if q % 2 == 0 and not early(t, 2):
                        pe.wait_ge(rel_done, 2 * (t - 2) + q // 2 + 1)
                    for m, (a, w) in enumerate(((0, 0), (1, 0), (0, 1))):
                        last = nc.tensor.matmul(ph[s][:, q * ROWS:(q + 1) * ROWS], w1c[:, u, w, q * P:(q + 1) * P],
                                                xs[:, s, a, :], start=(m == 0), stop=(m == 2))
                    if q % 2:
                        last.then_inc(up_done, 1)

            def down(t, u):
                s = u % 2
                pe.wait_ge(hid_done, 2 * t + 2)
                if not early(t, 2):
                    pe.wait_ge(kept, t - 1)
                for h in range(HALVES):
                    for q in range(FC):
                        last = nc.tensor.matmul(po[s][:, h * D:(h + 1) * D],
                                                hid[:, s, q * ROWS + h * P:q * ROWS + (h + 1) * P],
                                                w2c[:, u, q, :], start=(q == 0), stop=(q == FC - 1))
                last.then_inc(down_done, 1)

            def front():
                turn(0, 0)
                turn(1, 1)
                up(0, 0)

            def body(t, u):
                if not beyond(t, 1):
                    up(t + 1, (u + 1) % U)
                if not beyond(t, 2):
                    turn(t + 2, (u + 2) % U)
                down(t, u)
            tiles(pe, front, body)

        @block.scalar
        def _(act):
            def high(t, u):
                act.wait_ge(turned, t + 1)
                if not early(t, 2):
                    act.wait_ge(up_done, 2 * (t - 2) + 2)
                nc.scalar.copy(xs[:, u % 2, 0, :], px[u % 2][:]).then_inc(x_high, 1)

            def rectified(t, u):
                s = u % 2
                for h in range(2):
                    o = h * 2 * ROWS
                    act.wait_ge(up_done, 2 * t + h + 1)
                    if not early(t, 1):
                        act.wait_ge(hid_done, 2 * t + h - 1)
                    nc.scalar.activation(rel[:, h, :], ph[s][:, o:o + 2 * ROWS], ACT.Relu).then_inc(rel_done, 1)

            def squared(t, u):
                s = u % 2
                for h in range(2):
                    o = h * 2 * ROWS
                    act.wait_ge(rel_done, 2 * t + h + 1)
                    if h == 0 and not early(t, 2):
                        act.wait_ge(down_done, t - 1)
                    nc.scalar.activation(hid[:, s, o:o + 2 * ROWS], rel[:, h, :], ACT.Square).then_inc(hid_done, 1)

            def front():
                high(0, 0)
                high(1, 1)
                rectified(0, 0)
                squared(0, 0)

            def body(t, u):
                if not beyond(t, 1):
                    rectified(t + 1, (u + 1) % U)
                if not beyond(t, 2):
                    high(t + 2, (u + 2) % U)
                if not beyond(t, 1):
                    squared(t + 1, (u + 1) % U)
            tiles(act, front, body)

        @block.vector
        def _(dve):
            def take_part(t, u):
                if not early(t, U):
                    dve.wait_ge(gathered[u], passes(t - U, u))
                nc.vector.tensor_copy(take_st[:, u, :], take[:, bass.ds(t * HALVES, HALVES)]).then_inc(take_ready, 1)

            def put_part(t, u):
                if not early(t, U):
                    dve.wait_ge(scattered[u], passes(t - U, u))
                nc.vector.tensor_copy(put_st[:, u, :], put[:, bass.ds(t * HALVES, HALVES)]).then_inc(put_ready, 1)

            def weights(t, u):
                e = dve.value_load(expert[0:1, bass.ds(t, 1)], min_val=0, max_val=E - 1)
                if not early(t, U):
                    dve.wait_ge(down_done, t - U + 1)
                nc.vector.tensor_copy(w1c[:, u], w1[:, :, bass.ds(e, 1), :].rearrange("p a o f -> p a (o f)").bitcast(F32))
                nc.vector.tensor_copy(w2c[:, u], w2[:, bass.ds(e, 1)].rearrange("p o c d -> p (o c) d")
                                      ).then_inc(w_ready, 1)

            def low(t, u):
                dve.wait_ge(x_high, t + 1)
                nc.vector.tensor_tensor(xs[:, u % 2, 1, :], px[u % 2][:], xs[:, u % 2, 0, :].bitcast(F32), ALU.subtract
                                        ).then_inc(x_low, 1)

            def front():
                for t in range(4):
                    take_part(t, t)
                put_part(0, 0)
                for t in range(2):
                    weights(t, t)
                    low(t, t)
                weights(2, 2)

            def body(t, u):
                if not beyond(t, 4):
                    take_part(t + 4, u)
                if not beyond(t, 3):
                    weights(t + 3, (u + 3) % U)
                if not beyond(t, 2):
                    low(t + 2, (u + 2) % U)
                dve.wait_ge(down_done, t + 1)
                if not early(t, U):
                    dve.wait_ge(scattered[u], passes(t - U, u))
                nc.vector.tensor_copy(ob[:, u].rearrange("p h d -> p (h d)"), po[u % 2][:]).then_inc(kept, 1)
                if not beyond(t, 1):
                    put_part(t + 1, (u + 1) % U)
            tiles(dve, front, body)


def finish(nc, y_all, weight, pick_dram, out):
    with ExitStack() as c:
        def sb(name, shape, dt=F32):
            return c.enter_context(nc.sbuf_tensor("finish_" + name, shape, dt))

        def sem(name):
            return c.enter_context(nc.semaphore("finish_" + name))

        pick = sb("pick", [P, 2, 2, GT, D])
        one = sb("one", [P, 2, GT, D])
        res = sb("resf", [P, 2, GT, D])
        stats = sb("statsf", [P, 2, GT, 6])
        mv = sb("mvf", [P, 2, GT, 2])
        std = sb("stdf", [P, 2, GT])
        rstd = sb("rstdf", [P, 2, GT])
        eps = sb("epsf", [P, 1])
        xo = sb("xo", [P, 2, GT, D])
        picked = [sem(f"picked{i}") for i in range(2)]
        one_done = sem("one_done")
        res_done = sem("res_done_f")
        stats_done = sem("stats_done_f")
        var_done = sem("var_done_f")
        std_done = sem("std_done_f")
        rstd_done = sem("rstd_done_f")
        xo_done = sem("xo_done")
        eps_set = sem("eps_set")
        stored = [sem(f"stored_f{i}") for i in range(2)]
        block = c.enter_context(nc.Block())

        def groups(eng, front, body):
            front()
            body(0, 0)
            body(1, 1)
            with eng.Fori(2, NG - 3, 2) as g:
                body(g, 0)
                body(g + 1, 1)
            body(NG - 2, 0)
            body(NG - 1, 1)

        def early(g, n):
            return isinstance(g, int) and g < n

        @block.sync
        def _(sp):
            ov = out.rearrange("b (j p) d -> (b j) p d", p=P)

            def load(g, s):
                if not early(g, 2):
                    sp.wait_ge(res_done, g - 1)
                for r in range(2):
                    sp.dma_start(pick[:, s, r], pick_dram[bass.ds(g * (GT * P) + r * NTOK, GT * P), :]
                                 .rearrange("(t p) d -> p t d", p=P)).then_inc(picked[s], 16)

            def front():
                load(0, 0)
                load(1, 1)

            def body(g, s):
                if not (isinstance(g, int) and g >= NG - 2):
                    load(g + 2, s)
                sp.wait_ge(xo_done, g + 1)
                sp.dma_start(ov[bass.ds(g * GT, GT)].rearrange("j p d -> p j d"), xo[:, s]).then_inc(stored[s], 16)
            groups(sp, front, body)
            for i in range(2):
                sp.wait_ge(stored[i], 16 * NG // 2)

        @block.gpsimd
        def _(pool):
            def body(g, s):
                pool.wait_ge(picked[s], 16 * (g - s) + 32)
                if not early(g, 2):
                    pool.wait_ge(res_done, g - 1)
                wv = weight[:, 0, bass.ds(g * GT, GT)].unsqueeze(2).broadcast_to([P, GT, D])
                nc.gpsimd.tensor_tensor(one[:, s], pick[:, s, 0], wv, ALU.mult).then_inc(one_done, 1)
            groups(pool, lambda: None, body)

        @block.scalar
        def _(act):
            def body(g, s):
                act.wait_ge(var_done, g + 1)
                nc.scalar.activation(std[:, s], mv[:, s, :, 1], ACT.Sqrt, bias=eps[:]).then_inc(std_done, 1)

            def front():
                act.wait_ge(eps_set, 1)
            groups(act, front, body)

        @block.vector
        def _(dve):
            nc.vector.memset(eps[:], EPS).then_inc(eps_set, 1)

            def add(g, s):
                dve.wait_ge(picked[s], 16 * (g - s) + 32)
                if not early(g, 2):
                    dve.wait_ge(xo_done, g - 1)
                for t in range(GT):
                    last = nc.vector.scalar_tensor_tensor(
                        res[:, s, t, :], pick[:, s, 1, t, :], weight[:, 1, bass.ds(g * GT + t, 1)],
                        y_all[:, bass.ds(g * GT + t, 1), :].rearrange("p o d -> p (o d)"), ALU.mult, ALU.add)
                last.then_inc(stats_done, 1)
                dve.wait_ge(one_done, g + 1)
                dve.wait_ge(stats_done, 3 * g + 1)
                nc.vector.tensor_tensor(res[:, s], res[:, s], one[:, s], ALU.add).then_inc(res_done, 1)
                dve.wait_ge(res_done, g + 1)
                for t in range(GT):
                    last = nc.vector.bn_stats(stats[:, s, t, :], res[:, s, t, :])
                last.then_inc(stats_done, 1)
                dve.wait_ge(stats_done, 3 * g + 2)
                nc.vector.sem_inc(stats_done, 1)
                for t in range(GT):
                    last = nc.vector.bn_aggr(mv[:, s, t, :], stats[:, s, t, :])
                last.then_inc(var_done, 1)

            def normalise(g, s):
                dve.wait_ge(std_done, g + 1)
                nc.vector.reciprocal(rstd[:, s], std[:, s]).then_inc(rstd_done, 1)
                dve.wait_ge(rstd_done, g + 1)
                if not early(g, 2):
                    dve.wait_ge(stored[s], 8 * (g - s))
                for t in range(GT):
                    last = nc.vector.tensor_scalar(xo[:, s, t, :], res[:, s, t, :], mv[:, s, t, 0:1],
                                                   rstd[:, s, t:t + 1], ALU.subtract, ALU.mult)
                last.then_inc(xo_done, 1)

            def body(g, s):
                if not (isinstance(g, int) and g == NG - 1):
                    add(g + 1, 1 - s)
                normalise(g, s)
            groups(dve, lambda: add(0, 0), body)


INS = ["L0_attn_x", "L0_attn_W_in", "L0_attn_conv_k", "L0_attn_theta", "L0_attn_decay_slopes",
       "L0_attn_anchor_slopes", "L0_attn_score_scale", "L0_attn_W_re", "L0_attn_W_im",
       "L0_attn_norm_scale", "L0_attn_W_out", "L0_ffn_router_w", "L0_ffn_w_fc", "L0_ffn_w_proj",
       "L0_ffn_shared_fc", "L0_ffn_shared_proj"]


def kernel(**inputs):
    import numpy as np
    import concourse.bacc as bacc
    from concourse import mybir as mb
    from concourse.bass_utils import run_bass_kernel_spmd as run

    nc = bacc.Bacc("TRN2", target_bir_lowering=False, num_devices=1)
    tables = np.zeros((P, 2 * P + L + P + NT), np.float32)
    tables[:, 0:P] = np.eye(P)
    tables[:, P:2 * P] = np.triu(np.ones((P, P)))
    pos = np.arange(L)
    tables[:, 2 * P:2 * P + L] = [(L - 1 - pos) if k % K < K - 4 else pos for k in range(P)]
    tables[:, 2 * P + L:3 * P + L] = np.arange(P)
    tables[:, 3 * P + L:] = 1 + np.arange(P)[:, None] + P * np.arange(NT)
    arrays = {n: np.ascontiguousarray(inputs[n]) for n in INS}
    arrays["tables"] = tables
    args = [nc.dram_tensor(n, a.shape, mb.dt.float32, kind="ExternalInput").ap() for n, a in arrays.items()]
    out = nc.dram_tensor("out", (B, L, D), mb.dt.float32, kind="ExternalOutput").ap()
    build(nc, *args, out)
    r = run(nc, [arrays], core_ids=[0])
    return r.results[0]["out"]
```

```python
from contextlib import ExitStack

import concourse.bass as bass
from concourse import mybir

ALU = mybir.AluOpType
ACT = mybir.ActivationFunctionType
AX = mybir.AxisListType
F32 = mybir.dt.float32
F32R = mybir.dt.float32r
I32 = mybir.dt.int32
U32 = mybir.dt.uint32

P = 128
D = 128
B, L = 4, 1024
TPB = L // P
NT = B * TPB
K, H, M, KQ = 32, 4, 8, 4
REP = K // KQ
KH = K * H
HM = H * M
NF = KH * M
TAPS = 4
HALO = TAPS - 1
E, FF = 8, 512
FC = FF // P
NE = E + 1
GT = 4
NG = NT // GT
NTOK = B * L
SG = NG // 2
NINV = 1
ROWS = 256
TILES = (2 * NTOK + E * (ROWS - 1)) // ROWS
SLOTS = TILES * ROWS // P
ROUND = 12582912.0
TURN = 6.283185
HALF_PI = 1.5707963267948966
EPS = 1e-5


def build(nc, x, W_in, conv_k, theta, decay_slopes, anchor_slopes, score_scale, W_re, W_im,
          norm_scale, W_out, router_w, w_fc, w_proj, shared_fc, shared_proj, tables, out):
    ctx = ExitStack()

    def sb(name, shape, dt=F32, c=ctx):
        return c.enter_context(nc.sbuf_tensor(name, shape, dt))

    def ps(name, shape, c):
        return c.enter_context(nc.psum_tensor(name, shape, F32))

    with ctx:
        x_tok = sb("x_tok", [P, NT + 1, D])
        xT = sb("xT", [P, 2, B, HALO + L + P], F32R)
        y_all = sb("y_all", [P, NT + GT, KH])
        p_tok = sb("p_tok", [P, TPB, B, K])
        inv_den = sb("inv_den", [P, TPB, B, K])
        ident = sb("ident", [P, P])
        tri = sb("tri", [P, P])
        wconv = sb("wconv", [P, 2, TAPS, KH], F32R)
        wq = sb("wq", [P, 2, 2 * KQ * HM], F32R)
        thblk = sb("thblk", [P, 2, NF], F32R)
        w_out = sb("w_out", [P, D])
        routerT = sb("routerT", [P, E])
        half_pi = sb("half_pi", [P, 1])
        rows = sb("rows", [P, P + NT])
        x1_dram = nc.dram_tensor("x1_scratch", (NTOK, D), F32, kind="Internal").ap()
        pick_dram = nc.dram_tensor("pick_scratch", (2 * NTOK, D), F32, kind="Internal").ap()

        setup(nc, x, W_in, conv_k, theta, decay_slopes, anchor_slopes, score_scale, W_re, W_im,
              norm_scale, W_out, router_w, tables, x_tok, xT, p_tok, inv_den, ident, tri, wconv, wq,
              thblk, w_out, routerT, half_pi, rows)
        memory(nc, xT, y_all, p_tok, inv_den, tri, wconv, wq, thblk, half_pi)
        x1T = xT[:].rearrange("p a b l -> p a (b l)")[:, :, 0:NTOK]
        mixture(nc, x_tok, x1T, y_all, ident, tri, rows, w_out, routerT, w_fc, w_proj, shared_fc, shared_proj,
                x1_dram, pick_dram, out)


def setup(nc, x, W_in, conv_k, theta, decay_slopes, anchor_slopes, score_scale, W_re, W_im,
          norm_scale, W_out, router_w, tables, x_tok, xT, p_tok, inv_den, ident, tri, wconv, wq,
          thblk, w_out, routerT, half_pi, rows):
    with ExitStack() as c:
        def sb(name, shape, dt=F32):
            return c.enter_context(nc.sbuf_tensor("setup_" + name, shape, dt))

        def ps(name, shape):
            return c.enter_context(nc.psum_tensor("setup_" + name, shape, F32))

        def sem(name):
            return c.enter_context(nc.semaphore("setup_" + name))

        TOTAL = KH + K + 2 * KQ * HM
        w_in = sb("w_in", [P, TOTAL])
        taps_row = sb("taps_row", [P, TAPS, KH])
        theta_k = sb("theta_k", [P, M])
        slot_par = sb("slot_par", [K, 2 + TAPS])
        spread = sb("spread", [K, B, K])
        par = sb("par", [P, 2 + TAPS])
        dist = sb("dist", [P, L])
        diag = sb("diag", [P, 2, H])
        norm = sb("norm", [P, 2, H])
        coef = sb("coef", [P, 2, H])
        ncoef = sb("ncoef", [P, 2, H])
        r_w = sb("r_w", [E, D])
        ones = sb("ones", [P, P])
        wconv_f = sb("wconv_f", [P, TAPS, KH])
        wq_f = sb("wq_f", [P, 2, KQ, HM])
        wq_t = sb("wq_t", [P, 2, KQ, HM])
        th_f = sb("th_f", [P, NF])
        ws_f = sb("ws_f", [P, B, P])
        ws = sb("ws", [P, 2, B, P], F32R)
        zs = sb("zs", [P, HALO + L])
        lp = sb("lp", [P, L])
        lq = sb("lq", [P, L])
        sp = sb("sp", [P, 8])
        cum = sb("cum", [P, TPB - 1, B * K])
        pst = [ps(f"pst{i}", [P, 512]) for i in range(2)]
        pz = ps("pz", [P, L])
        pp = ps("pp", [P, 1024])
        pt = ps("pt", [P, E + 2 + TAPS])

        x_in = [sem(f"x_in{b}") for b in range(B)]
        w_arrived = sem("w_arrived")
        tabs_in = sem("tabs_in")
        ident_in = sem("ident_in")
        small_in = sem("small_in")
        slot_in = sem("slot_in")
        spread_done = sem("spread_done")
        par_done = sem("par_done")
        theta_scaled = sem("theta_scaled")
        coef_done = sem("coef_done")
        pchain = sem("pchain")
        made = sem("made")
        made_high = sem("made_high")
        cum_done = sem("cum_done")
        folded = sem("folded")
        dchain = sem("dchain")
        x_turned = sem("x_turned")
        x_high = sem("x_high")
        x_low = sem("x_low")
        z_done = sem("z_done")
        z_kept = sem("z_kept")
        soft_exp = sem("soft_exp")
        soft_in = sem("soft_in")
        lp_ready = sem("lp_ready")
        p_exp = sem("p_exp")
        p_turned = sem("p_turned")
        p_kept = sem("p_kept")
        sums = sem("sums")
        r_turned = sem("r_turned")
        block = c.enter_context(nc.Block())
        N_SMALL = 7

        @block.sync
        def _(sp_):
            sp_.dma_start(ident[:], tables[:, 0:P]).then_inc(ident_in, 16)
            for b in range(B):
                sp_.dma_start(x_tok[:, b * TPB:(b + 1) * TPB, :],
                              x[b].rearrange("(j p) d -> p j d", p=P)).then_inc(x_in[b], 16)
            sp_.dma_start(tri[:], tables[:, P:2 * P]).then_inc(tabs_in, 16)
            sp_.dma_start(dist[:], tables[:, 2 * P:2 * P + L]).then_inc(tabs_in, 16)
            sp_.dma_start(rows[:], tables[:, 2 * P + L:]).then_inc(tabs_in, 16)
            sp_.wait_ge(tabs_in, 48)

        @block.scalar
        def _(act):
            act.dma_start(w_in[:], W_in).then_inc(w_arrived, 16)
            with nc.allow_non_contiguous_dma(reason="small parameter rows"):
                act.dma_start(slot_par[0:K - 4, 0:1], decay_slopes.unsqueeze(1)).then_inc(slot_in, 16)
                act.dma_start(slot_par[K - 4:K, 0:1], anchor_slopes.unsqueeze(1)).then_inc(slot_in, 16)
                act.dma_start(slot_par[:, 1:2], score_scale.unsqueeze(1)).then_inc(slot_in, 16)
                act.dma_start(slot_par[:, 2:], conv_k[:, 0, KH:KH + K].rearrange("t k -> k t")).then_inc(slot_in, 16)
                act.dma_start(taps_row[:], conv_k[:, 0, 0:KH].unsqueeze(0).broadcast_to([P, TAPS, KH])
                              ).then_inc(small_in, 16)
                act.dma_start(theta_k[:], theta[0, 0].rearrange("k h m -> (k h) m")).then_inc(small_in, 16)
                for i, w in enumerate((W_re, W_im)):
                    dg = w.rearrange("a b -> (a b)")[0:H * H:H + 1]
                    act.dma_start(diag[:, i, :], dg.unsqueeze(0).broadcast_to([P, H])).then_inc(small_in, 16)
                act.dma_start(norm[:], norm_scale.rearrange("(i h) -> i h", i=2).unsqueeze(0)
                              .broadcast_to([P, 2, H])).then_inc(small_in, 16)
                act.dma_start(w_out[:], W_out).then_inc(small_in, 16)
                act.dma_start(r_w[:], router_w).then_inc(small_in, 16)
            for g in range(2 * B):
                act.wait_ge(x_turned, g + 1)
                b, half = g // 2, g % 2
                nc.scalar.copy(xT[:, 0, b, HALO + half * 512:HALO + (half + 1) * 512], pst[g % 2][:]
                               ).then_inc(x_high, 1)
                if g == 3:
                    act.wait_ge(soft_in, 1)
                    nc.scalar.activation(sp[:, 1:2], sp[:, 0:1], ACT.Exp).then_inc(soft_exp, 1)
            for half in range(2):
                act.wait_ge(z_done, half + 1)
                nc.scalar.copy(zs[:, HALO + half * 512:HALO + (half + 1) * 512], pz[:, half * 512:(half + 1) * 512]
                               ).then_inc(z_kept, 1)
            act.wait_ge(made, 1)
            nc.scalar.copy(wconv[:, 0], wconv_f[:]).then_inc(made_high, 1)
            act.wait_ge(made, 2)
            nc.scalar.copy(thblk[:, 0], th_f[:]).then_inc(made_high, 1)
            act.wait_ge(lp_ready, 1)
            nc.scalar.activation(lq[:], lp[:], ACT.Exp).then_inc(p_exp, 1)
            act.wait_ge(p_turned, 1)
            nc.scalar.copy(p_tok[:].rearrange("p j b k -> p (j b k)"), pp[:]).then_inc(p_kept, 1)
            act.wait_ge(made, 3)
            nc.scalar.copy(wq[:, 0], wq_f[:].rearrange("p i q m -> p (i q m)")).then_inc(made_high, 1)

        @block.gpsimd
        def _(pool):
            n = [0]

            def link(ins):
                n[0] += 1
                ins.then_inc(pchain, 1)
                pool.wait_ge(pchain, n[0])

            pool.wait_ge(small_in, 16 * N_SMALL)
            pool.wait_ge(w_arrived, 16)
            nc.gpsimd.tensor_tensor(wconv_f[:], taps_row[:], w_in[:, 0:KH].unsqueeze(1).broadcast_to([P, TAPS, KH]),
                                    ALU.mult).then_inc(made, 1)
            pool.wait_ge(theta_scaled, 1)
            pool.wait_ge(ident_in, 16)
            nc.gpsimd.tensor_tensor(th_f[:].rearrange("p (c m) -> p c m", m=M),
                                    ident[:].unsqueeze(2).broadcast_to([P, P, M]),
                                    theta_k[:].unsqueeze(1).broadcast_to([P, P, M]), ALU.mult).then_inc(made, 1)
            pool.wait_ge(coef_done, 1)
            wv = w_in[:, KH + K:TOTAL].rearrange("p (q h m r) -> p q h m r", q=KQ, h=H, m=M)
            for q in range(KQ):
                qr, qi = wv[:, q, :, :, 0], wv[:, q, :, :, 1]
                cb, na, nb = (t[:, i, :].unsqueeze(2).broadcast_to([P, H, M])
                              for t, i in ((coef, 1), (ncoef, 0), (ncoef, 1)))
                ca = coef[:, 0, :].unsqueeze(2).broadcast_to([P, H, M])
                v = [t[:, i, q, :].rearrange("p (h m) -> p h m", m=M) for t in (wq_f, wq_t) for i in range(2)]
                nc.gpsimd.tensor_tensor(v[0], qi, na, ALU.mult)
                nc.gpsimd.tensor_tensor(v[2], qr, nb, ALU.mult)
                nc.gpsimd.tensor_tensor(v[1], qr, ca, ALU.mult)
                last = nc.gpsimd.tensor_tensor(v[3], qi, cb, ALU.mult)
            link(last)
            nc.gpsimd.tensor_tensor(wq_f[:, 0], wq_f[:, 0], wq_t[:, 0], ALU.add)
            nc.gpsimd.tensor_tensor(wq_f[:, 1], wq_f[:, 1], wq_t[:, 1], ALU.subtract).then_inc(made, 1)
            wf = wq_f[:].rearrange("p i q m -> p (i q m)")
            for m, (full, parts) in enumerate(((wconv_f[:], wconv), (th_f[:], thblk), (wf, wq))):
                pool.wait_ge(made_high, m + 1)
                if m == 2:
                    pool.wait_ge(made, 3)
                nc.gpsimd.tensor_tensor(parts[:, 1], full, parts[:, 0].bitcast(F32), ALU.subtract)

        @block.tensor
        def _(pe):
            pe.wait_ge(ident_in, 16)

            def turn(g):
                b, half = g // 2, g % 2
                if half == 0:
                    pe.wait_ge(x_in[b], 16)
                if g >= 2:
                    pe.wait_ge(x_low, g - 1)
                for q in range(4):
                    last = nc.tensor.transpose(pst[g % 2][:, q * P:(q + 1) * P],
                                               x_tok[:, b * TPB + half * 4 + q, :], ident[:])
                last.then_inc(x_turned, 1)

            def scores(b):
                pe.wait_ge(x_low, 2 * b + 2)
                pe.wait_ge(folded, 1)
                for half in range(2):
                    for m, (a, w) in enumerate(((0, 0), (1, 0), (0, 1))):
                        last = nc.tensor.matmul(pz[:, half * 512:(half + 1) * 512], ws[:, w, b, :],
                                                xT[:, a, b, HALO + half * 512:HALO + (half + 1) * 512],
                                                start=(b == 0 and m == 0), stop=(b == B - 1 and m == 2))
                    if b == B - 1:
                        last.then_inc(z_done, 1)

            turn(0)
            turn(1)
            pe.wait_ge(slot_in, 64)
            pe.wait_ge(spread_done, 1)
            nc.tensor.matmul(pt[:, E:], spread[:].rearrange("k b c -> k (b c)"), slot_par[:], start=True, stop=True
                             ).then_inc(par_done, 1)
            for b in range(1, B):
                turn(2 * b)
                turn(2 * b + 1)
                scores(b - 1)
            scores(B - 1)
            pe.wait_ge(small_in, 16 * N_SMALL)
            nc.tensor.transpose(pt[:, 0:E], r_w[:], ident[0:E, 0:E]).then_inc(r_turned, 1)
            pe.wait_ge(p_exp, 1)
            for j in range(TPB):
                last = nc.tensor.transpose(pp[:, j * P:(j + 1) * P], lq[:, j * P:(j + 1) * P], ident[:])
            last.then_inc(p_turned, 1)
            pe.wait_ge(tabs_in, 48)
            pe.wait_ge(p_kept, 1)
            pv = p_tok[:].rearrange("p j b k -> p (j b k)")
            cv = cum[:].rearrange("p j c -> p (j c)")
            for h in range(2):
                nc.tensor.matmul(pp[:, h * 512:(h + 1) * 512], tri[:], pv[:, h * 512:(h + 1) * 512],
                                 start=True, stop=False)
            pe.wait_ge(cum_done, TPB - 1)
            nc.tensor.matmul(pp[:, P:512], ones[:], cv[:, 0:512 - P], start=False, stop=True)
            nc.tensor.matmul(pp[:, 512:], ones[:], cv[:, 512 - P:], start=False, stop=True).then_inc(sums, 1)

        @block.vector
        def _(dve):
            n = [0]

            def link(ins):
                n[0] += 1
                ins.then_inc(dchain, 1)
                dve.wait_ge(dchain, n[0])

            nc.vector.memset(ones[:], 1.0)
            nc.vector.memset(half_pi[:], HALF_PI)
            nc.vector.memset(xT[:, :, :, 0:HALO].bitcast(F32), 0.0)
            nc.vector.memset(xT[:, :, :, HALO + L:].bitcast(F32), 0.0)
            nc.vector.memset(zs[:, 0:HALO], 0.0)
            nc.vector.memset(x_tok[:, NT, :], 0.0)
            link(nc.vector.memset(ws_f[:], 0.0))
            dve.wait_ge(w_arrived, 16)
            for b in range(B):
                last = nc.vector.tensor_copy(ws_f[:, b, b * K:(b + 1) * K], w_in[:, KH:KH + K])
            link(last)
            link(nc.vector.tensor_copy(ws[:, 0], ws_f[:]))
            nc.vector.tensor_tensor(ws[:, 1], ws_f[:], ws[:, 0].bitcast(F32), ALU.subtract).then_inc(folded, 1)
            dve.wait_ge(ident_in, 16)
            nc.vector.tensor_copy(spread[:], ident[0:K, 0:K].unsqueeze(1).broadcast_to([K, B, K])
                                  ).then_inc(spread_done, 1)

            def low(g):
                b, half = g // 2, g % 2
                dve.wait_ge(x_high, g + 1)
                hi = xT[:, 0, b, HALO + half * 512:HALO + (half + 1) * 512]
                nc.vector.tensor_tensor(xT[:, 1, b, HALO + half * 512:HALO + (half + 1) * 512],
                                        pst[g % 2][:], hi.bitcast(F32), ALU.subtract).then_inc(x_low, 1)
            slope, score, taps_s = par[:, 0:1], par[:, 1:2], par[:, 2:]
            low(0)
            low(1)
            dve.wait_ge(par_done, 1)
            link(nc.vector.tensor_copy(par[:], pt[:, E:]))
            link(nc.vector.tensor_scalar(sp[:, 2:3], slope, -1.0, None, ALU.mult))
            nc.vector.tensor_tensor(sp[:, 0:1], slope, sp[:, 2:3], ALU.min).then_inc(soft_in, 1)
            low(2)
            low(3)
            dve.wait_ge(soft_exp, 1)
            ex, zt, z2, acc = sp[:, 1:2], sp[:, 3:4], sp[:, 4:5], sp[:, 5:6]
            link(nc.vector.tensor_scalar(zt, ex, 2.0, None, ALU.add))
            link(nc.vector.reciprocal(z2, zt))
            link(nc.vector.tensor_tensor(zt, z2, ex, ALU.mult))
            link(nc.vector.tensor_tensor(z2, zt, zt, ALU.mult))
            link(nc.vector.tensor_scalar(acc, z2, 1.0 / 17, 1.0 / 15, ALU.mult, ALU.add))
            low(4)
            low(5)
            for k in (13, 11, 9, 7):
                link(nc.vector.tensor_tensor(acc, acc, z2, ALU.mult))
                link(nc.vector.tensor_scalar(acc, acc, 1.0 / k, None, ALU.add))
            low(6)
            low(7)
            for k in (5, 3, 1):
                link(nc.vector.tensor_tensor(acc, acc, z2, ALU.mult))
                link(nc.vector.tensor_scalar(acc, acc, 1.0 / k, None, ALU.add))
            link(nc.vector.tensor_tensor(acc, acc, zt, ALU.mult))
            link(nc.vector.tensor_scalar(acc, acc, 2.0, None, ALU.mult))
            link(nc.vector.tensor_scalar(sp[:, 6:7], slope, 0.0, None, ALU.max))
            link(nc.vector.tensor_tensor(acc, acc, sp[:, 6:7], ALU.add))
            link(nc.vector.tensor_scalar(sp[:, 7:8], acc, -1.0, None, ALU.mult))
            dve.wait_ge(small_in, 16 * N_SMALL)
            nc.vector.tensor_scalar(theta_k[:], theta_k[:], 0.15915494309189535, None, ALU.mult
                                    ).then_inc(theta_scaled, 1)
            link(nc.vector.tensor_tensor(coef[:], norm[:], diag[:], ALU.mult))
            nc.vector.tensor_scalar(ncoef[:], coef[:], -1.0, None, ALU.mult).then_inc(coef_done, 1)
            dve.wait_ge(z_kept, 2)
            link(nc.vector.tensor_scalar(lp[:], zs[:, 0:L], taps_s[:, 0:1], None, ALU.mult))
            for t in range(1, TAPS):
                link(nc.vector.scalar_tensor_tensor(lp[:], zs[:, t:t + L], taps_s[:, t:t + 1], lp[:],
                                                    ALU.mult, ALU.add))
            link(nc.vector.tensor_scalar(lp[:], lp[:], score, 20.0, ALU.mult, ALU.min))
            link(nc.vector.tensor_scalar(lp[:], lp[:], -20.0, None, ALU.max))
            dve.wait_ge(tabs_in, 48)
            nc.vector.scalar_tensor_tensor(lp[:], dist[:], sp[:, 7:8], lp[:], ALU.mult, ALU.add
                                           ).then_inc(lp_ready, 1)
            dve.wait_ge(r_turned, 1)
            nc.vector.tensor_copy(routerT[:], pt[:, 0:E])
            dve.wait_ge(p_kept, 1)
            pt_v = p_tok[:].rearrange("p j b k -> p j (b k)")
            nc.vector.tensor_copy(cum[:, 0], pt_v[:, 0]).then_inc(cum_done, 1)
            for j in range(1, TPB - 1):
                dve.wait_ge(cum_done, j)
                nc.vector.tensor_tensor(cum[:, j], cum[:, j - 1], pt_v[:, j], ALU.add).then_inc(cum_done, 1)
            dve.wait_ge(sums, 1)
            dv = inv_den[:].rearrange("p j b k -> p (j b k)")
            link(nc.vector.tensor_scalar(dv, pp[:], 1e-4, None, ALU.max))
            first = inv_den[:, 0:NINV].rearrange("p j b k -> p (j b k)")
            nc.vector.reciprocal(first, first)


def memory(nc, xT, y_all, p_tok, inv_den, tri, wconv, wq, thblk, half_pi):
    with ExitStack() as c:
        def sb(name, shape, dt=F32):
            return c.enter_context(nc.sbuf_tensor("memory_" + name, shape, dt))

        def ps(name, shape):
            return c.enter_context(nc.psum_tensor("memory_" + name, shape, F32))

        def sem(name):
            return c.enter_context(nc.semaphore("memory_" + name))

        x_st = sb("x_st", [P, 2, 2, P], F32R)
        k_st = sb("k_st", [P, 2, 2, P], F32R)
        rounded = sb("rounded", [P, 2, NF])
        frac = sb("frac", [P, 2, NF])
        afrac = sb("afrac", [P, 2, NF])
        feat = sb("feat", [P, 2, 2, NF])
        wfeat = sb("wfeat", [P, 2, 2, NF])
        query = sb("query", [P, B, 2 * KQ * HM])
        prod = sb("prod", [P, 2, NF])
        y_raw = sb("y_raw", [P, KH])
        last_rows = sb("last_rows", [P, B, 2 * NF])
        warm = sb("warm", [P, 1])
        ph = ps("ph", [P, NF])
        nsum = ps("nsum", [P, 2 * NF])
        pk = ps("pk", [P, P])
        pq = ps("pq", [P, 2 * KQ * HM])

        x_ready = sem("x_ready")
        k_done = sem("k_done")
        k_high = sem("k_high")
        k_low = sem("k_low")
        q_done = sem("q_done")
        q_kept = sem("q_kept")
        ph_done = sem("ph_done")
        rnd_done = sem("rnd_done")
        frac_done = sem("frac_done")
        abs_done = sem("abs_done")
        feat_done = sem("feat_done")
        wfeat_done = sem("wfeat_done")
        carried = [sem(f"carried{b}") for b in range(B)]
        carry_due = sem("carry_due")
        sum_done = sem("sum_done")
        prod_done = sem("prod_done")
        rows_kept = sem("rows_kept")
        red_done = sem("red_done")
        y_done = sem("y_done")
        warmed = sem("warmed")
        inverted = sem("inverted")
        block = c.enter_context(nc.Block())

        def steps(eng, front, body):
            front()
            body(0, True, False)
            with eng.Fori(1, TPB - 1) as step:
                body(step, False, False)
            body(TPB - 1, False, True)

        def ahead(step, b, n):
            return (step, b + n) if b + n < B else (step + 1, b + n - B)

        @block.tensor
        def _(pe):
            def values(step, b, lead=False):
                i, s = B * step + b, b % 2
                if not lead or b > 0:
                    pe.wait_ge(k_low, i)
                n = 0
                for t in range(TAPS):
                    for a, w in ((0, 0), (1, 0), (0, 1)):
                        last = nc.tensor.matmul(pk[:], wconv[:, w, t, :],
                                                xT[:, a, b, bass.ds(step * P + t, P)],
                                                start=(n == 0), stop=(n == 3 * TAPS - 1))
                        n += 1
                last.then_inc(k_done, 1)

            def phases(step, b, lead=False):
                i, s = B * step + b, b % 2
                pe.wait_ge(x_ready, i + 1)
                if not lead or b > 0:
                    pe.wait_ge(q_kept, i)
                for n, (a, w) in enumerate(((0, 0), (1, 0), (0, 1))):
                    last = nc.tensor.matmul(pq[:], x_st[:, s, a, :], wq[:, w, :], start=(n == 0), stop=(n == 2))
                last.then_inc(q_done, 1)
                pe.wait_ge(k_low, i + 1)
                if not lead or b > 0:
                    pe.wait_ge(frac_done, i)
                for h in range(2):
                    for n, (a, w) in enumerate(((0, 0), (1, 0), (0, 1))):
                        last = nc.tensor.matmul(ph[:, h * 512:(h + 1) * 512], k_st[:, s, a, :],
                                                thblk[:, w, h * 512:(h + 1) * 512], start=(n == 0), stop=(n == 2))
                last.then_inc(ph_done, 1)

            def sums(step, b, first, last):
                i, s = B * step + b, b % 2
                pe.wait_ge(wfeat_done, i + 1)
                if not first:
                    pe.wait_ge(carried[b], 16 * step)
                for h in range(2):
                    if not (first and b == 0):
                        pe.wait_ge(prod_done, 2 * i - 1 + h)
                        if not (last and b > 0):
                            pe.wait_ge(rows_kept, 2 * i - 1 + h)
                    for q in range(2):
                        o = h * NF + q * 512
                        end = nc.tensor.matmul(nsum[:, o:o + 512], tri[:],
                                               wfeat[:, s, h, q * 512:(q + 1) * 512], start=True, stop=True)
                    end.then_inc(sum_done, 1)

            def front():
                values(0, 0, True)
                for b in range(3):
                    values(0, b + 1, True)
                    phases(0, b, True)

            def body(step, first, last):
                for b in range(B):
                    if not (last and b + 3 >= B):
                        phases(*ahead(step, b, 3))
                    if not last:
                        values(*ahead(step, b, 4))
                    sums(step, b, first, last)
            steps(pe, front, body)

        @block.scalar
        def _(act):
            def k_part(step, b, lead=False):
                i, s = B * step + b, b % 2
                act.wait_ge(k_done, i + 1)
                if not lead or b >= 2:
                    act.wait_ge(ph_done, i - 1)
                nc.scalar.copy(k_st[:, s, 0, :], pk[:]).then_inc(k_high, 1)

            def rounding(step, b, lead=False):
                i, s = B * step + b, b % 2
                act.wait_ge(ph_done, i + 1)
                if not lead or b >= 2:
                    act.wait_ge(frac_done, i - 1)
                nc.scalar.activation(rounded[:, s, :], ph[:], ACT.Copy, bias=ROUND).then_inc(rnd_done, 1)
                act.wait_ge(q_done, i + 1)
                if not (lead or isinstance(step, int) and step == 0):
                    act.wait_ge(prod_done, 2 * i - 6)
                nc.scalar.copy(query[:, b, :], pq[:]).then_inc(q_kept, 1)

            def sine(step, b, lead=False):
                i, s = B * step + b, b % 2
                act.wait_ge(frac_done, i + 1)
                nc.scalar.activation(afrac[:, s, :], frac[:, s, :], ACT.Abs).then_inc(abs_done, 1)
                if not lead:
                    act.wait_ge(wfeat_done, i - 1)
                nc.scalar.activation(feat[:, s, 0, :], frac[:, s, :], ACT.Sin, scale=TURN)

            def cosine(step, b):
                i, s = B * step + b, b % 2
                act.wait_ge(abs_done, i + 1)
                nc.scalar.activation(feat[:, s, 1, :], afrac[:, s, :], ACT.Sin, scale=-TURN,
                                     bias=half_pi[:]).then_inc(feat_done, 1)

            def rows(step, b, h, first):
                i = B * step + b
                if not first:
                    act.wait_ge(carried[b], 16 * step)
                act.wait_ge(prod_done, 2 * i + 1 + h)
                nc.scalar.copy(last_rows[96:P, b, h * NF:(h + 1) * NF], nsum[96:P, h * NF:(h + 1) * NF]
                               ).then_inc(rows_kept, 1)

            def front():
                nc.scalar.activation(warm[:], half_pi[:], ACT.Sin).then_inc(warmed, 1)
                act.wait_ge(warmed, 1)
                k_part(0, 0, True)
                k_part(0, 1, True)
                for b in range(3):
                    rounding(0, b, True)
                    if b < 2:
                        k_part(0, b + 2, True)
                        sine(0, b, True)
                        cosine(0, b)

            def body(step, first, last):
                for b in range(B):
                    if not (last and b + 3 >= B):
                        rounding(*ahead(step, b, 3))
                    if not last:
                        k_part(*ahead(step, b, 4))
                    if not (last and b + 2 >= B):
                        sine(*ahead(step, b, 2))
                    if not last:
                        rows(step, b, 0, first)
                    if not (last and b + 2 >= B):
                        cosine(*ahead(step, b, 2))
                    if not last:
                        rows(step, b, 1, first)
            steps(act, front, body)
            nc.scalar.activation(warm[:], half_pi[:], ACT.Silu)

        @block.vector
        def _(dve):
            def x_part(step, b, lead=False):
                i, s = B * step + b, b % 2
                if not lead or b >= 2:
                    dve.wait_ge(q_done, i - 1)
                nc.vector.tensor_copy(x_st[:, s], xT[:, :, b, bass.ds(step * P + HALO, P)].bitcast(F32)
                                      ).then_inc(x_ready, 1)

            def k_part(step, b, lead=False):
                i, s = B * step + b, b % 2
                dve.wait_ge(k_high, i + 1)
                nc.vector.tensor_tensor(k_st[:, s, 1, :], pk[:], k_st[:, s, 0, :].bitcast(F32), ALU.subtract
                                        ).then_inc(k_low, 1)

            def fraction(step, b, lead=False):
                i, s = B * step + b, b % 2
                dve.wait_ge(rnd_done, i + 1)
                if not lead or b >= 2:
                    dve.wait_ge(feat_done, i - 1)
                nc.vector.scalar_tensor_tensor(frac[:, s, :], rounded[:, s, :], -ROUND, ph[:],
                                               ALU.add, ALU.subtract).then_inc(frac_done, 1)

            def read_out(step, b, first):
                i, s = B * step + b, b % 2
                dve.wait_ge(q_kept, i + 1)
                if not (first and b == 0):
                    dve.wait_ge(red_done, i)
                for h in range(2):
                    dve.wait_ge(sum_done, 2 * i + 1 + h)
                    nv = nsum[:, h * NF:(h + 1) * NF].rearrange("p (q r c) -> p q r c", q=KQ, r=REP)
                    qv = query[:, b, h * KQ * HM:(h + 1) * KQ * HM].rearrange("p (q c) -> p q c", q=KQ)
                    nc.vector.tensor_tensor(prod[:, h, :].rearrange("p (q r c) -> p q r c", q=KQ, r=REP),
                                            nv, qv.unsqueeze(2).broadcast_to([P, KQ, REP, HM]), ALU.mult
                                            ).then_inc(prod_done, 1)
                dve.wait_ge(prod_done, 2 * i + 2)
                if not (first and b == 0):
                    dve.wait_ge(y_done, i)
                nc.vector.tensor_reduce(y_raw[:], prod[:].rearrange("p h (c m) -> p c h m", m=M), AX.XY, ALU.add
                                        ).then_inc(red_done, 1)
                dve.wait_ge(red_done, i + 1)
                nc.vector.tensor_tensor(
                    y_all[:, bass.ds(step + b * TPB, 1), :].rearrange("p o (k h) -> p (o k) h", h=H),
                    y_raw[:].rearrange("p (k h) -> p k h", h=H),
                    inv_den[:, bass.ds(step, 1), b, :].rearrange("p o k -> p (o k)").unsqueeze(2)
                    .broadcast_to([P, K, H]), ALU.mult).then_inc(y_done, 1)

            HALF = (NINV + TPB) // 2

            def invert(a, b):
                part = inv_den[:, a:b].rearrange("p j b k -> p (j b k)")
                nc.vector.reciprocal(part, part).then_inc(inverted, 1)

            def front():
                x_part(0, 0, True)
                x_part(0, 1, True)
                k_part(0, 0, True)
                k_part(0, 1, True)
                invert(NINV, HALF)
                for b in range(3):
                    fraction(0, b, True)
                    if b < 2:
                        x_part(0, b + 2, True)
                        k_part(0, b + 2, True)
                    if b == 0:
                        invert(HALF, TPB)

            def body(step, first, last):
                if not first:
                    dve.wait_ge(inverted, 2)
                for b in range(B):
                    if not (last and b + 3 >= B):
                        fraction(*ahead(step, b, 3))
                    if not last:
                        x_part(*ahead(step, b, 4))
                        k_part(*ahead(step, b, 4))
                    read_out(step, b, first)
            steps(dve, front, body)

        @block.gpsimd
        def _(pool):
            def weigh(step, b, lead, first):
                i, s = B * step + b, b % 2
                pool.wait_ge(feat_done, i + 1)
                if not lead:
                    pool.wait_ge(sum_done, 2 * i - 2)
                pv = p_tok[:, bass.ds(step, 1), b, :].rearrange("p o k -> p (o k)").unsqueeze(2)
                for h in range(2):
                    ins = nc.gpsimd.tensor_tensor(wfeat[:, s, h].rearrange("p (k c) -> p k c", k=K),
                                                  feat[:, s, h].rearrange("p (k c) -> p k c", k=K),
                                                  pv.broadcast_to([P, K, HM]), ALU.mult)
                ins.then_inc(wfeat_done, 1)
                if not first:
                    pool.wait_ge(wfeat_done, i + 1)
                    pool.wait_ge(rows_kept, 2 * (i - B) + 2)
                    nc.gpsimd.sem_inc(carry_due, 1)
                    pool.dma_start(wfeat[0:1, s].rearrange("p h c -> p (h c)"),
                                   last_rows[P - 1:P, b, :], accum_op=ALU.add).then_inc(carried[b], 16)

            for b in range(B):
                weigh(0, b, b < 2, True)
            with pool.Fori(1, TPB) as step:
                for b in range(B):
                    weigh(step, b, False, False)


def mixture(nc, x_tok, x1T, y_all, ident, tri, rows, w_out, routerT, w_fc, w_proj, shared_fc, shared_proj,
            x1_dram, pick_dram, out):
    with ExitStack() as ctx:
        w1 = ctx.enter_context(nc.sbuf_tensor("w1", [P, 2, NE, FF], F32R))
        w2 = ctx.enter_context(nc.sbuf_tensor("w2", [P, NE, FC, D], F32))
        logits = ctx.enter_context(nc.sbuf_tensor("logits", [P, NT, E], F32))
        weight = ctx.enter_context(nc.sbuf_tensor("weight", [P, 2, NT], F32))
        take = ctx.enter_context(nc.sbuf_tensor("take", [P, SLOTS + ROWS // P], U32))
        put = ctx.enter_context(nc.sbuf_tensor("put", [P, SLOTS], U32))
        expert = ctx.enter_context(nc.sbuf_tensor("expert", [1, TILES], I32))
        project(nc, x_tok, x1T, y_all, ident, w_out, routerT, w_fc, w_proj, shared_fc, shared_proj, w1, w2,
                logits, x1_dram)
        route(nc, x1T, y_all, w1, w2, logits, tri, rows, weight, take, put, expert)
        routed(nc, x1T, y_all, ident, w1, w2, take, put, expert, x1_dram, pick_dram)
        finish(nc, y_all, weight, pick_dram, out)


def project(nc, x_tok, x1T, y_all, ident, w_out, routerT, w_fc, w_proj, shared_fc, shared_proj, w1, w2,
            logits, x1_dram):
    with ExitStack() as c:
        def sb(name, shape, dt=F32):
            return c.enter_context(nc.sbuf_tensor("project_" + name, shape, dt))

        def ps(name, shape):
            return c.enter_context(nc.psum_tensor("project_" + name, shape, F32))

        def sem(name):
            return c.enter_context(nc.semaphore("project_" + name))

        w_nat = sb("w_nat", [P, 2, 2, FC, D])
        sy = sb("sy", [P, GT * KH])
        syT = sb("syT", [P, GT, P])
        res = sb("res", [P, GT, D])
        stats = sb("stats", [P, GT, 6])
        mv = sb("mv", [P, GT, 2])
        std = sb("std", [P, GT])
        rstd = sb("rstd", [P, GT])
        eps = sb("eps", [P, 1])
        xn = sb("xn", [P, 2, GT, D])
        xnT = sb("xnT", [P, GT, P])
        pw = [ps(f"pw{m}", [P, 512]) for m in range(2)]
        pa = ps("pa", [P, 512])
        pb = ps("pb", [P, 512])
        pl = ps("pl", [P, GT * E])

        w_in = [sem(f"w_in_slot{i}") for i in range(2)]
        turned = sem("w_turned")
        w_kept = sem("w_kept")
        w_low = sem("w_low")
        silu_done = sem("silu_done")
        sy_ready = sem("sy_ready")
        yT_done = sem("yT_done")
        yT_kept = sem("yT_kept")
        proj_done = sem("proj_done")
        res_done = sem("res_done")
        stats_due = sem("stats_due")
        var_done = sem("var_done")
        std_done = sem("std_done")
        rstd_done = sem("rstd_done")
        xn_done = sem("xn_done")
        xnT_done = sem("xnT_done")
        xnT_kept = sem("xnT_kept")
        xs_high = sem("xs_high")
        xs_done = sem("xs_done")
        x1_kept = sem("x1_kept")
        padded = sem("padded")
        log_done = sem("log_done")
        log_kept = sem("log_kept")
        stored = [sem(f"stored{i}") for i in range(2)]
        block = c.enter_context(nc.Block())

        def groups(eng, front, body):
            front()
            body(0, 0, 2)
            body(1, 1, 2)
            with eng.Fori(2, NG - 3, 2) as g:
                body(g, 0, 2)
                body(g + 1, 1, 2)
            body(NG - 2, 0, 1)
            body(NG - 1, 1, 0)


        @block.sync
        def _(sp):
            def load(n, s, fc, pj):
                sp.dma_start(w_nat[:, s, 0], fc.rearrange("(c p) d -> p c d", p=P)).then_inc(w_in[s], 16)
                sp.dma_start(w_nat[:, s, 1].rearrange("p c d -> p (c d)"), pj).then_inc(w_in[s], 16)

            def front():
                load(0, 1, shared_fc, shared_proj)
                load(1, 0, w_fc[0], w_proj[0])

            def body(g, s, left):
                if left:
                    sp.wait_ge(turned, 2 * g + 2)
                    load(g + 2, 1 - s, w_fc[bass.ds(g + 1, 1), :, :].rearrange("o f d -> (o f) d"),
                         w_proj[bass.ds(g + 1, 1), :, :].rearrange("o d f -> (o d) f"))
                sp.wait_ge(xn_done, g + 1)
                sp.dma_start(x1_dram[bass.ds(g * (GT * P), GT * P), :].rearrange("(t p) d -> p t d", p=P), xn[:, s]
                             ).then_inc(stored[s], 16)
            groups(sp, front, body)
            for i in range(2):
                sp.wait_ge(stored[i], 16 * NG // 2)

        @block.tensor
        def _(pe):
            def turn(n, s, arrived, first=False):
                pe.wait_ge(w_in[s], arrived)
                for m in range(2):
                    if not first:
                        if m == 0:
                            pe.wait_ge(w_low, n)
                        else:
                            pe.wait_ge(w_kept, 2 * n)
                    for q in range(FC):
                        last = nc.tensor.transpose(pw[m][:, q * P:(q + 1) * P], w_nat[:, s, m, q, :], ident[:])
                    last.then_inc(turned, 1)

            def turn_y(g):
                pe.wait_ge(sy_ready, g + 1)
                if not (isinstance(g, int) and g == 0):
                    pe.wait_ge(res_done, g)
                for t in range(GT):
                    last = nc.tensor.transpose(pa[:, t * P:(t + 1) * P], sy[:, t * KH:(t + 1) * KH], ident[:])
                last.then_inc(yT_done, 1)

            def proj(g):
                pe.wait_ge(yT_kept, g + 1)
                for t in range(GT):
                    last = nc.tensor.matmul(pa[:, t * D:(t + 1) * D], syT[:, t, :], w_out[:], start=True, stop=True)
                last.then_inc(proj_done, 1)

            def turn_x(g, s):
                pe.wait_ge(xn_done, g + 1)
                if not (isinstance(g, int) and g == 0):
                    pe.wait_ge(xs_done, g)
                for t in range(GT):
                    last = nc.tensor.transpose(pb[:, t * P:(t + 1) * P], xn[:, s, t, :], ident[:])
                last.then_inc(xnT_done, 1)

            def route_x(g):
                pe.wait_ge(xnT_kept, g + 1)
                if not (isinstance(g, int) and g == 0):
                    pe.wait_ge(log_kept, g)
                for t in range(GT):
                    last = nc.tensor.matmul(pl[:, t * E:(t + 1) * E], xnT[:, t, :], routerT[:], start=True, stop=True)
                last.then_inc(log_done, 1)

            def front():
                turn(0, 1, 32, True)
                turn_y(0)
                proj(0)
                turn_y(1)
                turn_x(0, 0)
                proj(1)
                route_x(0)
                turn_y(2)

            def body(g, s, left):
                if left > 1:
                    proj(g + 2)
                if left:
                    turn_x(g + 1, 1 - s)
                turn(g + 1, s, 16 * (g - s) + 32 + 32 * s)
                if left:
                    route_x(g + 1)
                if left > 1:
                    turn_y(g + 3)
            groups(pe, front, body)

        @block.scalar
        def _(act):
            def keep(n, e):
                act.wait_ge(turned, 2 * n + 1)
                nc.scalar.copy(w1[:, 0, bass.ds(e, 1), :].rearrange("p o f -> p (o f)"), pw[0][:]).then_inc(w_kept, 1)
                act.wait_ge(turned, 2 * n + 2)
                nc.scalar.copy(w2[:, bass.ds(e, 1)].rearrange("p o c d -> p (o c d)"), pw[1][:]).then_inc(w_kept, 1)

            def keep_y(g):
                act.wait_ge(yT_done, g + 1)
                nc.scalar.copy(syT[:].rearrange("p t c -> p (t c)"), pa[:]).then_inc(yT_kept, 1)

            def root(g):
                act.wait_ge(var_done, g + 1)
                nc.scalar.activation(std[:], mv[:, :, 1], ACT.Sqrt, bias=eps[:]).then_inc(std_done, 1)

            def keep_x(g, s):
                act.wait_ge(xnT_done, g + 1)
                if not (isinstance(g, int) and g == 0):
                    act.wait_ge(log_done, g)
                nc.scalar.copy(xnT[:].rearrange("p t c -> p (t c)"), pb[:]).then_inc(xnT_kept, 1)
                nc.scalar.copy(x1T[:, 0, bass.ds(g * (GT * P), GT * P)], pb[:]).then_inc(xs_high, 1)
                nc.scalar.copy(y_all[:, bass.ds(g * GT, GT), :], xn[:, s]).then_inc(x1_kept, 1)

            def silu(n):
                v = y_all[:, n * GT:(n + 1) * GT, :]
                nc.scalar.activation(v, v, ACT.Silu).then_inc(silu_done, 1)

            def front():
                silu(0)
                silu(1)
                keep_y(0)
                for n in range(2, NG):
                    silu(n)
                keep(0, E)
                root(0)
                keep_y(1)
                keep_x(0, 0)
                root(1)
                keep_y(2)

            def body(g, s, left):
                if left:
                    keep_x(g + 1, 1 - s)
                if left > 1:
                    root(g + 2)
                keep(g + 1, g)
                if left > 1:
                    keep_y(g + 3)
            groups(act, front, body)

        @block.vector
        def _(dve):
            nc.vector.memset(eps[:], EPS)

            def low(n, e):
                dve.wait_ge(w_kept, 2 * n + 1)
                nc.vector.tensor_tensor(w1[:, 1, bass.ds(e, 1), :].rearrange("p o f -> p (o f)"), pw[0][:],
                                        w1[:, 0, bass.ds(e, 1), :].rearrange("p o f -> p (o f)").bitcast(F32),
                                        ALU.subtract).then_inc(w_low, 1)

            def take_y(g, first):
                if first:
                    dve.wait_ge(silu_done, 1)
                else:
                    dve.wait_ge(silu_done, 2 if isinstance(g, int) and g == 1 else NG)
                    dve.wait_ge(yT_done, g)
                nc.vector.tensor_copy(sy[:], y_all[:, bass.ds(g * GT, GT), :].rearrange("p t c -> p (t c)")
                                      ).then_inc(sy_ready, 1)

            def measure(g, first):
                dve.wait_ge(proj_done, g + 1)
                if not first:
                    dve.wait_ge(xn_done, g)
                nc.vector.tensor_tensor(res[:].rearrange("p t c -> p (t c)"), pa[:],
                                        x_tok[:, bass.ds(g * GT, GT), :].rearrange("p t c -> p (t c)"), ALU.add
                                        ).then_inc(res_done, 1)
                dve.wait_ge(res_done, g + 1)
                for t in range(GT):
                    last = nc.vector.bn_stats(stats[:, t, :], res[:, t, :])
                last.then_inc(stats_due, 1)
                dve.wait_ge(stats_due, 2 * g + 1)
                nc.vector.sem_inc(stats_due, 1)
                for t in range(GT):
                    last = nc.vector.bn_aggr(mv[:, t, :], stats[:, t, :])
                last.then_inc(var_done, 1)

            def invert(g):
                dve.wait_ge(std_done, g + 1)
                nc.vector.reciprocal(rstd[:], std[:]).then_inc(rstd_done, 1)

            def normalise(g, s):
                dve.wait_ge(rstd_done, g + 1)
                if not (isinstance(g, int) and g < 2):
                    dve.wait_ge(stored[s], 8 * (g - s))
                    dve.wait_ge(x1_kept, g - 1)
                    dve.wait_ge(xnT_done, g - 1)
                for t in range(GT):
                    last = nc.vector.tensor_scalar(xn[:, s, t, :], res[:, t, :], mv[:, t, 0:1], rstd[:, t:t + 1],
                                                   ALU.subtract, ALU.mult)
                last.then_inc(xn_done, 1)

            def low_x(g):
                dve.wait_ge(xs_high, g + 1)
                cols = bass.ds(g * (GT * P), GT * P)
                nc.vector.tensor_tensor(x1T[:, 1, cols], pb[:], x1T[:, 0, cols].bitcast(F32), ALU.subtract
                                        ).then_inc(xs_done, 1)

            def keep_logits(g):
                dve.wait_ge(log_done, g + 1)
                nc.vector.tensor_copy(logits[:, bass.ds(g * GT, GT), :].rearrange("p t e -> p (t e)"), pl[:]
                                      ).then_inc(log_kept, 1)

            def front():
                nc.vector.memset(y_all[:, NT:, :], 0.0).then_inc(padded, 1)
                dve.wait_ge(padded, 1)
                take_y(0, True)
                take_y(1, False)
                measure(0, True)
                low(0, E)
                invert(0)
                normalise(0, 0)
                low_x(0)
                take_y(2, False)
                measure(1, False)
                invert(1)
                normalise(1, 1)
                keep_logits(0)

            def body(g, s, left):
                if left > 1:
                    take_y(g + 3, False)
                    measure(g + 2, False)
                if left:
                    low_x(g + 1)
                if left > 1:
                    invert(g + 2)
                    normalise(g + 2, s)
                low(g + 1, g)
                if left:
                    keep_logits(g + 1)
            groups(dve, front, body)


def route(nc, x1T, y_all, w1, w2, logits, tri, rows, weight, take, put, expert):
    TP = 8
    TURNS = 2 * NT // TP
    COLS = SLOTS + SLOTS % 2
    MOST = NTOK // ROWS
    with ExitStack() as c:
        def sb(name, shape, dt=F32):
            return c.enter_context(nc.sbuf_tensor("route_" + name, shape, dt))

        def ps(name, shape):
            return c.enter_context(nc.psum_tensor("route_" + name, shape, F32))

        def sem(name):
            return c.enter_context(nc.semaphore("route_" + name))

        prob = sb("prob", [P, NT, E])
        tmp = sb("tmp", [P, NT, E])
        order = sb("order", [P, NT, E])
        oh = sb("oh", [P, 2, NT, E])
        sel = sb("sel", [P, NT, E])
        mx = sb("mx", [P, 6, NT])
        ones = sb("ones_r", [P, P])
        keep = sb("keep", [P, E, NT])
        total = sb("total", [P, E, NT])
        upto = sb("upto", [P, E, NT])
        base = sb("base", [P, NT, E])
        steps = sb("steps", [P, MOST])
        fills = sb("fills", [P, E, MOST])
        tiles = sb("tiles", [P, 4, E])
        texp = sb("texp", [P, TILES, E])
        tex = sb("tex", [P, TILES])
        pos = sb("pos", [P, 2, NT])
        hi = sb("hi", [P, 2, NT])
        lo = sb("lo", [P, 2, NT])
        val = sb("val", [P, 2, NT])
        oneA = sb("oneA", [P, 2, TP, P], F32R)
        oneH = sb("oneH", [P, 2, TP, COLS])
        oneB = sb("oneB", [P, 2, TP, COLS], F32R)
        sl = sb("sl", [P, 3, SLOTS])
        srel = sb("srel", [P, 2, GT * P])
        shid = sb("shid", [P, 2, FC, GT * P])
        sout = sb("sout", [P, 2, GT * D])
        sph = [ps(f"sph{i}", [P, GT * P]) for i in range(2)]
        spo = ps("spo", [P, GT * D])
        pr = ps("pr", [P, NT * E])
        pt = ps("pt", [P, NT * E])
        plist = ps("plist", [P, COLS])
        s_up_done = sem("s_up_done")
        s_rel_done = sem("s_rel_done")
        s_hid_done = sem("s_hid_done")
        s_down_done = sem("s_down_done")
        s_out_kept = sem("s_out_kept")
        s_added = sem("s_added")
        chain = sem("chain")
        shifted = sem("shifted")
        exp_done = sem("exp_done")
        sel_done = sem("sel_done")
        ranked = sem("ranked")
        valued = sem("valued")
        hotA = sem("hotA")
        hotH = sem("hotH")
        hotB = sem("hotB")
        listed = sem("listed")
        block = c.enter_context(nc.Block())
        iota = rows[:, 0:P]
        token = rows[:, P:P + NT]
        def turns(eng, body):
            body(0, 0, True)
            body(1, 1, True)
            with eng.Fori(2, TURNS - 1, 2) as n:
                body(n, 0, False)
                body(n + 1, 1, False)

        @block.scalar
        def _(act):
            act.wait_ge(shifted, 1)
            nc.scalar.activation(prob[:], tmp[:], ACT.Exp).then_inc(exp_done, 1)

            def relu(g, q):
                act.wait_ge(s_up_done, g * FC + q + 1)
                if g * FC + q >= 2:
                    act.wait_ge(s_hid_done, g * FC + q - 1)
                nc.scalar.activation(srel[:, q % 2, :], sph[q % 2][:], ACT.Relu).then_inc(s_rel_done, 1)

            def square(g, q):
                act.wait_ge(s_rel_done, g * FC + q + 1)
                if g >= 2:
                    act.wait_ge(s_down_done, g - 1)
                nc.scalar.activation(shid[:, g % 2, q, :], srel[:, q % 2, :], ACT.Square).then_inc(s_hid_done, 1)

            def keep(g):
                act.wait_ge(s_down_done, g + 1)
                if g >= 2:
                    act.wait_ge(s_added, g - 1)
                nc.scalar.copy(sout[:, g % 2, :], spo[:]).then_inc(s_out_kept, 1)

            for g in range(SG):
                for q in range(FC):
                    relu(g, q)
                    if q:
                        square(g, q - 1)
                square(g, FC - 1)
                if g:
                    keep(g - 1)
            keep(SG - 1)

        @block.tensor
        def _(pe):
            def up(g):
                for q in range(FC):
                    n = g * FC + q
                    if n >= 2:
                        pe.wait_ge(s_rel_done, n - 1)
                    for m, (a, w) in enumerate(((0, 0), (1, 0), (0, 1))):
                        end = nc.tensor.matmul(sph[q % 2][:], w1[:, w, E, q * P:(q + 1) * P],
                                               x1T[:, a, g * GT * P:(g + 1) * GT * P], start=(m == 0), stop=(m == 2))
                    end.then_inc(s_up_done, 1)

            def down(g):
                pe.wait_ge(s_hid_done, g * FC + FC)
                if g:
                    pe.wait_ge(s_out_kept, g)
                for t in range(GT):
                    for q in range(FC):
                        end = nc.tensor.matmul(spo[:, t * D:(t + 1) * D], shid[:, g % 2, q, t * P:(t + 1) * P],
                                               w2[:, E, q, :], start=(q == 0), stop=(q == FC - 1))
                end.then_inc(s_down_done, 1)
            up(0)
            up(1)
            pe.wait_ge(sel_done, 1)
            sv = sel[:].rearrange("p i e -> p (i e)")
            nc.tensor.matmul(pr[:], tri[:], sv, start=True, stop=True)
            nc.tensor.matmul(pt[:], ones[:], sv, start=True, stop=True).then_inc(ranked, 1)
            for g in range(2, SG):
                down(g - 2)
                up(g)
            down(SG - 2)

            def body(n, s, first, last):
                pe.wait_ge(hotA, n + 1)
                pe.wait_ge(hotB, n + 1)
                for u in range(TP):
                    end = nc.tensor.matmul(plist[:], oneA[:, s, u, :], oneB[:, s, u, :], start=(first and u == 0),
                                           stop=(last and u == TP - 1))
                end.then_inc(listed, 1)
            body(0, 0, True, False)
            body(1, 1, False, False)
            with pe.Fori(2, TURNS - 3, 2) as n:
                body(n, 0, False, False)
                body(n + 1, 1, False, False)
            body(TURNS - 2, 0, False, False)
            body(TURNS - 1, 1, False, True)
            down(SG - 1)

        @block.gpsimd
        def _(pool):
            vv = val[:].rearrange("p r i -> p (r i)")

            def body(n, s, first):
                pool.wait_ge(hotH, n + 1)
                if not first:
                    pool.wait_ge(listed, n - 1)
                nc.gpsimd.tensor_tensor(oneB[:, s], oneH[:, s],
                                        vv[:, bass.ds(n * TP, TP)].unsqueeze(2).broadcast_to([P, TP, COLS]), ALU.mult
                                        ).then_inc(hotB, 1)
            def add(g):
                pool.wait_ge(s_out_kept, g + 1)
                v = y_all[:, g * GT:(g + 1) * GT, :].rearrange("p t c -> p (t c)")
                nc.gpsimd.tensor_tensor(v, sout[:, g % 2, :], v, ALU.add).then_inc(s_added, 1)
            add(0)
            add(1)
            pool.wait_ge(valued, 1)
            turns(pool, body)
            for g in range(2, SG):
                add(g)
            pool.wait_ge(s_added, SG)

        @block.vector
        def _(dve):
            cnt = [0]

            def link(ins):
                cnt[0] += 1
                ins.then_inc(chain, 1)
                dve.wait_ge(chain, cnt[0])

            def over_e(v):
                return v.unsqueeze(2).broadcast_to([P, NT, E])

            for e in range(E):
                nc.vector.memset(order[:, :, e], float(E - e))
            nc.vector.memset(ones[:], 1.0)
            nc.vector.memset(take[:, SLOTS:], 0)
            nc.vector.memset(keep[:, :, 1:], 1.0)
            nc.vector.memset(keep[:, :, 0:1], 0.0)
            nc.vector.tensor_scalar(steps[:], iota[:, 0:MOST], float(ROWS), None, ALU.mult)
            link(nc.vector.tensor_reduce(mx[:, 0], logits[:], AX.X, ALU.max))
            nc.vector.tensor_tensor(tmp[:], logits[:], over_e(mx[:, 0]), ALU.subtract).then_inc(shifted, 1)
            dve.wait_ge(exp_done, 1)
            link(nc.vector.tensor_reduce(mx[:, 1], prob[:], AX.X, ALU.add))
            link(nc.vector.reciprocal(mx[:, 2], mx[:, 1]))
            link(nc.vector.tensor_tensor(prob[:], prob[:], over_e(mx[:, 2]), ALU.mult))
            for r in range(2):
                link(nc.vector.tensor_reduce(mx[:, 3 + r], prob[:], AX.X, ALU.max))
                link(nc.vector.tensor_tensor(tmp[:], prob[:], over_e(mx[:, 3 + r]), ALU.is_equal))
                link(nc.vector.tensor_tensor(tmp[:], tmp[:], order[:], ALU.mult))
                link(nc.vector.tensor_reduce(mx[:, 5], tmp[:], AX.X, ALU.max))
                link(nc.vector.tensor_tensor(oh[:, r], tmp[:], over_e(mx[:, 5]), ALU.is_equal))
                if r == 0:
                    link(nc.vector.scalar_tensor_tensor(prob[:], oh[:, 0], -2.0, prob[:], ALU.mult, ALU.add))
            nc.vector.tensor_tensor(sel[:], oh[:, 0], oh[:, 1], ALU.add).then_inc(sel_done, 1)
            link(nc.vector.tensor_tensor(mx[:, 0], mx[:, 3], mx[:, 4], ALU.add))
            link(nc.vector.tensor_scalar(mx[:, 0], mx[:, 0], 1e-9, None, ALU.max))
            link(nc.vector.reciprocal(mx[:, 1], mx[:, 0]))
            for r in range(2):
                nc.vector.tensor_tensor(weight[:, r], mx[:, 3 + r], mx[:, 1], ALU.mult)
            nc.vector.tensor_copy(val[:, 0], token)
            nc.vector.tensor_scalar(val[:, 1], token, -1.0, None, ALU.mult).then_inc(valued, 1)
            dve.wait_ge(ranked, 1)
            link(nc.vector.tensor_copy(total[:], pt[:].rearrange("p (i e) -> p e i", e=E)))
            fl = "p e i -> p (e i)"
            link(nc.vector.tensor_tensor_scan(upto[:].rearrange(fl), keep[:].rearrange(fl), total[:].rearrange(fl),
                                              0.0, ALU.mult, ALU.add))
            link(nc.vector.tensor_tensor(fills[:], upto[:, :, NT - 1:NT].broadcast_to([P, E, MOST]),
                                         steps[:].unsqueeze(1).broadcast_to([P, E, MOST]), ALU.is_gt))
            link(nc.vector.tensor_reduce(tiles[:, 0], fills[:], AX.X, ALU.add))
            link(nc.vector.memset(tiles[:, 1], 1.0))
            link(nc.vector.tensor_tensor_scan(tiles[:, 2], tiles[:, 1], tiles[:, 0], 0.0, ALU.mult, ALU.add))
            link(nc.vector.tensor_tensor(tiles[:, 3], tiles[:, 2], tiles[:, 0], ALU.subtract))
            link(nc.vector.tensor_tensor(texp[:], iota[:, 0:TILES].unsqueeze(2).broadcast_to([P, TILES, E]),
                                         tiles[:, 2].unsqueeze(1).broadcast_to([P, TILES, E]), ALU.is_ge))
            link(nc.vector.tensor_reduce(tex[:], texp[:], AX.X, ALU.add))
            nc.vector.tensor_scalar(expert[:], tex[0:1, :], float(E - 1), None, ALU.min)
            link(nc.vector.tensor_tensor(total[:], upto[:], total[:], ALU.subtract))
            link(nc.vector.tensor_scalar(tiles[:, 3], tiles[:, 3], float(ROWS), -1.0, ALU.mult, ALU.add))
            link(nc.vector.tensor_tensor(base[:], pr[:].rearrange("p (i e) -> p i e", e=E),
                                         total[:].rearrange("p e i -> p i e"), ALU.add))
            link(nc.vector.tensor_tensor(base[:], base[:], tiles[:, 3].unsqueeze(1).broadcast_to([P, NT, E]),
                                         ALU.add))
            for r in range(2):
                link(nc.vector.tensor_tensor(tmp[:], base[:], oh[:, r], ALU.mult))
                link(nc.vector.tensor_reduce(pos[:, r], tmp[:], AX.X, ALU.add))
            link(nc.vector.tensor_scalar(hi[:], pos[:], 1.0 / P, -127.0 / 256, ALU.mult, ALU.add))
            link(nc.vector.tensor_scalar(hi[:], hi[:], ROUND, -ROUND, ALU.add, ALU.add))
            link(nc.vector.scalar_tensor_tensor(lo[:], hi[:], -float(P), pos[:], ALU.mult, ALU.add))
            lv, hv = (v[:].rearrange("p r i -> p (r i)") for v in (lo, hi))

            def body(n, s, first):
                if not first:
                    dve.wait_ge(listed, n - 1)
                nc.vector.tensor_tensor(oneA[:, s], iota.unsqueeze(1).broadcast_to([P, TP, P]),
                                        lv[:, bass.ds(n * TP, TP)].unsqueeze(2).broadcast_to([P, TP, P]), ALU.is_equal
                                        ).then_inc(hotA, 1)
                if not first:
                    dve.wait_ge(hotB, n - 1)
                nc.vector.tensor_tensor(oneH[:, s], iota[:, 0:COLS].unsqueeze(1).broadcast_to([P, TP, COLS]),
                                        hv[:, bass.ds(n * TP, TP)].unsqueeze(2).broadcast_to([P, TP, COLS]),
                                        ALU.is_equal).then_inc(hotH, 1)
            turns(dve, body)
            dve.wait_ge(listed, TURNS)
            link(nc.vector.tensor_copy(sl[:, 0], plist[:, 0:SLOTS]))
            link(nc.vector.tensor_scalar(sl[:, 1], sl[:, 0], -1.0, None, ALU.mult))
            link(nc.vector.tensor_tensor(sl[:, 1], sl[:, 1], sl[:, 0], ALU.max))
            link(nc.vector.tensor_scalar(sl[:, 1], sl[:, 1], -1.0, None, ALU.add))
            nc.vector.tensor_scalar(take[:, 0:SLOTS], sl[:, 1], 0.0, None, ALU.max)
            link(nc.vector.tensor_scalar(sl[:, 2], sl[:, 0], 0.0, float(NTOK), ALU.is_lt, ALU.mult))
            link(nc.vector.tensor_tensor(sl[:, 1], sl[:, 1], sl[:, 2], ALU.add))
            link(nc.vector.tensor_scalar(sl[:, 2], sl[:, 0], 0.0, float(4 * NTOK), ALU.is_equal, ALU.mult))
            nc.vector.tensor_tensor(put[:], sl[:, 1], sl[:, 2], ALU.add)


def routed(nc, x1T, y_all, ident, w1, w2, take, put, expert, x1_dram, pick_dram):
    HALVES = ROWS // P
    U = 4
    HF = FC // 2
    with ExitStack() as c:
        def sb(name, shape, dt=F32):
            return c.enter_context(nc.sbuf_tensor("routed_" + name, shape, dt))

        def ps(name, shape):
            return c.enter_context(nc.psum_tensor("routed_" + name, shape, F32))

        def sem(name):
            return c.enter_context(nc.semaphore("routed_" + name))

        take_st = sb("take_st", [P, U, HALVES], U32)
        put_st = sb("put_st", [P, U, HALVES], U32)
        xg = sb("xg", [P, U, HALVES, D])
        xs = sb("xsr", [P, 2, 2, ROWS], F32R)
        w1c = sb("w1c", [P, U, 2, FF], F32R)
        w2c = sb("w2c", [P, U, FC, D])
        rel = sb("relr", [P, 2, 2 * ROWS])
        hid = sb("hidr", [P, 2, FC * ROWS])
        ob = sb("ob", [P, U, HALVES, D])
        srel = sb("srel", [P, 2, HF * ROWS])
        shid = sb("shid", [P, FC * ROWS])
        px = ps("px", [P, ROWS])
        ph = [ps(f"phr{i}", [P, FC * ROWS]) for i in range(2)]
        po = ps("por", [P, HALVES * D])
        sph = ps("sph", [P, HF * ROWS])
        spo = ps("spo", [P, HALVES * D])
        take_ready = sem("take_ready")
        put_ready = sem("put_ready")
        gather_due = sem("gather_due")
        scatter_due = sem("scatter_due")
        gathered = [sem(f"gathered{u}") for u in range(U)]
        scattered = [sem(f"scattered{u}") for u in range(U)]
        turned = sem("x_turned_r")
        x_high = sem("x_high_r")
        x_low = sem("x_low_r")
        w_ready = sem("w_ready")
        up_done = sem("up_done_r")
        rel_done = sem("rel_done_r")
        hid_done = sem("hid_done_r")
        down_done = sem("down_done_r")
        kept = sem("kept")
        HEAD = 4
        s_up_done = sem("s_up_done")
        s_rel_done = sem("s_rel_done")
        s_hid_done = sem("s_hid_done")
        s_down_done = sem("s_down_done")
        s_added = sem("s_added")
        block = c.enter_context(nc.Block())
        LAST = TILES // U * U if TILES % U else TILES - U

        FIRST = SG * GT * P
        assert FIRST + (LAST - U) // U * ROWS == NTOK
        assert U == 4 and D == P and ROWS % U == 0

        def tiles(eng, front, body):
            front()
            for u in range(U):
                body(u, u, None)
            with eng.Fori(U, LAST - U + 1, U) as t:
                for u in range(U):
                    body(t + u, u, t - U)
            for u in range(TILES - LAST):
                body(LAST + u, u, None)

        def beyond(t, n):
            return isinstance(t, int) and t + n >= TILES

        def early(t, n):
            return isinstance(t, int) and t < n

        def passes(t, u):
            return (16 * HALVES // U) * (t - u) + 16 * HALVES

        @block.gpsimd
        def _(pool):
            def gather(t, u):
                pool.wait_ge(take_ready, t + 1)
                if not early(t, U):
                    pool.wait_ge(turned, t - U + 1)
                pool.sem_inc(gather_due, 1)
                for h in range(HALVES):
                    nc.gpsimd.indirect_dma_start(
                        out=xg[:, u, h, :], out_offset=None, in_=x1_dram,
                        in_offset=bass.IndirectOffsetOnAxis(ap=take_st[:, u, h:h + 1], axis=0)
                    ).then_inc(gathered[u], 16)

            def front():
                for t in range(U):
                    gather(t, t)

            def body(t, u, k):
                if not beyond(t, U):
                    gather(t + U, u)
                pool.wait_ge(kept, t + 1)
                pool.wait_ge(put_ready, t + 1)
                pool.sem_inc(scatter_due, 1)
                for h in range(HALVES):
                    nc.gpsimd.indirect_dma_start(
                        out=pick_dram, in_=ob[:, u, h, :], in_offset=None,
                        out_offset=bass.IndirectOffsetOnAxis(ap=put_st[:, u, h:h + 1], axis=0),
                        bounds_check=2 * NTOK - 1, oob_is_err=False).then_inc(scattered[u], 16)
            tiles(pool, front, body)
            for u in range(U):
                pool.wait_ge(scattered[u], 16 * HALVES * len(range(u, TILES, U)))

        @block.tensor
        def _(pe):
            def turn(t, u):
                pe.wait_ge(gathered[u], passes(t, u))
                if not early(t, 1):
                    pe.wait_ge(x_low, t)
                for h in range(HALVES):
                    last = nc.tensor.transpose(px[:, h * P:(h + 1) * P], xg[:, u, h, :], ident[:])
                last.then_inc(turned, 1)

            def up(t, u):
                s = u % 2
                pe.wait_ge(x_low, t + 1)
                pe.wait_ge(w_ready, t + 1)
                for q in range(FC):
                    if q % 2 == 0 and not early(t, 2):
                        pe.wait_ge(rel_done, 2 * (t - 2) + q // 2 + 1)
                    for m, (a, w) in enumerate(((0, 0), (1, 0), (0, 1))):
                        last = nc.tensor.matmul(ph[s][:, q * ROWS:(q + 1) * ROWS], w1c[:, u, w, q * P:(q + 1) * P],
                                                xs[:, s, a, :], start=(m == 0), stop=(m == 2))
                    if q % 2:
                        last.then_inc(up_done, 1)

            def down(t, u):
                s = u % 2
                pe.wait_ge(hid_done, 2 * t + 2)
                if not early(t, 1):
                    pe.wait_ge(kept, t)
                for h in range(HALVES):
                    for q in range(FC):
                        last = nc.tensor.matmul(po[:, h * D:(h + 1) * D],
                                                hid[:, s, q * ROWS + h * P:q * ROWS + (h + 1) * P],
                                                w2c[:, u, q, :], start=(q == 0), stop=(q == FC - 1))
                last.then_inc(down_done, 1)

            def shared_up(k, h):
                pe.wait_ge(s_rel_done, k + 2 * h + HEAD)
                for q in range(HF):
                    c0 = (h * HF + q) * P
                    for m, (a, w) in enumerate(((0, 0), (1, 0), (0, 1))):
                        last = nc.tensor.matmul(sph[:, q * ROWS:(q + 1) * ROWS], w1[:, w, E, c0:c0 + P],
                                                x1T[:, a, bass.ds(k * (ROWS // U) + FIRST, ROWS)],
                                                start=(m == 0), stop=(m == 2))
                last.then_inc(s_up_done, 2)

            def shared_down(k):
                pe.wait_ge(s_hid_done, k + 4 + HEAD)
                pe.wait_ge(s_added, k + HEAD)
                for h in range(HALVES):
                    for q in range(FC):
                        last = nc.tensor.matmul(spo[:, h * D:(h + 1) * D],
                                                shid[:, q * ROWS + h * P:q * ROWS + (h + 1) * P],
                                                w2[:, E, q, :], start=(q == 0), stop=(q == FC - 1))
                last.then_inc(s_down_done, 4)

            def front():
                nc.tensor.sem_inc(s_up_done, HEAD)
                nc.tensor.sem_inc(s_down_done, HEAD)
                turn(0, 0)
                turn(1, 1)
                up(0, 0)

            def body(t, u, k):
                if not beyond(t, 1):
                    up(t + 1, (u + 1) % U)
                if k is not None and u < 2:
                    shared_up(k, u)
                if not beyond(t, 2):
                    turn(t + 2, (u + 2) % U)
                down(t, u)
                if k is not None and u == 2:
                    shared_down(k)
            tiles(pe, front, body)

        @block.scalar
        def _(act):
            def high(t, u):
                act.wait_ge(turned, t + 1)
                if not early(t, 2):
                    act.wait_ge(up_done, 2 * (t - 2) + 2)
                nc.scalar.copy(xs[:, u % 2, 0, :], px[:]).then_inc(x_high, 1)

            def rectified(t, u):
                s = u % 2
                for h in range(2):
                    o = h * 2 * ROWS
                    act.wait_ge(up_done, 2 * t + h + 1)
                    if not early(t, 1):
                        act.wait_ge(hid_done, 2 * t + h - 1)
                    nc.scalar.activation(rel[:, h, :], ph[s][:, o:o + 2 * ROWS], ACT.Relu).then_inc(rel_done, 1)

            def squared(t, u):
                s = u % 2
                for h in range(2):
                    o = h * 2 * ROWS
                    act.wait_ge(rel_done, 2 * t + h + 1)
                    if h == 0 and not early(t, 2):
                        act.wait_ge(down_done, t - 1)
                    nc.scalar.activation(hid[:, s, o:o + 2 * ROWS], rel[:, h, :], ACT.Square).then_inc(hid_done, 1)

            def shared_relu(k, h):
                act.wait_ge(s_up_done, k + 2 * h + 2 + HEAD)
                act.wait_ge(s_hid_done, k + 2 * h - 2 + HEAD)
                nc.scalar.activation(srel[:, h, :], sph[:], ACT.Relu).then_inc(s_rel_done, 2)

            def shared_square(k, h):
                act.wait_ge(s_rel_done, k + 2 * h + 2 + HEAD)
                act.wait_ge(s_down_done, k + HEAD)
                nc.scalar.activation(shid[:, h * HF * ROWS:(h + 1) * HF * ROWS], srel[:, h, :], ACT.Square
                                     ).then_inc(s_hid_done, 2)

            def front():
                nc.scalar.sem_inc(s_rel_done, HEAD)
                nc.scalar.sem_inc(s_hid_done, HEAD)
                high(0, 0)
                high(1, 1)
                rectified(0, 0)
                squared(0, 0)

            def body(t, u, k):
                if not beyond(t, 1):
                    rectified(t + 1, (u + 1) % U)
                if not beyond(t, 2):
                    high(t + 2, (u + 2) % U)
                if k is not None and u < 2:
                    shared_relu(k, u)
                if not beyond(t, 1):
                    squared(t + 1, (u + 1) % U)
                if k is not None and u < 2:
                    shared_square(k, u)
            tiles(act, front, body)

        @block.vector
        def _(dve):
            def take_part(t, u):
                if not early(t, U):
                    dve.wait_ge(gathered[u], passes(t - U, u))
                nc.vector.tensor_copy(take_st[:, u, :], take[:, bass.ds(t * HALVES, HALVES)]).then_inc(take_ready, 1)

            def put_part(t, u):
                if not early(t, U):
                    dve.wait_ge(scattered[u], passes(t - U, u))
                nc.vector.tensor_copy(put_st[:, u, :], put[:, bass.ds(t * HALVES, HALVES)]).then_inc(put_ready, 1)

            def weights(t, u):
                e = dve.value_load(expert[0:1, bass.ds(t, 1)], min_val=0, max_val=E - 1)
                if not early(t, U):
                    dve.wait_ge(down_done, t - U + 1)
                nc.vector.tensor_copy(w1c[:, u], w1[:, :, bass.ds(e, 1), :].rearrange("p a o f -> p a (o f)").bitcast(F32))
                nc.vector.tensor_copy(w2c[:, u], w2[:, bass.ds(e, 1)].rearrange("p o c d -> p (o c) d")
                                      ).then_inc(w_ready, 1)

            def low(t, u):
                dve.wait_ge(x_high, t + 1)
                nc.vector.tensor_tensor(xs[:, u % 2, 1, :], px[:], xs[:, u % 2, 0, :].bitcast(F32), ALU.subtract
                                        ).then_inc(x_low, 1)

            def shared_add(k):
                dve.wait_ge(s_down_done, k + 4 + HEAD)
                v = y_all[:].rearrange("p t c -> p (t c)")[:, bass.ds(k * (ROWS // U) + FIRST, ROWS)]
                nc.vector.tensor_tensor(v, spo[:], v, ALU.add).then_inc(s_added, 4)

            def front():
                nc.vector.sem_inc(s_added, HEAD)
                for t in range(4):
                    take_part(t, t)
                put_part(0, 0)
                for t in range(2):
                    weights(t, t)
                    low(t, t)
                weights(2, 2)

            def body(t, u, k):
                if not beyond(t, 4):
                    take_part(t + 4, u)
                if not beyond(t, 3):
                    weights(t + 3, (u + 3) % U)
                if not beyond(t, 2):
                    low(t + 2, (u + 2) % U)
                dve.wait_ge(down_done, t + 1)
                if not early(t, U):
                    dve.wait_ge(scattered[u], passes(t - U, u))
                nc.vector.tensor_copy(ob[:, u].rearrange("p h d -> p (h d)"), po[:]).then_inc(kept, 1)
                if not beyond(t, 1):
                    put_part(t + 1, (u + 1) % U)
                if k is not None and u == 2:
                    shared_add(k)
            tiles(dve, front, body)


def finish(nc, y_all, weight, pick_dram, out):
    with ExitStack() as c:
        def sb(name, shape, dt=F32):
            return c.enter_context(nc.sbuf_tensor("finish_" + name, shape, dt))

        def sem(name):
            return c.enter_context(nc.semaphore("finish_" + name))

        pick = sb("pick", [P, 2, 2, GT, D])
        one = sb("one", [P, 2, GT, D])
        two = sb("two", [P, 2, GT, D])
        res = sb("resf", [P, 2, GT, D])
        stats = sb("statsf", [P, 2, GT, 6])
        mv = sb("mvf", [P, 2, GT, 2])
        std = sb("stdf", [P, 2, GT])
        rstd = sb("rstdf", [P, 2, GT])
        shift = sb("shift", [P, 2, GT])
        eps = sb("epsf", [P, 1])
        xo = sb("xo", [P, 2, GT, D])
        picked = [sem(f"picked{i}") for i in range(2)]
        one_scaled = sem("one_scaled")
        one_done = sem("one_done")
        two_done = sem("two_done")
        res_done = sem("res_done_f")
        stats_done = sem("stats_done_f")
        var_done = sem("var_done_f")
        std_done = sem("std_done_f")
        rstd_done = sem("rstd_done_f")
        shift_done = sem("shift_done")
        xo_done = sem("xo_done")
        xo_part = sem("xo_part")
        eps_set = sem("eps_set")
        stored = [sem(f"stored_f{i}") for i in range(2)]
        block = c.enter_context(nc.Block())

        def groups(eng, front, body):
            front()
            body(0, 0)
            body(1, 1)
            with eng.Fori(2, NG - 3, 2) as g:
                body(g, 0)
                body(g + 1, 1)
            body(NG - 2, 0)
            body(NG - 1, 1)

        def early(g, n):
            return isinstance(g, int) and g < n

        @block.sync
        def _(sp):
            ov = out.rearrange("b (j p) d -> (b j) p d", p=P)

            def load(g, s):
                if not early(g, 2):
                    sp.wait_ge(one_scaled, g - 1)
                    sp.wait_ge(two_done, g - 1)
                for r in range(2):
                    sp.dma_start(pick[:, s, r], pick_dram[bass.ds(g * (GT * P) + r * NTOK, GT * P), :]
                                 .rearrange("(t p) d -> p t d", p=P)).then_inc(picked[s], 16)

            def store(g, s):
                sp.wait_ge(xo_done, g + 1)
                sp.wait_ge(xo_part, g + 1)
                sp.dma_start(ov[bass.ds(g * GT, GT)].rearrange("j p d -> p j d"), xo[:, s]).then_inc(stored[s], 16)
            for g in range(4):
                load(g, g % 2)
            with sp.Fori(0, NG - 5, 2) as g:
                for s in range(2):
                    load(g + s + 4, s)
                    store(g + s, s)
            with sp.Fori(NG - 4, NG - 1, 2) as g:
                for s in range(2):
                    store(g + s, s)
            for i in range(2):
                sp.wait_ge(stored[i], 16 * NG // 2)

        @block.gpsimd
        def _(pool):
            def body(g, s):
                pool.wait_ge(picked[s], 16 * (g - s) + 32)
                if not early(g, 2):
                    pool.wait_ge(res_done, g - 1)
                wv = weight[:, 0, bass.ds(g * GT, GT)].unsqueeze(2).broadcast_to([P, GT, D])
                nc.gpsimd.tensor_tensor(one[:, s], pick[:, s, 0], wv, ALU.mult).then_inc(one_scaled, 1)
                pool.wait_ge(one_scaled, g + 1)
                nc.gpsimd.tensor_tensor(one[:, s], one[:, s], y_all[:, bass.ds(g * GT, GT), :], ALU.add
                                        ).then_inc(one_done, 1)
            groups(pool, lambda: None, body)

        @block.scalar
        def _(act):
            def second(g, s):
                act.wait_ge(picked[s], 16 * (g - s) + 32)
                if not early(g, 2):
                    act.wait_ge(res_done, g - 1)
                for t in range(GT):
                    last = nc.scalar.mul(two[:, s, t, :], pick[:, s, 1, t, :], weight[:, 1, bass.ds(g * GT + t, 1)])
                last.then_inc(two_done, 1)

            def root(g, s):
                act.wait_ge(var_done, g + 1)
                nc.scalar.activation(std[:, s], mv[:, s, :, 1], ACT.Sqrt, bias=eps[:]).then_inc(std_done, 1)

            def normalise(g, s):
                act.wait_ge(shift_done, g + 1)
                if not early(g, 2):
                    act.wait_ge(stored[s], 8 * (g - s))
                for t in range(GT - 1):
                    last = nc.scalar.activation(xo[:, s, t, :], res[:, s, t, :], ACT.Identity,
                                                bias=shift[:, s, t:t + 1], scale=rstd[:, s, t:t + 1])
                last.then_inc(xo_done, 1)

            def front():
                act.wait_ge(eps_set, 1)
                second(0, 0)
                second(1, 1)

            def body(g, s):
                root(g, s)
                if not (isinstance(g, int) and g >= NG - 2):
                    second(g + 2, s)
                normalise(g, s)
            groups(act, front, body)

        @block.vector
        def _(dve):
            nc.vector.memset(eps[:], EPS).then_inc(eps_set, 1)

            def add(g, s):
                dve.wait_ge(one_done, g + 1)
                dve.wait_ge(two_done, g + 1)
                if not early(g, 2):
                    dve.wait_ge(xo_done, g - 1)
                    dve.wait_ge(xo_part, g - 1)
                nc.vector.tensor_tensor(res[:, s], one[:, s], two[:, s], ALU.add).then_inc(res_done, 1)

            def measure(g, s):
                dve.wait_ge(res_done, g + 1)
                for t in range(GT):
                    last = nc.vector.bn_stats(stats[:, s, t, :], res[:, s, t, :])
                last.then_inc(stats_done, 1)
                dve.wait_ge(stats_done, 2 * g + 1)
                nc.vector.sem_inc(stats_done, 1)
                for t in range(GT):
                    last = nc.vector.bn_aggr(mv[:, s, t, :], stats[:, s, t, :])
                last.then_inc(var_done, 1)

            def invert(g, s):
                dve.wait_ge(std_done, g + 1)
                nc.vector.reciprocal(rstd[:, s], std[:, s]).then_inc(rstd_done, 1)
                dve.wait_ge(rstd_done, g + 1)
                nc.vector.scalar_tensor_tensor(shift[:, s], mv[:, s, :, 0], -1.0, rstd[:, s], ALU.mult, ALU.mult
                                               ).then_inc(shift_done, 1)
                if not early(g, 2):
                    dve.wait_ge(stored[s], 8 * (g - s))
                t = GT - 1
                nc.vector.tensor_scalar(xo[:, s, t, :], res[:, s, t, :], mv[:, s, t, 0:1], rstd[:, s, t:t + 1],
                                        ALU.subtract, ALU.mult).then_inc(xo_part, 1)

            def front():
                add(0, 0)
                measure(0, 0)

            def body(g, s):
                more = not (isinstance(g, int) and g == NG - 1)
                if more:
                    add(g + 1, 1 - s)
                invert(g, s)
                if more:
                    measure(g + 1, 1 - s)
            groups(dve, front, body)


INS = ["L0_attn_x", "L0_attn_W_in", "L0_attn_conv_k", "L0_attn_theta", "L0_attn_decay_slopes",
       "L0_attn_anchor_slopes", "L0_attn_score_scale", "L0_attn_W_re", "L0_attn_W_im",
       "L0_attn_norm_scale", "L0_attn_W_out", "L0_ffn_router_w", "L0_ffn_w_fc", "L0_ffn_w_proj",
       "L0_ffn_shared_fc", "L0_ffn_shared_proj"]


def kernel(**inputs):
    import numpy as np
    import concourse.bacc as bacc
    from concourse import mybir as mb
    from concourse.bass_utils import run_bass_kernel_spmd as run

    nc = bacc.Bacc("TRN2", target_bir_lowering=False, num_devices=1)
    tables = np.zeros((P, 2 * P + L + P + NT), np.float32)
    tables[:, 0:P] = np.eye(P)
    tables[:, P:2 * P] = np.triu(np.ones((P, P)))
    pos = np.arange(L)
    tables[:, 2 * P:2 * P + L] = [(L - 1 - pos) if k % K < K - 4 else pos for k in range(P)]
    tables[:, 2 * P + L:3 * P + L] = np.arange(P)
    tables[:, 3 * P + L:] = 1 + np.arange(P)[:, None] + P * np.arange(NT)
    arrays = {n: np.ascontiguousarray(inputs[n]) for n in INS}
    arrays["tables"] = tables
    args = [nc.dram_tensor(n, a.shape, mb.dt.float32, kind="ExternalInput").ap() for n, a in arrays.items()]
    out = nc.dram_tensor("out", (B, L, D), mb.dt.float32, kind="ExternalOutput").ap()
    build(nc, *args, out)
    r = run(nc, [arrays], core_ids=[0])
    return r.results[0]["out"]
```
